# Optimizing a Trainium2 kernel written in Bass

```python
import numpy as np
import jax
import jax.numpy as jnp

def _softmax(x, axis=-1):
    return jax.nn.softmax(x, axis=axis)

def _gelu(x):
    return jax.nn.gelu(x, approximate=True)

def _silu(x):
    return jax.nn.silu(x)

def _sigmoid(x):
    return jax.nn.sigmoid(x)

def _layernorm(x, axis=-1, eps=1e-05):
    m = jnp.mean(x, axis=axis, keepdims=True)
    v = jnp.var(x, axis=axis, keepdims=True)
    return (x - m) / jnp.sqrt(v + eps)

def _scatter_add(tgt, idx, src, axis=0):
    return tgt.at[idx].add(src)

def _segment_sum(src, seg, n):
    return jax.ops.segment_sum(src, seg, n)
kernel_name = 'mk_adj_ffn_d2_adj_r2_3c74ca'

def setup_inputs(seed: int=0):
    np.random.seed(seed)
    _w = jnp.asarray

    def _rec_inputs():
        import jax
        import jax.numpy as jnp
        _gk = jax.random.key(seed)
        x = -0.0002928 + 1 * jax.random.normal(jax.random.fold_in(_gk, 1), (128, 64, 128), jnp.float32)
        _a = jax.random.bernoulli(jax.random.fold_in(_gk, 2), 0.125, (128, 64, 64))
        adj = _a.astype(jnp.int32)
        _nm = jnp.ones((128, 64), dtype=bool)
        nodemask = jnp.where(_nm, 1.0, 0.0).astype(jnp.float32)
        return (x, adj, nodemask)
    x, adj, nodemask = _rec_inputs()

    def _L0_gnn_setup():
        import jax, jax.numpy as jnp
        import numpy as np
        OUT = 128
        NUM_LAYERS = 3

        def _gru_cell(inp, h, w_ih, w_hh, b_ih, b_hh):
            gi = inp @ w_ih.T + b_ih
            gh = h @ w_hh.T + b_hh
            i_r, i_z, i_n = jnp.split(gi, 3, axis=-1)
            h_r, h_z, h_n = jnp.split(gh, 3, axis=-1)
            r = jax.nn.sigmoid(i_r + h_r)
            z = jax.nn.sigmoid(i_z + h_z)
            n = jnp.tanh(i_n + r * h_n)
            return (1.0 - z) * n + z * h
        key = jax.random.key(seed)
        ks = jax.random.split(key, 8)
        B, N, D = (32, 256, 128)
        x = jax.random.normal(ks[0], (B, N, D), dtype=jnp.float32)
        adj = jax.random.randint(ks[1], (B, N, N), 0, 2, dtype=jnp.int32)
        s = 1.0 / np.sqrt(OUT)
        weight = jax.random.uniform(ks[2], (NUM_LAYERS, OUT, OUT), jnp.float32, -s, s)
        w_ih = jax.random.uniform(ks[3], (3 * OUT, OUT), jnp.float32, -s, s)
        w_hh = jax.random.uniform(ks[4], (3 * OUT, OUT), jnp.float32, -s, s)
        b_ih = jax.random.uniform(ks[5], (3 * OUT,), jnp.float32, -s, s)
        b_hh = jax.random.uniform(ks[6], (3 * OUT,), jnp.float32, -s, s)
        return {'x': x, 'adj': adj, 'weight': weight, 'w_ih': w_ih, 'w_hh': w_hh, 'b_ih': b_ih, 'b_hh': b_hh}
    _L0_gnn_all = _L0_gnn_setup()
    _L0_gnn_in = {k: v for k, v in _L0_gnn_all.items() if k in ('weight', 'w_ih', 'w_hh', 'b_ih', 'b_hh')}
    del _L0_gnn_all

    def _L0_ffn_setup():
        import jax, jax.numpy as jnp
        import numpy as np
        B, S, D, H, E, K = (8, 4096, 128, 512, 8, 2)
        key = jax.random.key(seed)
        ks = jax.random.split(key, 7)
        s_in = 1.0 / np.sqrt(D)
        s_hid = 1.0 / np.sqrt(H)
        return {'x': jax.random.normal(ks[0], (B, S, D), dtype=jnp.float32), 'Wg': jax.random.uniform(ks[1], (E, D), jnp.float32, -s_in, s_in), 'bg': jax.random.uniform(ks[2], (E,), jnp.float32, -s_in, s_in), 'W1': jax.random.uniform(ks[3], (E, H, D), jnp.float32, -s_in, s_in), 'b1': jax.random.uniform(ks[4], (E, H), jnp.float32, -s_in, s_in), 'W2': jax.random.uniform(ks[5], (E, D, H), jnp.float32, -s_hid, s_hid), 'b2': jax.random.uniform(ks[6], (E, D), jnp.float32, -s_hid, s_hid)}
    _L0_ffn_all = _L0_ffn_setup()
    _L0_ffn_in = {k: v for k, v in _L0_ffn_all.items() if k in ('Wg', 'bg', 'W1', 'b1', 'W2', 'b2')}
    del _L0_ffn_all

    def _L1_gnn_setup():
        import jax, jax.numpy as jnp
        import numpy as np
        D_MODEL = 128
        NUM_REL = 40

        def _direction(x, W, Wg, b, bg, adj, rel_ids):
            h = x @ W.T
            g = h @ Wg.T
            vals = (h[:, :, None, :] + b) * jax.nn.sigmoid(g[:, :, None, :] + bg)
            onehot = (adj[..., None] == rel_ids).astype(h.dtype)
            return jnp.einsum('bnmr,bmrd->bnd', onehot, vals)
        key = jax.random.key(seed)
        ks = jax.random.split(key, 16)
        B, N, d = (2, 256, D_MODEL)
        s = 0.02
        inp = {'node': jax.random.normal(ks[0], (B, N, d), dtype=jnp.float32), 'node_mask': jnp.ones((B, N), dtype=jnp.float32), 'adj_mat': jax.random.randint(ks[1], (B, N, N), 0, 41, dtype=jnp.int32), 'W_fwd': jax.random.normal(ks[2], (d, d), dtype=jnp.float32) * s, 'W_bwd': jax.random.normal(ks[3], (d, d), dtype=jnp.float32) * s, 'W_loop': jax.random.normal(ks[4], (d, d), dtype=jnp.float32) * s, 'Wg_fwd': jax.random.normal(ks[5], (d, d), dtype=jnp.float32) * s, 'Wg_bwd': jax.random.normal(ks[6], (d, d), dtype=jnp.float32) * s, 'Wg_loop': jax.random.normal(ks[7], (d, d), dtype=jnp.float32) * s, 'b_fwd': jax.random.normal(ks[8], (NUM_REL - 1, d), dtype=jnp.float32) * s, 'b_bwd': jax.random.normal(ks[9], (NUM_REL - 1, d), dtype=jnp.float32) * s, 'b_loop': jax.random.normal(ks[10], (1, d), dtype=jnp.float32) * s, 'bg_fwd': jax.random.normal(ks[11], (NUM_REL - 1, d), dtype=jnp.float32) * s, 'bg_bwd': jax.random.normal(ks[12], (NUM_REL - 1, d), dtype=jnp.float32) * s, 'bg_loop': jax.random.normal(ks[13], (1, d), dtype=jnp.float32) * s}
        return inp
    _L1_gnn_all = _L1_gnn_setup()
    _L1_gnn_in = {k: v for k, v in _L1_gnn_all.items() if k in ('W_fwd', 'W_bwd', 'W_loop', 'Wg_fwd', 'Wg_bwd', 'Wg_loop', 'b_fwd', 'b_bwd', 'b_loop', 'bg_fwd', 'bg_bwd', 'bg_loop')}
    del _L1_gnn_all

    def _L1_ffn_setup():
        import jax, jax.numpy as jnp
        import numpy as np
        TOP_K = 2
        LN_EPS = 1e-05
        key = jax.random.key(seed)
        ks = jax.random.split(key, 8)
        B, S, D, E, H = (16, 512, 128, 8, 512)
        x = jax.random.normal(ks[0], (B, S, D), dtype=jnp.float32)
        Wr = jax.random.normal(ks[1], (D, E), dtype=jnp.float32) * 0.1
        br = jnp.zeros((E,), dtype=jnp.float32)
        ln_g = jnp.ones((E, D), dtype=jnp.float32)
        ln_b = jnp.zeros((E, D), dtype=jnp.float32)
        W1 = jax.random.normal(ks[2], (E, D, H), dtype=jnp.float32) * (1.0 / np.sqrt(D))
        b1 = jnp.zeros((E, H), dtype=jnp.float32)
        W2 = jax.random.normal(ks[3], (E, H, D), dtype=jnp.float32) * (1.0 / np.sqrt(H))
        b2 = jnp.zeros((E, D), dtype=jnp.float32)
        return {'x': x, 'Wr': Wr, 'br': br, 'ln_g': ln_g, 'ln_b': ln_b, 'W1': W1, 'b1': b1, 'W2': W2, 'b2': b2}
    _L1_ffn_all = _L1_ffn_setup()
    _L1_ffn_in = {k: v for k, v in _L1_ffn_all.items() if k in ('Wr', 'br', 'ln_g', 'ln_b', 'W1', 'b1', 'W2', 'b2')}
    del _L1_ffn_all
    return {'x': x, 'adj': adj, 'nodemask': nodemask, 'L0_gnn_weight': _L0_gnn_in['weight'], 'L0_gnn_w_ih': _L0_gnn_in['w_ih'], 'L0_gnn_w_hh': _L0_gnn_in['w_hh'], 'L0_gnn_b_ih': _L0_gnn_in['b_ih'], 'L0_gnn_b_hh': _L0_gnn_in['b_hh'], 'L0_ffn_Wg': _L0_ffn_in['Wg'], 'L0_ffn_bg': _L0_ffn_in['bg'], 'L0_ffn_W1': _L0_ffn_in['W1'], 'L0_ffn_b1': _L0_ffn_in['b1'], 'L0_ffn_W2': _L0_ffn_in['W2'], 'L0_ffn_b2': _L0_ffn_in['b2'], 'L1_gnn_W_fwd': _L1_gnn_in['W_fwd'], 'L1_gnn_W_bwd': _L1_gnn_in['W_bwd'], 'L1_gnn_W_loop': _L1_gnn_in['W_loop'], 'L1_gnn_Wg_fwd': _L1_gnn_in['Wg_fwd'], 'L1_gnn_Wg_bwd': _L1_gnn_in['Wg_bwd'], 'L1_gnn_Wg_loop': _L1_gnn_in['Wg_loop'], 'L1_gnn_b_fwd': _L1_gnn_in['b_fwd'], 'L1_gnn_b_bwd': _L1_gnn_in['b_bwd'], 'L1_gnn_b_loop': _L1_gnn_in['b_loop'], 'L1_gnn_bg_fwd': _L1_gnn_in['bg_fwd'], 'L1_gnn_bg_bwd': _L1_gnn_in['bg_bwd'], 'L1_gnn_bg_loop': _L1_gnn_in['bg_loop'], 'L1_ffn_Wr': _L1_ffn_in['Wr'], 'L1_ffn_br': _L1_ffn_in['br'], 'L1_ffn_ln_g': _L1_ffn_in['ln_g'], 'L1_ffn_ln_b': _L1_ffn_in['ln_b'], 'L1_ffn_W1': _L1_ffn_in['W1'], 'L1_ffn_b1': _L1_ffn_in['b1'], 'L1_ffn_W2': _L1_ffn_in['W2'], 'L1_ffn_b2': _L1_ffn_in['b2']}

def reference(x, adj, nodemask, L0_gnn_weight, L0_gnn_w_ih, L0_gnn_w_hh, L0_gnn_b_ih, L0_gnn_b_hh, L0_ffn_Wg, L0_ffn_bg, L0_ffn_W1, L0_ffn_b1, L0_ffn_W2, L0_ffn_b2, L1_gnn_W_fwd, L1_gnn_W_bwd, L1_gnn_W_loop, L1_gnn_Wg_fwd, L1_gnn_Wg_bwd, L1_gnn_Wg_loop, L1_gnn_b_fwd, L1_gnn_b_bwd, L1_gnn_b_loop, L1_gnn_bg_fwd, L1_gnn_bg_bwd, L1_gnn_bg_loop, L1_ffn_Wr, L1_ffn_br, L1_ffn_ln_g, L1_ffn_ln_b, L1_ffn_W1, L1_ffn_b1, L1_ffn_W2, L1_ffn_b2):
    import jax
    import jax.numpy as jnp

    def _L0_gnn_ref(x, adj, weight, w_ih, w_hh, b_ih, b_hh):
        import jax, jax.numpy as jnp
        import numpy as np
        OUT = 128
        NUM_LAYERS = 3

        def _gru_cell(inp, h, w_ih, w_hh, b_ih, b_hh):
            gi = inp @ w_ih.T + b_ih
            gh = h @ w_hh.T + b_hh
            i_r, i_z, i_n = jnp.split(gi, 3, axis=-1)
            h_r, h_z, h_n = jnp.split(gh, 3, axis=-1)
            r = jax.nn.sigmoid(i_r + h_r)
            z = jax.nn.sigmoid(i_z + h_z)
            n = jnp.tanh(i_n + r * h_n)
            return (1.0 - z) * n + z * h
        A = (adj != 0).astype(x.dtype)
        h = x
        L = weight.shape[0]
        for i in range(L):
            m = jnp.einsum('bnd,de->bne', h, weight[i])
            aggr = jnp.einsum('bst,bsd->btd', A, m)
            h = _gru_cell(aggr, h, w_ih, w_hh, b_ih, b_hh)
        return h

    def _L0_ffn_ref(x, Wg, bg, W1, b1, W2, b2):
        import jax, jax.numpy as jnp
        import numpy as np
        B, S, D, H, E, K = (8, 4096, 128, 512, 8, 2)
        gate_scores = jnp.einsum('bsd,ed->bse', x, Wg) + bg
        topk_scores, topk_idx = jax.lax.top_k(gate_scores, K)
        topk_probs = jax.nn.softmax(topk_scores, axis=-1)
        combine = jnp.sum(topk_probs[..., None] * jax.nn.one_hot(topk_idx, E, dtype=x.dtype), axis=-2)
        out = jnp.zeros_like(x)
        for e in range(E):
            h = jax.nn.relu(jnp.einsum('bsd,hd->bsh', x, W1[e]) + b1[e])
            y = jnp.einsum('bsh,dh->bsd', h, W2[e]) + b2[e]
            out = out + combine[..., e:e + 1] * y
        return out

    def _L1_gnn_ref(node, node_mask, adj_mat, W_fwd, W_bwd, W_loop, Wg_fwd, Wg_bwd, Wg_loop, b_fwd, b_bwd, b_loop, bg_fwd, bg_bwd, bg_loop):
        import jax, jax.numpy as jnp
        import numpy as np
        D_MODEL = 128
        NUM_REL = 40

        def _direction(x, W, Wg, b, bg, adj, rel_ids):
            h = x @ W.T
            g = h @ Wg.T
            vals = (h[:, :, None, :] + b) * jax.nn.sigmoid(g[:, :, None, :] + bg)
            onehot = (adj[..., None] == rel_ids).astype(h.dtype)
            return jnp.einsum('bnmr,bmrd->bnd', onehot, vals)
        rels = jnp.arange(2, NUM_REL + 1, dtype=adj_mat.dtype)
        rel1 = jnp.array([1], dtype=adj_mat.dtype)
        adj_t = jnp.swapaxes(adj_mat, -1, -2)
        out = _direction(node, W_fwd, Wg_fwd, b_fwd, bg_fwd, adj_mat, rels)
        out = out + _direction(node, W_bwd, Wg_bwd, b_bwd, bg_bwd, adj_t, rels)
        out = out + _direction(node, W_loop, Wg_loop, b_loop, bg_loop, adj_t, rel1)
        return jax.nn.relu(out)

    def _L1_ffn_ref(x, Wr, br, ln_g, ln_b, W1, b1, W2, b2):
        import jax, jax.numpy as jnp
        import numpy as np
        TOP_K = 2
        LN_EPS = 1e-05
        B, S, D = x.shape
        N = B * S
        xt = x.reshape(N, D)
        logits = xt @ Wr + br
        probs = jax.nn.softmax(logits, axis=-1)
        top_p, top_idx = jax.lax.top_k(probs, TOP_K)
        weights = top_p / top_p.sum(axis=-1, keepdims=True)
        mu = xt.mean(axis=-1, keepdims=True)
        var = ((xt - mu) ** 2).mean(axis=-1, keepdims=True)
        xn = (xt - mu) * jax.lax.rsqrt(var + LN_EPS)
        xe = xn[None, :, :] * ln_g[:, None, :] + ln_b[:, None, :]
        h = jax.nn.gelu(jnp.einsum('end,edh->enh', xe, W1) + b1[:, None, :], approximate=False)
        y = jnp.einsum('enh,ehd->end', h, W2) + b2[:, None, :]
        y_tok = jnp.transpose(y, (1, 0, 2))
        sel = jnp.take_along_axis(y_tok, top_idx[:, :, None], axis=1)
        out = (weights[:, :, None] * sel).sum(axis=1)
        return out.reshape(B, S, D)
    x = x + _L0_gnn_ref(_layernorm(x, axis=-1), adj, L0_gnn_weight, L0_gnn_w_ih, L0_gnn_w_hh, L0_gnn_b_ih, L0_gnn_b_hh)
    x = x + _L0_ffn_ref(_layernorm(x, axis=-1), L0_ffn_Wg, L0_ffn_bg, L0_ffn_W1, L0_ffn_b1, L0_ffn_W2, L0_ffn_b2)
    x = x + _L1_gnn_ref(_layernorm(x, axis=-1), nodemask, adj, L1_gnn_W_fwd, L1_gnn_W_bwd, L1_gnn_W_loop, L1_gnn_Wg_fwd, L1_gnn_Wg_bwd, L1_gnn_Wg_loop, L1_gnn_b_fwd, L1_gnn_b_bwd, L1_gnn_b_loop, L1_gnn_bg_fwd, L1_gnn_bg_bwd, L1_gnn_bg_loop)
    x = x + _L1_ffn_ref(_layernorm(x, axis=-1), L1_ffn_Wr, L1_ffn_br, L1_ffn_ln_g, L1_ffn_ln_b, L1_ffn_W1, L1_ffn_b1, L1_ffn_W2, L1_ffn_b2)
    return x

_drawn_inputs = setup_inputs


def setup_inputs(seed=0):
    import zlib

    import numpy as np

    out = dict(_drawn_inputs(seed))
    spreads = {'L1_ffn_br': (0.0, 0.1),
     'L1_ffn_ln_g': (1.0, 0.2),
     'L1_ffn_ln_b': (0.0, 0.1),
     'L1_ffn_b1': (0.0, 0.1),
     'L1_ffn_b2': (0.0, 0.1)}
    factors = {'L1_gnn_Wg_loop': 2.772, 'L1_gnn_bg_loop': 4.938}
    for name, (base, spread) in spreads.items():
        noise = np.random.default_rng([zlib.crc32(name.encode()), seed]).standard_normal(out[name].shape)
        drawn = base * np.exp(spread * noise) if base else spread * noise
        out[name] = jnp.asarray(drawn.astype(out[name].dtype))
    for name, factor in factors.items():
        out[name] = (out[name] * factor).astype(out[name].dtype)
    return out
```

```python
from contextlib import ExitStack

import concourse.bass as bass
from concourse import mybir

F32 = mybir.dt.float32
F16 = mybir.dt.float16
I32 = mybir.dt.int32
ALU = mybir.AluOpType
ACT = mybir.ActivationFunctionType
AX_X = mybir.AxisListType.X

P = 128
NODES = 64
E = 8
HID = 512
CH = HID // P
LAYERS = 3
GT = 4
GW = GT * P
BLK = 512
RING = 3
RELS = 39
AS = 16.0
WS = 64.0
PS = AS * WS
EPS = 1e-5
BIG = 3.0e38


def flat(ap):
    return ap.rearrange("p a b -> p (a b)")


def wait_from(eng, sem, value):
    if not isinstance(value, int) or value > 0:
        eng.wait_ge(sem, value)


def turns(eng, n, step):
    step(0)
    with eng.Fori(1, n) as i:
        step(i)


def program(nc, ins, out):
    TOK = ins["x"].shape[0] * NODES
    NT = TOK // P
    NG = NT // GT
    NBLK = 2 * TOK // BLK + E - 1
    NBLK += -NBLK % RING
    PAIRS = NG // 2
    x_v = ins["x"].rearrange("(t g) n d -> (g n) t d", g=2)
    out_v = out.rearrange("(t g) n d -> (g n) t d", g=2)
    adj_v = ins["adj"].rearrange("(t g) s n -> (g s) t n", g=2)

    with ExitStack() as ctx:
        def sb(name, shape, dt, c=ctx):
            return c.enter_context(nc.sbuf_tensor(name, shape, dt))

        slots = nc.dram_tensor("slots", [NBLK * BLK, 2 * P], F16).ap()
        results = nc.dram_tensor("results", [NBLK * BLK, P], F32).ap()

        X = sb("X", [P, NT, P], F32)
        ADJ = sb("ADJ", [P, NT, NODES], I32)
        MASK = sb("MASK", [P, NT, P], F16)
        W1 = sb("W1", [P, 2, E * HID], F16)
        W2 = sb("W2", [P, 2, E * CH * P], F16)
        ROWS = sb("ROWS", [P, NT, 2 * P], F16)
        ident = sb("ident", [P, P], F16)
        identf = sb("identf", [P, P], F32)
        before = sb("before", [P, P], F16)
        ones = sb("ones", [P, P], F16)
        ones16 = sb("ones16", [1, P], F16)
        hold = sb("hold", [P, 1], F32)
        mhalf = sb("mhalf", [P, GT], F32)
        revidx = sb("revidx", [P, E], F32)
        WHH = sb("WHH", [P, 2, 3 * P], F16)
        WIH = sb("WIH", [P, LAYERS, 2, 3 * P], F16)
        WREL = sb("WREL", [P, 3, 2, 2 * P], F16)
        WGATE = sb("WGATE", [P, 2, 2, E], F16)
        VT = sb("VT", [P, 96], F32)
        gru_b = sb("gru_b", [P, 4], F32)
        b2rows = sb("b2rows", [1, 2, 2, E * P], F16)
        relbias = sb("relbias", [1, 2, 2 * P], F16)
        gate_b = sb("gate_b", [P, 2, E], F32)
        S = sb("S", [P, NT, E], F32)
        prob = sb("prob", [P, 2, NT], F32)
        pos = sb("pos", [P, 2, NT], I32)
        owner = sb("owner", [P, NBLK], I32)
        general = sb("general", [P, 1], I32)

        C_B1A, C_B1B, C_LNG, C_LNB, C_IH, C_HH, C_WG = 0, 32, 64, 72, 80, 83, 86
        NV = C_WG + E

        banks = [ctx.enter_context(nc.psum_tensor(f"bank{i}", [P, 512], F32)) for i in range(8)]

        setup(nc, ins, locals())
        gated_graph(nc, locals())
        route(nc, locals(), "1")
        scatter(nc, locals(), "1")
        experts(nc, locals(), "1", ACT.Relu, C_B1A, 0)
        second_weights(nc, ins, locals())
        relational(nc, ins, locals())
        route(nc, locals(), "2")
        scatter(nc, locals(), "2")
        experts(nc, locals(), "2", ACT.Gelu, C_B1B, 1)
        combine(nc, locals())


def setup(nc, ins, k):
    X, ADJ, MASK, W1, W2, ROWS = k["X"], k["ADJ"], k["MASK"], k["W1"], k["W2"], k["ROWS"]
    banks, VT, NT, NBLK = k["banks"], k["VT"], k["NT"], k["NBLK"]
    ident, identf = k["ident"], k["identf"]
    with ExitStack() as ctx:
        def sb(name, shape, dt):
            return ctx.enter_context(nc.sbuf_tensor(name, shape, dt))

        def sem(name):
            return ctx.enter_context(nc.semaphore(name))

        V = sb("V", [P, P], F32)
        SM = sb("SM", [P, 15, P], F32)
        ST = sb("ST", [P, 12, P], F32)
        b2f = sb("b2f", [1, 2, E * P], F32)
        rbf = sb("rbf", [1, 2 * P], F32)
        wr = sb("wr", [P, E], F32)
        gbf = sb("gbf", [P, 2, E], F32)
        cnt = sb("cnt", [P, 2], F32)
        cnth = sb("cnth", [P, 1], F32)
        onesf = sb("onesf", [P, P], F32)
        zero = sb("zero", [P, 4 * P], F16)
        prod = sb("prod", [P, 6, 3 * P], F32)
        STG = sb("STG", [P, E * HID], F32)
        SPL = ROWS[:, :, :].rearrange("p t c -> p (t c)")[:, 0:2 * E * HID].rearrange("p (s n) -> p s n", s=2)

        loaded = sem("small_loaded")
        x_loaded = sem("x_loaded")
        adj_loaded = sem("adj_loaded")
        w1_loaded, w2_loaded = sem("w1_loaded"), sem("w2_loaded")
        zeroed = sem("slots_zeroed")
        consts = sem("consts")
        pchain, vchain, achain = sem("pool_chain"), sem("dve_chain"), sem("act_chain")
        small_ps, small_sb = sem("small_ps"), sem("small_sb")
        split_ready, t_ps, t_sb = sem("split_ready"), sem("t_ps"), sem("t_sb")

        nsmall = [0]
        block = ctx.enter_context(nc.Block())
        slots = k["slots"]

        @block.sync
        def _(sp):
            def small(dst, src):
                sp.dma_start(dst, src).then_inc(loaded, 16)
                nsmall[0] += 16
            rows = lambda a: a.rearrange("e (c p) -> (e c) p", p=P)
            small(V[0:32, :], rows(ins["L0_ffn_b1"]))
            small(V[32:64, :], rows(ins["L1_ffn_b1"]))
            small(V[64:72, :], ins["L1_ffn_ln_g"])
            small(V[72:80, :], ins["L1_ffn_ln_b"])
            small(V[80:83, :], ins["L0_gnn_b_ih"].rearrange("(c p) -> c p", p=P))
            small(V[83:86, :], ins["L0_gnn_b_hh"].rearrange("(c p) -> c p", p=P))
            small(V[86:94, :], ins["L0_ffn_Wg"])
            small(SM[:, 0:3, :], ins["L0_gnn_w_ih"].rearrange("(c p) d -> p c d", p=P))
            small(SM[:, 3:6, :], ins["L0_gnn_w_hh"].rearrange("(c p) d -> p c d", p=P))
            small(SM[:, 6:9, :], ins["L0_gnn_weight"].rearrange("l d e -> d l e"))
            for n, w in enumerate(("loop", "fwd", "bwd")):
                small(SM[:, 9 + n, :], ins[f"L1_gnn_W_{w}"])
                small(SM[:, 12 + n, :], ins[f"L1_gnn_Wg_{w}"])
            small(b2f[:, 0, :], ins["L0_ffn_b2"].rearrange("(a e) d -> a (e d)", a=1))
            small(b2f[:, 1, :], ins["L1_ffn_b2"].rearrange("(a e) d -> a (e d)", a=1))
            small(rbf[:, 0:P], ins["L1_gnn_b_loop"])
            small(rbf[:, P:2 * P], ins["L1_gnn_bg_loop"])
            small(wr[:, :], ins["L1_ffn_Wr"])
            small(gbf[:, 0, :], ins["L0_ffn_bg"].rearrange("(a e) -> a e", a=1).to_broadcast([P, E]))
            small(gbf[:, 1, :], ins["L1_ffn_br"].rearrange("(a e) -> a e", a=1).to_broadcast([P, E]))
            sp.dma_start(STG[:, :].rearrange("p (n d) -> p n d", d=P),
                         ins["L0_ffn_W1"].rearrange("e (c p) d -> p (e c) d", p=P)).then_inc(w1_loaded, 16)
            sp.dma_start(X[:, :, :], k["x_v"]).then_inc(x_loaded, 16)
            sp.wait_ge(split_ready, 2)
            sp.dma_start(STG[:, :].rearrange("p (e h) -> p e h", e=E),
                         ins["L0_ffn_W2"].rearrange("e d h -> d e h")).then_inc(w2_loaded, 16)
            sp.wait_ge(x_loaded, 16)

        NSMALL = nsmall[0]

        @block.gpsimd
        def _(pool):
            pool.memset(zero[:, :], 0.0).then_inc(pchain, 1)
            pool.memset(ident[:, :], 0.0).then_inc(pchain, 1)
            pool.memset(identf[:, :], 0.0).then_inc(pchain, 1)
            pool.memset(k["before"][:, :], 0.0).then_inc(pchain, 1)
            pool.memset(k["ones"][:, :], 1.0)
            pool.memset(k["mhalf"][:, :], -0.5)
            pool.memset(onesf[:, :], 1.0)
            pool.memset(k["ones16"][:, :], AS).then_inc(consts, 1)
            pool.wait_ge(pchain, 4)
            for m in (ident, identf):
                pool.affine_select(out=m[:, :], in_=m[:, :], compare_op=ALU.not_equal, fill=1.0, base=0,
                                   pattern=[[-1, P]], channel_multiplier=1).then_inc(consts, 1)
            pool.affine_select(out=k["before"][:, :], in_=k["before"][:, :], compare_op=ALU.is_ge, fill=1.0,
                               base=0, pattern=[[-1, P]], channel_multiplier=1).then_inc(consts, 1)
            for e in range(E):
                pool.memset(k["revidx"][:, e:e + 1], float(E - e)).then_inc(pchain, 1)
            pool.memset(MASK[:, :, :], 0.0).then_inc(pchain, 1)
            pool.wait_ge(adj_loaded, 16)
            pool.wait_ge(pchain, 5 + E)
            pool.tensor_scalar(MASK[0:NODES, :, 0:NODES], ADJ[0:NODES, :, :], 0, 0, ALU.is_equal, ALU.is_equal)\
                .then_inc(pchain, 1)
            pool.wait_ge(pchain, 6 + E)
            pool.tensor_scalar(MASK[NODES:P, :, NODES:P], ADJ[NODES:P, :, :], 0, 0, ALU.is_equal, ALU.is_equal)

        @block.scalar
        def _(act):
            act.dma_start(ADJ[:, :, :], k["adj_v"]).then_inc(adj_loaded, 16)
            act.wait_ge(pchain, 1)
            zrows = slots.rearrange("(n p r) c -> n p (r c)", p=P, r=2)
            for n in range(zrows.shape[0]):
                act.dma_start(zrows[n], zero[:, :]).then_inc(zeroed, 16)
            act.wait_ge(w1_loaded, 16)
            act.activation(SPL[:, 0, :], STG[:, :], ACT.Copy, scale=WS).then_inc(split_ready, 1)
            for b in range(16):
                act.wait_ge(t_ps, b + 1)
                act.activation(W1[:, b // 8, (b % 8) * 512:(b % 8 + 1) * 512],
                               banks[4 + b % 4][:, 0:256].bitcast(F16), ACT.Copy).then_inc(t_sb, 1)
            act.wait_ge(w2_loaded, 16)
            act.activation(SPL[:, 0, :], STG[:, :], ACT.Copy, scale=WS).then_inc(split_ready, 1)
            for b in range(16, 32):
                act.wait_ge(t_ps, b + 1)
                act.activation(W2[:, b // 8 - 2, (b % 8) * 512:(b % 8 + 1) * 512],
                               banks[4 + b % 4][:, 0:256].bitcast(F16), ACT.Copy).then_inc(t_sb, 1)
            act.wait_ge(zeroed, 16 * zrows.shape[0])

        @block.tensor
        def _(pe):
            pe.wait_ge(consts, 4)
            pe.wait_ge(loaded, NSMALL)
            pe.wait_ge(vchain, 1)
            pe.transpose(banks[0][:, 0:k["NV"]], V[0:k["NV"], :], identf[0:k["NV"], 0:k["NV"]]).then_inc(small_ps, 1)
            for n, src in enumerate([0, 1, 2, 3, 4, 5, 6, 7, 8, 12, 13, 14]):
                pe.transpose(banks[1 + n // 4][:, n % 4 * P:(n % 4 + 1) * P], SM[:, src, :],
                             identf[:, :]).then_inc(small_ps, 1)
            pe.wait_ge(small_sb, 4)
            for l in range(LAYERS):
                pe.matmul(banks[l][:, 0:3 * P], ST[:, 6 + l, :], flat(ST[:, 0:3, :]),
                          start=True, stop=True).then_inc(small_ps, 1)
            pe.wait_ge(small_sb, 7)
            for n in range(3):
                pe.matmul(banks[n][:, 0:P], SM[:, 9 + n, :], ST[:, 9 + n, :], start=True, stop=True)
                pe.transpose(banks[n][:, P:2 * P], SM[:, 9 + n, :], identf[:, :]).then_inc(small_ps, 1)
            for b in range(32):
                if b % 16 == 0:
                    pe.wait_ge(split_ready, 2 + 2 * (b // 16))
                if b >= 4:
                    pe.wait_ge(t_sb, b - 3)
                for q in range(4):
                    n = (b % 8) * 4 + q
                    last = pe.transpose(banks[4 + b % 4][:, q * 64:(q + 1) * 64].bitcast(F16),
                                        SPL[:, b // 8 % 2, n * P:(n + 1) * P], ident[:, :])
                last.then_inc(t_ps, 1)

        @block.vector
        def _(dve):
            done = [0]

            def link(i):
                done[0] += 1
                i.then_inc(vchain, 1)
                dve.wait_ge(vchain, done[0])

            def split(hi, lo, src, scale):
                link(dve.tensor_scalar(hi, src, scale, None, ALU.mult))
                dve.scalar_tensor_tensor(out=lo, in0=src, scalar=scale, in1=hi, op0=ALU.mult, op1=ALU.subtract)

            dve.memset(cnt[:, :], 0.0)
            link(dve.memset(k["general"][:, :], 0))
            dve.wait_ge(loaded, NSMALL)
            for m in range(2):
                split(k["b2rows"][:, m, 0, :], k["b2rows"][:, m, 1, :], b2f[:, m, :], WS)
            split(k["relbias"][:, 0, :], k["relbias"][:, 1, :], rbf[:, :], WS)
            split(k["WGATE"][:, 1, 0, :], k["WGATE"][:, 1, 1, :], wr[:, :], WS)
            dve.tensor_scalar(flat(k["gate_b"][:, :, :]), flat(gbf[:, :, :]), PS, None, ALU.mult)
            dve.wait_ge(small_ps, 1)
            dve.tensor_copy(VT[:, 0:k["NV"]], banks[0][:, 0:k["NV"]]).then_inc(small_sb, 1)
            for n in range(3):
                dve.wait_ge(small_ps, 5 + 4 * n)
                dve.tensor_copy(flat(ST[:, 4 * n:4 * n + 4, :]), banks[1 + n][:, :]).then_inc(small_sb, 1)
            dve.wait_ge(small_sb, 4)
            dve.tensor_tensor(k["gru_b"][:, 0:2], VT[:, k["C_IH"]:k["C_IH"] + 2], VT[:, k["C_HH"]:k["C_HH"] + 2], ALU.add)
            dve.tensor_copy(k["gru_b"][:, 2:3], VT[:, k["C_IH"] + 2:k["C_IH"] + 3])
            dve.tensor_scalar(k["gru_b"][:, 3:4], VT[:, k["C_HH"] + 2:k["C_HH"] + 3], PS, None, ALU.mult)
            split(k["WGATE"][:, 0, 0, :], k["WGATE"][:, 0, 1, :], VT[:, k["C_WG"]:k["C_WG"] + E], WS)
            split(k["WHH"][:, 0, :], k["WHH"][:, 1, :], flat(ST[:, 3:6, :]), WS)
            for l in range(LAYERS):
                dve.wait_ge(small_ps, 14 + l)
                dve.tensor_copy(prod[:, l, :], banks[l][:, 0:3 * P]).then_inc(small_sb, 1)
            dve.wait_ge(small_sb, 7)
            for l in range(LAYERS):
                split(k["WIH"][:, l, 0, :], k["WIH"][:, l, 1, :], prod[:, l, :], WS)
            for n in range(3):
                dve.wait_ge(small_ps, 17 + n)
                link(dve.tensor_copy(prod[:, 3 + n, P:2 * P], banks[n][:, 0:P]))
                link(dve.tensor_copy(prod[:, 3 + n, 0:P], banks[n][:, P:2 * P]))
                split(k["WREL"][:, n, 0, :], k["WREL"][:, n, 1, :], prod[:, 3 + n, 0:2 * P], WS)
            for m in range(2):
                dve.wait_ge(split_ready, 1 + 2 * m)
                if m:
                    dve.wait_ge(t_ps, 16)
                dve.scalar_tensor_tensor(out=SPL[:, 1, :], in0=STG[:, :], scalar=WS, in1=SPL[:, 0, :],
                                         op0=ALU.mult, op1=ALU.subtract).then_inc(split_ready, 1)


def normalise(dve, k, x_of, out_of, st, mv, rstd, sems, n):
    stats_done, aggr_done, var_done, rstd_done, norm_done = sems
    dve.memset(k["hold"][:, :], 0.0)
    for q in range(GT):
        i = dve.bn_stats(st[:, q, :], x_of(q))
    i.then_inc(stats_done, 1)
    dve.wait_ge(stats_done, n)
    dve.memset(k["hold"][:, :], 0.0)
    for q in range(GT):
        i = dve.bn_aggr(mv[:, q, :], st[:, q, :])
    i.then_inc(aggr_done, 1)
    dve.wait_ge(aggr_done, n)
    dve.tensor_scalar(mv[:, :, 1], mv[:, :, 1], EPS, None, ALU.add).then_inc(var_done, 1)
    dve.wait_ge(rstd_done, n)
    for q in range(GT):
        i = dve.tensor_scalar(out_of(q), x_of(q), mv[:, q, 0:1], rstd[:, q:q + 1], ALU.subtract, ALU.mult)
    i.then_inc(norm_done, 1)


def root(pool, k, mv, rstd, sems, n):
    pool.wait_ge(sems[2], n)
    pool.tensor_tensor(rstd[:, :], mv[:, :, 1], k["mhalf"][:, :], ALU.pow).then_inc(sems[3], 1)


def tile_of(buf, t):
    return flat(buf[:, bass.ds(t, 1), :])


def tiles_of(buf, t, n):
    return buf[:, bass.ds(t, n), :]


def passes(pe, out, lhs, rhs, start, stop):
    pe.matmul(out, lhs(0), rhs(0), start=start, stop=False, skip_group_check=True)
    pe.matmul(out, lhs(0), rhs(1), start=False, stop=False, skip_group_check=True)
    return pe.matmul(out, lhs(1), rhs(0), start=False, stop=stop, skip_group_check=True)


def gated_graph(nc, k):
    X, MASK, ROWS, WHH, WIH, WGATE = k["X"], k["MASK"], k["ROWS"], k["WHH"], k["WIH"], k["WGATE"]
    ident, gru_b, S, gate_b, banks, PAIRS = k["ident"], k["gru_b"], k["S"], k["gate_b"], k["banks"], k["PAIRS"]
    with ExitStack() as ctx:
        def sb(name, shape, dt):
            return ctx.enter_context(nc.sbuf_tensor(name, shape, dt))

        def sem(name):
            return ctx.enter_context(nc.semaphore("a_" + name))

        two = range(2)
        norm = [sb(f"a_norm{p}", [P, GT, P], F32) for p in two]
        tok = [sb(f"a_tok{p}", [P, 2, GT, P], F16) for p in two]
        hT = [sb(f"a_hT{p}", [P, 2, GW], F16) for p in two]
        H = [sb(f"a_H{p}", [P, GW], F32) for p in two]
        agg = [sb(f"a_agg{p}", [P, 2, GW], F16) for p in two]
        R = [sb(f"a_R{p}", [P, GW], F32) for p in two]
        Z = [sb(f"a_Z{p}", [P, GW], F32) for p in two]
        N = [sb(f"a_N{p}", [P, GW], F32) for p in two]
        T = [sb(f"a_T{p}", [P, GW], F32) for p in two]
        st = [sb(f"a_st{p}", [P, GT, 6], F32) for p in two]
        mv = [sb(f"a_mv{p}", [P, GT, 2], F32) for p in two]
        rstd = [sb(f"a_rstd{p}", [P, GT], F32) for p in two]

        lns = [sem(n) for n in ("stats", "aggr", "var", "rstd", "norm")]
        hi0, lo0, in_ps, hT_sb, H_sb = (sem(n) for n in ("hi0", "lo0", "in_ps", "hT_sb", "H_sb"))
        x_half, x_new, hi1, lo1, rows_ps, rowsT, score_ps, score, rows_kept = (
            sem(n) for n in ("x_half", "x_new", "hi1", "lo1", "rows_ps", "rowsT", "score_ps", "score", "rows_kept"))
        agg_ps, agg_hi, agg_lo, hn_ps, r_ps, z_ps, n_ps, r_sb, z_sb = (
            sem(n) for n in ("agg_ps", "agg_hi", "agg_lo", "hn_ps", "r_ps", "z_ps", "n_ps", "r_sb", "z_sb"))
        t1, t2, n_sb, d_sb, e_sb, h_new, h_hi, h_lo, tok_ps, tok_sb = (
            sem(n) for n in ("t1", "t2", "n_sb", "d_sb", "e_sb", "h_new", "h_hi", "h_lo", "tok_ps", "tok_sb"))
        AG, TR = banks[0:2], banks[2:4]
        BR, BZ, BH, BN = banks[4:8]
        TRh = [b[:, :].bitcast(F16).rearrange("p (s n) -> p s n", s=2) for b in TR]

        block = ctx.enter_context(nc.Block())

        @block.tensor
        def _(pe):
            def h_parts(n, p):
                wait_from(pe, r_sb, n)
                passes(pe, BR[:, :], lambda s: WHH[:, s, 0:P], lambda s: hT[p][:, s, :], True, False)
                wait_from(pe, z_sb, n)
                passes(pe, BZ[:, :], lambda s: WHH[:, s, P:2 * P], lambda s: hT[p][:, s, :], True, False)
                wait_from(pe, t1, n)
                passes(pe, BH[:, :], lambda s: WHH[:, s, 2 * P:], lambda s: hT[p][:, s, :], True, True)\
                    .then_inc(hn_ps, 1)

            def agg_parts(n, l, p):
                pe.wait_ge(agg_lo, n + 1)
                passes(pe, BR[:, :], lambda s: WIH[:, l, s, 0:P], lambda s: agg[p][:, s, :], False, True)\
                    .then_inc(r_ps, 1)
                passes(pe, BZ[:, :], lambda s: WIH[:, l, s, P:2 * P], lambda s: agg[p][:, s, :], False, True)\
                    .then_inc(z_ps, 1)
                wait_from(pe, t2, n)
                passes(pe, BN[:, :], lambda s: WIH[:, l, s, 2 * P:], lambda s: agg[p][:, s, :], True, True)\
                    .then_inc(n_ps, 1)

            def aggregate(n, g, p):
                for q in range(GT):
                    for s in range(2):
                        i = pe.matmul(AG[p][:, q * P:(q + 1) * P], tok[p][:, s, q, :], tile_of(MASK, 4 * g + q),
                                      start=(q == 0 and s == 0), stop=(s == 1), skip_group_check=True)
                i.then_inc(agg_ps, 1)

            def turn_over(dst, src):
                for s in range(2):
                    for q in range(GT):
                        i = pe.transpose(dst[:, s, q * P:(q + 1) * P], src(s, q), ident[:, :])
                return i

            def pair(it):
                for p in two:
                    g = 2 * it + p
                    pe.wait_ge(lo0, g + 1)
                    wait_from(pe, rowsT, g - 1)
                    turn_over(TRh[p], lambda s, q: tok[p][:, s, q, :]).then_inc(in_ps, 1)
                for l in range(LAYERS):
                    for p in two:
                        n, g = 6 * it + 2 * l + p, 2 * it + p
                        if l:
                            pe.wait_ge(h_lo, n - 1)
                            wait_from(pe, tok_sb, 4 * it + 2 * (l - 2) + p + 1 if l == 2 else 0)
                            turn_over(TRh[p], lambda s, q: hT[p][:, s, q * P:(q + 1) * P]).then_inc(tok_ps, 1)
                        else:
                            pe.wait_ge(hT_sb, g + 1)
                            pe.wait_ge(H_sb, g + 1)
                        if p == 0:
                            h_parts(n, p)
                        if l:
                            pe.wait_ge(tok_sb, 4 * it + 2 * (l - 1) + p + 1)
                        aggregate(n, g, p)
                    n = 6 * it + 2 * l
                    agg_parts(n, l, 0)
                    h_parts(n + 1, 1)
                    agg_parts(n + 1, l, 1)
                for p in two:
                    g = 2 * it + p
                    pe.wait_ge(h_lo, 6 * it + 5 + p)
                    turn_over(TRh[p], lambda s, q: hT[p][:, s, q * P:(q + 1) * P]).then_inc(tok_ps, 1)
                for p in two:
                    g = 2 * it + p
                    pe.wait_ge(lo1, g + 1)
                    turn_over(TRh[p], lambda s, q: tok[p][:, s, q, :]).then_inc(rows_ps, 1)
                for p in two:
                    g = 2 * it + p
                    pe.wait_ge(rowsT, g + 1)
                    for q in range(GT):
                        i = passes(pe, AG[p][:, q * E:(q + 1) * E], lambda s: hT[p][:, s, q * P:(q + 1) * P],
                                   lambda s: WGATE[:, 0, s, :], q == 0, True)
                    i.then_inc(score_ps, 1)

            turns(pe, PAIRS, pair)

        @block.scalar
        def _(act):
            def pair(it):
                for p in two:
                    act.wait_ge(lns[4], 4 * it + p + 1)
                    if p is not None:
                        wait_from(act, rows_kept, 2 * it + p - 1)
                    act.activation(flat(tok[p][:, 0, :, :]), flat(norm[p][:, :, :]), ACT.Copy, scale=AS)\
                        .then_inc(hi0, 1)
                for p in two:
                    act.wait_ge(in_ps, 2 * it + p + 1)
                    act.activation(flat(hT[p][:, :, :]), flat(TRh[p]), ACT.Copy).then_inc(hT_sb, 1)
                for l in range(LAYERS):
                    n = 6 * it + 2 * l

                    def agg_part(p):
                        act.wait_ge(agg_ps, n + p + 1)
                        act.activation(agg[p][:, 0, :], AG[p][:, :], ACT.Copy).then_inc(agg_hi, 1)

                    def r_z(p):
                        act.wait_ge(r_ps, n + p + 1)
                        act.activation(R[p][:, :], BR[:, :], ACT.Sigmoid, bias=gru_b[:, 0:1], scale=1 / PS)\
                            .then_inc(r_sb, 1)
                        act.wait_ge(z_ps, n + p + 1)
                        act.activation(Z[p][:, :], BZ[:, :], ACT.Sigmoid, bias=gru_b[:, 1:2], scale=1 / PS)\
                            .then_inc(z_sb, 1)

                    def new(p):
                        act.wait_ge(t2, n + p + 1)
                        act.activation(N[p][:, :], T[p][:, :], ACT.Tanh, bias=gru_b[:, 2:3], scale=1 / PS)\
                            .then_inc(n_sb, 1)

                    def hi(p):
                        act.wait_ge(h_new, n + p + 1)
                        act.activation(hT[p][:, 0, :], H[p][:, :], ACT.Copy).then_inc(h_hi, 1)

                    def back(p):
                        if l < LAYERS - 1:
                            act.wait_ge(tok_ps, 6 * it + 2 * l + p + 1)
                            act.activation(tok[p][:, :, :, :].rearrange("p s q d -> p (s q d)"), flat(TRh[p]),
                                           ACT.Copy).then_inc(tok_sb, 1)

                    agg_part(0)
                    agg_part(1)
                    r_z(0)
                    new(0)
                    hi(0)
                    r_z(1)
                    new(1)
                    back(0)
                    hi(1)
                    back(1)
                for p in two:
                    act.wait_ge(lns[4], 4 * it + p + 3)
                    act.activation(flat(tok[p][:, 0, :, :]), flat(norm[p][:, :, :]), ACT.Copy, scale=AS)\
                        .then_inc(hi1, 1)
                for p in two:
                    act.wait_ge(rows_ps, 2 * it + p + 1)
                    act.activation(flat(hT[p][:, :, :]), flat(TRh[p]), ACT.Copy).then_inc(rowsT, 1)

            turns(act, PAIRS, pair)

        @block.vector
        def _(dve):
            def lo_part(p):
                return dve.scalar_tensor_tensor(out=flat(tok[p][:, 1, :, :]), in0=flat(norm[p][:, :, :]), scalar=AS,
                                                in1=flat(tok[p][:, 0, :, :]), op0=ALU.mult, op1=ALU.subtract)

            def pair(it):
                for p in two:
                    g = 2 * it + p
                    normalise(dve, k, lambda q: tile_of(X, 4 * g + q), lambda q: norm[p][:, q, :],
                              st[p], mv[p], rstd[p], lns, 4 * it + p + 1)
                for p in two:
                    dve.wait_ge(hi0, 2 * it + p + 1)
                    lo_part(p).then_inc(lo0, 1)
                for p in two:
                    dve.wait_ge(hT_sb, 2 * it + p + 1)
                    dve.tensor_tensor(H[p][:, :], TRh[p][:, 1, :], hT[p][:, 0, :], ALU.add).then_inc(H_sb, 1)
                for l in range(LAYERS):
                    n = 6 * it + 2 * l

                    def agg_part(p):
                        dve.wait_ge(agg_hi, n + p + 1)
                        dve.tensor_tensor(agg[p][:, 1, :], AG[p][:, :], agg[p][:, 0, :], ALU.subtract)\
                            .then_inc(agg_lo, 1)

                    def inner(p):
                        dve.wait_ge(r_sb, n + p + 1)
                        dve.scalar_tensor_tensor(out=T[p][:, :], in0=BH[:, :], scalar=gru_b[:, 3:4], in1=R[p][:, :],
                                                 op0=ALU.add, op1=ALU.mult).then_inc(t1, 1)
                        dve.wait_ge(n_ps, n + p + 1)
                        dve.wait_ge(t1, n + p + 1)
                        dve.tensor_tensor(T[p][:, :], T[p][:, :], BN[:, :], ALU.add).then_inc(t2, 1)

                    def diff(p):
                        dve.wait_ge(n_sb, n + p + 1)
                        dve.scalar_tensor_tensor(out=T[p][:, :], in0=N[p][:, :], scalar=-AS, in1=H[p][:, :],
                                                 op0=ALU.mult, op1=ALU.add).then_inc(d_sb, 1)

                    def state(p):
                        dve.wait_ge(e_sb, n + p + 1)
                        dve.scalar_tensor_tensor(out=H[p][:, :], in0=N[p][:, :], scalar=AS, in1=T[p][:, :],
                                                 op0=ALU.mult, op1=ALU.add).then_inc(h_new, 1)

                    agg_part(0)
                    agg_part(1)
                    inner(0)
                    diff(0)
                    state(0)
                    inner(1)
                    diff(1)
                    state(1)
                for p in two:
                    g = 2 * it + p
                    xg = flat(tiles_of(X, 4 * g, GT))
                    dve.wait_ge(tok_ps, 6 * it + 5 + p)
                    dve.scalar_tensor_tensor(out=flat(norm[p][:, :, :]), in0=TRh[p][:, 0, :], scalar=1 / AS, in1=xg,
                                             op0=ALU.mult, op1=ALU.add).then_inc(x_half, 1)
                    dve.wait_ge(x_half, g + 1)
                    dve.scalar_tensor_tensor(out=xg, in0=TRh[p][:, 1, :], scalar=1 / AS,
                                             in1=flat(norm[p][:, :, :]), op0=ALU.mult, op1=ALU.add).then_inc(x_new, 1)
                for p in two:
                    g = 2 * it + p
                    dve.wait_ge(x_new, g + 1)
                    normalise(dve, k, lambda q: tile_of(X, 4 * g + q), lambda q: norm[p][:, q, :],
                              st[p], mv[p], rstd[p], lns, 4 * it + p + 3)
                for p in two:
                    dve.wait_ge(hi1, 2 * it + p + 1)
                    lo_part(p).then_inc(lo1, 1)
                for p in two:
                    g = 2 * it + p
                    dve.wait_ge(score_ps, g + 1)
                    dve.tensor_tensor(tiles_of(S, 4 * g, GT), AG[p][:, 0:GT * E].rearrange("p (q e) -> p q e", e=E),
                                      gate_b[:, 0:1, :].to_broadcast([P, GT, E]), ALU.add).then_inc(score, 1)

            turns(dve, PAIRS, pair)

        @block.gpsimd
        def _(pool):
            def pair(it):
                for p in two:
                    root(pool, k, mv[p], rstd[p], lns, 4 * it + p + 1)
                for l in range(LAYERS):
                    for p in two:
                        n = 6 * it + 2 * l + p
                        pool.wait_ge(d_sb, n + 1)
                        pool.tensor_tensor(T[p][:, :], Z[p][:, :], T[p][:, :], ALU.mult).then_inc(e_sb, 1)
                        pool.wait_ge(h_hi, n + 1)
                        pool.tensor_tensor(hT[p][:, 1, :], H[p][:, :], hT[p][:, 0, :], ALU.subtract)\
                            .then_inc(h_lo, 1)
                for p in two:
                    root(pool, k, mv[p], rstd[p], lns, 4 * it + p + 3)
                for p in two:
                    g = 2 * it + p
                    pool.wait_ge(lo1, g + 1)
                    for s in range(2):
                        i = pool.tensor_copy(tiles_of(ROWS, 4 * g, GT)[:, :, s * P:(s + 1) * P], tok[p][:, s, :, :])
                    i.then_inc(rows_kept, 1)

            turns(pool, PAIRS, pair)


def route(nc, k, tag):
    S, prob, pos, owner, revidx, banks = k["S"], k["prob"], k["pos"], k["owner"], k["revidx"], k["banks"]
    NT, NBLK = k["NT"], k["NBLK"]
    with ExitStack() as ctx:
        def sb(name, shape, dt):
            return ctx.enter_context(nc.sbuf_tensor("r" + tag + name, shape, dt))

        def sem(name):
            return ctx.enter_context(nc.semaphore("r" + tag + name))

        top = [sb(f"top{c}", [P, NT], F32) for c in range(2)]
        who = sb("who", [P, NT], F32)
        tmp = sb("tmp", [P, NT, E], F32)
        hot = [sb(f"hot{c}", [P, NT, E], F32) for c in range(2)]
        both = sb("both", [P, NT, E], F16)
        gap = sb("gap", [P, NT], F32)
        pre = [sb(f"pre{c}", [P, NT, E], F32) for c in range(2)]
        counts = sb("counts", [P, NT, E], F32)
        steps = sb("steps", [P, 2 * NBLK], F32)
        full = sb("full", [P, E, 16 * 4], F32)
        nblk = [sb(f"nblk{c}", [P, E], F32) for c in range(2)]
        nown = sb("nown", [P, E], F32)
        ends = sb("ends", [P, NBLK, E], F32)
        who_b = sb("who_b", [P, NBLK], F32)
        posf = sb("posf", [P, 2, NT], F32)
        chain, picked, ranked, iota_done, weighed = (sem(n) for n in ("chain", "picked", "ranked", "iota", "weighed"))
        MAXB = NT * P // BLK
        block = ctx.enter_context(nc.Block())

        @block.gpsimd
        def _(pool):
            pool.iota(steps[:, :], pattern=[[1, 2 * NBLK]], base=0, channel_multiplier=0,
                      allow_small_or_imprecise_dtypes=True).then_inc(iota_done, 1)

        @block.vector
        def _(dve):
            done = [0]

            def link(i):
                done[0] += 1
                i.then_inc(chain, 1)
                dve.wait_ge(chain, done[0])

            wide = lambda a: a[:, :].rearrange("p (t o) -> p t o", o=1).to_broadcast([P, NT, E])
            by_e = lambda a: a.rearrange("p (o e) -> p o e", o=1).to_broadcast([P, NT, E])
            scores = S
            for c in range(2):
                link(dve.tensor_reduce(top[c][:, :], scores[:, :, :], AX_X, ALU.max))
                link(dve.tensor_tensor(tmp[:, :, :], scores[:, :, :], wide(top[c]), ALU.is_equal))
                link(dve.tensor_tensor(tmp[:, :, :], tmp[:, :, :], by_e(revidx[:, :]), ALU.mult))
                link(dve.tensor_reduce(who[:, :], tmp[:, :, :], AX_X, ALU.max))
                link(dve.tensor_tensor(hot[c][:, :, :], by_e(revidx[:, :]), wide(who), ALU.is_equal))
                if c == 0:
                    link(dve.scalar_tensor_tensor(out=pre[0][:, :, :], in0=hot[0][:, :, :], scalar=-BIG,
                                                  in1=S[:, :, :], op0=ALU.mult, op1=ALU.add))
                    scores = pre[0]
            dve.tensor_tensor(both[:, :, :], hot[0][:, :, :], hot[1][:, :, :], ALU.add).then_inc(picked, 1)
            dve.tensor_tensor(gap[:, :], top[0][:, :], top[1][:, :], ALU.subtract).then_inc(picked, 1)
            dve.wait_ge(ranked, 2)
            dve.tensor_copy(flat(counts[:, :, :]), banks[1][:, 0:NT * E])
            link(dve.tensor_copy(flat(pre[0][:, :, :]), banks[1][:, 0:NT * E]))
            a, b, step = 0, 1, 1
            while step < NT:
                dve.tensor_copy(pre[b][:, 0:step, :], pre[a][:, 0:step, :])
                link(dve.tensor_tensor(pre[b][:, step:, :], pre[a][:, step:, :], pre[a][:, 0:NT - step, :], ALU.add))
                a, b, step = b, a, 2 * step
            dve.wait_ge(iota_done, 1)
            link(dve.tensor_scalar(full[:, :, 0:MAXB],
                                   steps[:, 0:MAXB].rearrange("p (o m) -> p o m", o=1).to_broadcast([P, E, MAXB]),
                                   float(BLK), None, ALU.mult))
            link(dve.tensor_tensor(full[:, :, 0:MAXB], full[:, :, 0:MAXB],
                                   pre[a][:, NT - 1, :].rearrange("p (e o) -> p e o", o=1).to_broadcast([P, E, MAXB]),
                                   ALU.is_lt))
            link(dve.tensor_reduce(nown[:, :], full[:, :, 0:MAXB], AX_X, ALU.add))
            link(dve.tensor_copy(nblk[0][:, :], nown[:, :]))
            c, d, step = 0, 1, 1
            while step < E:
                dve.tensor_copy(nblk[d][:, 0:step], nblk[c][:, 0:step])
                link(dve.tensor_tensor(nblk[d][:, step:], nblk[c][:, step:], nblk[c][:, 0:E - step], ALU.add))
                c, d, step = d, c, 2 * step
            link(dve.tensor_tensor(ends[:, :, :],
                                   steps[:, 0:NBLK].rearrange("p (m o) -> p m o", o=1).to_broadcast([P, NBLK, E]),
                                   nblk[c][:, :].rearrange("p (o e) -> p o e", o=1).to_broadcast([P, NBLK, E]), ALU.is_ge))
            link(dve.tensor_reduce(who_b[:, :], ends[:, :, :], AX_X, ALU.add))
            dve.tensor_scalar(owner[:, :], who_b[:, :], float(E - 1), None, ALU.min)
            link(dve.tensor_tensor(nown[:, :], nblk[c][:, :], nown[:, :], ALU.subtract))
            link(dve.tensor_scalar(nown[:, :], nown[:, :], float(BLK), None, ALU.mult))
            link(dve.tensor_tensor(pre[a][:, :, :], pre[a][:, :, :], counts[:, :, :], ALU.subtract))
            link(dve.tensor_tensor(pre[a][:, :, :], pre[a][:, :, :], by_e(nown[:, :]), ALU.add))
            link(dve.tensor_tensor(pre[a][:, :, :], pre[a][:, :, :],
                                   banks[0][:, 0:NT * E].rearrange("p (t e) -> p t e", e=E), ALU.add))
            for n in range(2):
                link(dve.tensor_tensor(tmp[:, :, :], hot[n][:, :, :], pre[a][:, :, :], ALU.mult))
                link(dve.tensor_reduce(posf[:, n, :], tmp[:, :, :], AX_X, ALU.add))
            dve.tensor_copy(flat(pos[:, :, :]), flat(posf[:, :, :]))

        @block.tensor
        def _(pe):
            pe.wait_ge(picked, 1)
            pe.matmul(banks[0][:, 0:NT * E], k["before"][:, :], flat(both[:, :, :]), start=True, stop=True)\
                .then_inc(ranked, 1)
            pe.matmul(banks[1][:, 0:NT * E], k["ones"][:, :], flat(both[:, :, :]), start=True, stop=True)\
                .then_inc(ranked, 1)

        @block.scalar
        def _(act):
            act.wait_ge(picked, 2)
            act.activation(prob[:, 0, :], gap[:, :], ACT.Sigmoid, scale=1 / PS)
            act.activation(prob[:, 1, :], gap[:, :], ACT.Sigmoid, scale=-1 / PS)


def scatter(nc, k, tag):
    with ExitStack() as ctx:
        sent = ctx.enter_context(nc.semaphore("sent" + tag))
        block = ctx.enter_context(nc.Block())

        @block.gpsimd
        def _(pool):
            for t in range(k["NT"]):
                for c in range(2):
                    pool.indirect_dma_start(
                        out=k["slots"], out_offset=bass.IndirectOffsetOnAxis(ap=k["pos"][:, c, t:t + 1], axis=0),
                        in_=k["ROWS"][:, t, :], in_offset=None).then_inc(sent, 16)
            pool.wait_ge(sent, 32 * k["NT"])


def experts(nc, k, tag, func, b1_col, m):
    W1, W2, VT, b2rows, owner, banks, ident = (k[n] for n in ("W1", "W2", "VT", "b2rows", "owner", "banks", "ident"))
    NBLK = k["NBLK"]
    x_rows = k["slots"].rearrange("(b p r) c -> p b (r c)", p=P, r=BLK // P)
    y_rows = k["results"].rearrange("(b p r) c -> p b (r c)", p=P, r=BLK // P)
    with ExitStack() as ctx:
        def sb(name, shape, dt):
            return ctx.enter_context(nc.sbuf_tensor("e" + tag + name, shape, dt))

        def sem(name):
            return ctx.enter_context(nc.semaphore("e" + tag + name))

        ring = range(RING)
        xs = [sb(f"xs{j}", [P, GT, 2, P], F16) for j in ring]
        xT = [sb(f"xT{j}", [P, 2, BLK], F16) for j in ring]
        hf = [sb(f"hf{c}", [P, BLK], F32) for c in range(CH)]
        hs = [sb(f"hs{j}", [P, 2, CH, BLK], F16) for j in ring]
        ys = [sb(f"ys{j}", [P, BLK], F32) for j in ring]
        x_loaded = [sem(f"x_loaded{j}") for j in ring]
        y_stored = [sem(f"y_stored{j}") for j in ring]
        xT_ps, xT_sb, h_ps, h_f32, h_hi, h_lo, y_ps, y_sb = (
            sem(n) for n in ("xT_ps", "xT_sb", "h_ps", "h_f32", "h_hi", "h_lo", "y_ps", "y_sb"))
        HB, TB, YB = banks[0:4], banks[4], banks[5:8]
        TBh = TB[:, :].bitcast(F16).rearrange("p (s n) -> p s n", s=2)

        def rounds(eng, step):
            for j in ring:
                step(j, j, 0)
            with eng.Fori(1, NBLK // RING - 1) as i:
                for j in ring:
                    step(RING * i + j, j, i)
            for j in ring:
                step(NBLK - RING + j, j, NBLK // RING - 1)

        last = lambda b: isinstance(b, int) and b == NBLK - 1
        block = ctx.enter_context(nc.Block())

        @block.sync
        def _(sp):
            def load(b, j):
                sp.dma_start(xs[j][:, :, :, :].rearrange("p r s d -> p (r s d)"),
                             flat(x_rows[:, bass.ds(b, 1), :])).then_inc(x_loaded[j], 16)
            for j in ring:
                load(j, j)

            def step(b, j, i):
                if not (isinstance(b, int) and b + RING >= NBLK):
                    sp.wait_ge(xT_ps, b + 1)
                    load(b + RING, j)
                sp.wait_ge(y_sb, b + 1)
                sp.dma_start(flat(y_rows[:, bass.ds(b, 1), :]), ys[j][:, :]).then_inc(y_stored[j], 16)
            rounds(sp, step)
            for j in ring:
                sp.wait_ge(y_stored[j], 16 * (NBLK // RING))

        @block.tensor
        def _(pe):
            def turn_over(b, j, i):
                pe.wait_ge(x_loaded[j], 16 * (i + 1))
                wait_from(pe, xT_sb, b)
                for s in range(2):
                    for q in range(GT):
                        t = pe.transpose(TBh[:, s, q * P:(q + 1) * P], xs[j][:, q, s, :], ident[:, :])
                t.then_inc(xT_ps, 1)

            def up(b, j, e):
                pe.wait_ge(xT_sb, b + 1)
                for c in range(CH):
                    wait_from(pe, h_f32, 4 * b + c - 3)
                    passes(pe, HB[c][:, :], lambda s: W1[:, s, bass.ds(e * HID + c * P, P)],
                           lambda s: xT[j][:, s, :], True, True).then_inc(h_ps, 1)

            def down(b, j, e):
                wait_from(pe, y_sb, b - RING + 1)
                for q in range(GT):
                    o = YB[j][:, q * P:(q + 1) * P]
                    for s in range(2):
                        pe.matmul(o, k["ones16"][:, :], b2rows[:, m, s, bass.ds(e * P, P)],
                                  start=(q == 0 and s == 0), stop=False, skip_group_check=True)
                pe.wait_ge(h_lo, 4 * b + 4)
                for q in range(GT):
                    o = YB[j][:, q * P:(q + 1) * P]
                    for c in range(CH):
                        t = passes(pe, o, lambda s: hs[j][:, s, c, q * P:(q + 1) * P],
                                   lambda s: W2[:, s, bass.ds(e * HID + c * P, P)], False, c == CH - 1)
                t.then_inc(y_ps, 1)

            def who(b):
                return pe.value_load(owner[0:1, bass.ds(b, 1)], min_val=0, max_val=E - 1)

            turn_over(0, 0, 0)
            up(0, 0, who(0))
            turn_over(1, 1, 0)

            def step(b, j, i):
                if not last(b):
                    up(b + 1, (j + 1) % RING, who(b + 1))
                if not (isinstance(b, int) and b >= NBLK - 2):
                    turn_over(b + 2, (j + 2) % RING, i + (j + 2) // RING)
                down(b, j, who(b))
            rounds(pe, step)

        @block.scalar
        def _(act):
            def step(b, j, i):
                e = act.value_load(owner[0:1, bass.ds(b, 1)], min_val=0, max_val=E - 1)
                wait_from(act, y_ps, b - RING + 1)

                def hidden(c):
                    act.wait_ge(h_ps, 4 * b + c + 1)
                    wait_from(act, h_lo, 4 * b + c - 3)
                    act.activation(hf[c][:, :], HB[c][:, :], func, bias=VT[:, bass.ds(e * CH + b1_col + c, 1)],
                                   scale=1 / PS).then_inc(h_f32, 1)

                def hi(c):
                    act.wait_ge(h_f32, 4 * b + c + 1)
                    act.activation(hs[j][:, 0, c, :], hf[c][:, :], ACT.Copy, scale=AS).then_inc(h_hi, 1)

                hidden(0)
                for c in range(1, CH):
                    hidden(c)
                    hi(c - 1)
                hi(CH - 1)
            rounds(act, step)

        @block.vector
        def _(dve):
            def turned(b, j):
                dve.wait_ge(xT_ps, b + 1)
                wait_from(dve, h_ps, 4 * (b - RING + 1))
                dve.tensor_copy(flat(xT[j][:, :, :]), flat(TBh)).then_inc(xT_sb, 1)

            def lo(b, j, c):
                dve.wait_ge(h_hi, 4 * b + c + 1)
                dve.scalar_tensor_tensor(out=hs[j][:, 1, c, :], in0=hf[c][:, :], scalar=AS, in1=hs[j][:, 0, c, :],
                                         op0=ALU.mult, op1=ALU.subtract).then_inc(h_lo, 1)

            turned(0, 0)
            for c in range(CH):
                if c == 2:
                    turned(1, 1)
                lo(0, 0, c)

            def step(b, j, i):
                for c in range(CH):
                    if c == 2 and not (isinstance(b, int) and b >= NBLK - 2):
                        turned(b + 2, (j + 2) % RING)
                    if not last(b):
                        lo(b + 1, (j + 1) % RING, c)
                dve.wait_ge(y_ps, b + 1)
                wait_from(dve, y_stored[j], i * 16)
                dve.tensor_scalar(ys[j][:, :], YB[j][:, :], 1 / PS, None, ALU.mult).then_inc(y_sb, 1)
            rounds(dve, step)


def second_weights(nc, ins, k):
    W1, W2, VT, MASK, ADJ, banks, ROWS, NT = (k[n] for n in ("W1", "W2", "VT", "MASK", "ADJ", "banks", "ROWS", "NT"))
    with ExitStack() as ctx:
        def sem(name):
            return ctx.enter_context(nc.semaphore("w_" + name))

        STG = ROWS[:, :, :].rearrange("p t c -> p (t c)")[:, 0:4 * E * HID].bitcast(F32)
        up, down = STG[:, 0:E * HID], STG[:, E * HID:2 * E * HID]
        G = ctx.enter_context(nc.sbuf_tensor("w_gain", [P, E * HID], F32))
        few = ctx.enter_context(nc.sbuf_tensor("w_few", [P, NT * NODES], F16))
        cnt = ctx.enter_context(nc.sbuf_tensor("w_cnt", [P, 1], F32))
        onesf = ctx.enter_context(nc.sbuf_tensor("w_ones", [P, P], F32))
        up_loaded, down_loaded, gained, up_hi, down_hi, b_ps, chain, ones_set, counted, total, b_new = (
            sem(n) for n in ("up_loaded", "down_loaded", "gained", "up_hi", "down_hi", "b_ps", "chain",
                             "ones_set", "counted", "total", "b_new"))
        block = ctx.enter_context(nc.Block())

        @block.sync
        def _(sp):
            sp.dma_start(up.rearrange("p (e h) -> p e h", e=E),
                         ins["L1_ffn_W1"].rearrange("e d h -> d e h")).then_inc(up_loaded, 16)
            sp.dma_start(down.rearrange("p (n d) -> p n d", d=P),
                         ins["L1_ffn_W2"].rearrange("e (c p) d -> p (e c) d", p=P)).then_inc(down_loaded, 16)

        @block.gpsimd
        def _(pool):
            pool.memset(onesf[:, :], 1.0).then_inc(ones_set, 1)
            pool.wait_ge(ones_set, 1)
            pool.tensor_scalar(MASK[0:NODES, :, 0:NODES], ADJ[0:NODES, :, :], 1, None, ALU.is_equal).then_inc(ones_set, 1)
            pool.wait_ge(ones_set, 2)
            pool.tensor_scalar(MASK[NODES:P, :, NODES:P], ADJ[NODES:P, :, :], 1, None, ALU.is_equal)

        @block.scalar
        def _(act):
            act.wait_ge(gained, 1)
            act.activation(W1[:, 0, :], G[:, :], ACT.Copy, scale=WS).then_inc(up_hi, 1)
            act.wait_ge(down_loaded, 16)
            act.activation(W2[:, 0, :], down, ACT.Copy, scale=WS).then_inc(down_hi, 1)

        @block.vector
        def _(dve):
            dve.wait_ge(up_loaded, 16)
            for e in range(E):
                i = dve.tensor_scalar(G[:, e * HID:(e + 1) * HID], up[:, e * HID:(e + 1) * HID],
                                      VT[:, k["C_LNG"] + e:k["C_LNG"] + e + 1], None, ALU.mult)
            i.then_inc(gained, 1)
            dve.tensor_scalar(few[:, :], flat(ADJ[:, :, :]), 1, RELS + 2, ALU.max, ALU.min).then_inc(chain, 1)
            dve.wait_ge(chain, 1)
            dve.tensor_scalar(few[:, :], few[:, :], 21.0, None, ALU.subtract).then_inc(chain, 1)
            dve.wait_ge(chain, 2)
            dve.tensor_tensor(few[:, :], few[:, :], few[:, :], ALU.mult).then_inc(chain, 1)
            dve.wait_ge(chain, 3)
            dve.tensor_scalar(few[:, :], few[:, :], 400.0, None, ALU.is_lt).then_inc(chain, 1)
            dve.wait_ge(chain, 4)
            dve.tensor_reduce(cnt[:, :], few[:, :], AX_X, ALU.add).then_inc(counted, 1)
            dve.wait_ge(up_hi, 1)
            dve.scalar_tensor_tensor(out=W1[:, 1, :], in0=G[:, :], scalar=WS, in1=W1[:, 0, :],
                                     op0=ALU.mult, op1=ALU.subtract)
            dve.wait_ge(down_hi, 1)
            dve.scalar_tensor_tensor(out=W2[:, 1, :], in0=down, scalar=WS, in1=W2[:, 0, :],
                                     op0=ALU.mult, op1=ALU.subtract)
            dve.wait_ge(b_ps, 1)
            dve.tensor_tensor(VT[:, k["C_B1B"]:k["C_B1B"] + E * CH], VT[:, k["C_B1B"]:k["C_B1B"] + E * CH],
                              banks[0][:, 0:E * CH], ALU.add).then_inc(b_new, 1)
            dve.wait_ge(total, 1)
            dve.tensor_copy(k["general"][:, :], banks[1][:, 0:1])

        @block.tensor
        def _(pe):
            pe.wait_ge(up_loaded, 16)
            for n in range(E * CH):
                i = pe.matmul(banks[0][:, n:n + 1], up[:, n * P:(n + 1) * P],
                              VT[:, k["C_LNB"] + n // CH:k["C_LNB"] + n // CH + 1], start=True, stop=True)
            i.then_inc(b_ps, 1)
            pe.wait_ge(ones_set, 1)
            pe.wait_ge(counted, 1)
            pe.matmul(banks[1][:, 0:1], onesf[:, :], cnt[:, :], start=True, stop=True).then_inc(total, 1)


def mix(dve, k, gathered, G, t0, first, sem_half, sem_full, n):
    for c, done in ((0, sem_half), (1, sem_full)):
        for q in range(GT):
            x = tile_of(k["X"], t0 + q)
            i = dve.scalar_tensor_tensor(out=x, in0=G[c][:, q, :], scalar=k["prob"][:, c, bass.ds(t0 + q, 1)], in1=x,
                                         op0=ALU.mult, op1=ALU.add)
        i.then_inc(done, 1)
        dve.wait_ge(done, n)


def gather(pool, k, t, c, dst, sem):
    pool.indirect_dma_start(out=dst, out_offset=None, in_=k["results"],
                            in_offset=bass.IndirectOffsetOnAxis(ap=k["pos"][:, c, t:t + 1], axis=0)).then_inc(sem, 16)


def relational(nc, ins, k):
    X, MASK, ADJ, ROWS, WREL, WGATE, S = (k[n] for n in ("X", "MASK", "ADJ", "ROWS", "WREL", "WGATE", "S"))
    ident, banks, NG, NT = k["ident"], k["banks"], k["NG"], k["NT"]
    with ExitStack() as ctx:
        def sb(name, shape, dt):
            return ctx.enter_context(nc.sbuf_tensor("c_" + name, shape, dt))

        def sem(name):
            return ctx.enter_context(nc.semaphore("c_" + name))

        two = range(2)
        G = [[sb(f"G{p}{c}", [P, GT, P], F32) for c in two] for p in two]
        norm = [sb(f"norm{p}", [P, GT, P], F32) for p in two]
        norm2 = [sb(f"norm2{p}", [P, GT, P], F32) for p in two]
        tok = [sb(f"tok{p}", [P, 2, GT, P], F16) for p in two]
        xT = [sb(f"xT{p}", [P, 2, GW], F16) for p in two]
        sg = [sb(f"sg{p}", [P, GT, P], F32) for p in two]
        val = [sb(f"val{p}", [P, GT, P], F32) for p in two]
        vs = [sb(f"vs{p}", [P, 2, GT, P], F16) for p in two]
        st, mv, rstd = ([sb(f"{n}{p}", [P, GT, w], F32) for p in two] for n, w in (("st", 6), ("mv", 2), ("rs", 1)))
        AC, AT = sb("AC", [P, GT, P], F16), sb("AT", [P, GT, P], F16)
        HG = sb("HG", [P, GT, 2, 2, P], F32)
        BB = sb("BB", [P, 2, 2, P], F32)
        SUM = sb("SUM", [P, 2, 2, P], F32)
        SIG = sb("SIG", [P, 2, P], F32)
        VG = sb("VG", [P, 2, P], F32)
        VS = sb("VS", [P, 2, 2, P], F16)
        HOT = sb("HOT", [P, 2, P], F16)
        RV = sb("RV", [P, RELS], F32)
        relrows = nc.dram_tensor("relrows", [RELS, 4 * P], F32).ap()

        gathered = [sem(f"gathered{p}") for p in two]
        half, full = sem("half"), sem("full")
        lns = [sem(n) for n in ("stats", "aggr", "var", "rstd", "norm")]
        hi_a, lo_a, a_ps, a_sb, v_ps, sg_sb, val_sb, v_hi, v_lo, rel_ps, rel_sb, x_rel = (
            sem(n) for n in ("hi_a", "lo_a", "a_ps", "a_sb", "v_ps", "sg_sb", "val_sb", "v_hi", "v_lo",
                             "rel_ps", "rel_sb", "x_rel"))
        hi_b, lo_b, b_ps, b_sb, score_ps, score, hi_c, lo_c = (
            sem(n) for n in ("hi_b", "lo_b", "b_ps", "b_sb", "score_ps", "score", "hi_c", "lo_c"))
        rv_set, rows_packed, g_zero, g_clip, g_ps, g_at, g_hg_ps, g_hg, g_bias, g_sum, g_sig, g_val, g_hi, g_ops, g_used, g_direct = (
            sem("g_" + n) for n in ("rv", "packed", "zero", "clip", "ps", "at", "hgps", "hg", "bias", "sum", "sig",
                                    "val", "hi", "ops", "used", "direct"))
        TR, V, RL, SC, GB = banks[0:2], banks[2:4], banks[4:6], banks[6], banks[7]
        TRh = [b[:, :].bitcast(F16).rearrange("p (s n) -> p s n", s=2) for b in TR]
        Vv = [b[:, :].rearrange("p (q s d) -> p q s d", q=2, s=2) for b in V]
        GBh = GB[:, 0:256].bitcast(F16)

        def if_general(eng):
            n = eng.value_load(k["general"][0:1, 0:1], min_val=0, max_val=NT * P * NODES)
            return eng.If(n > 0)

        block = ctx.enter_context(nc.Block())

        @block.gpsimd
        def _(pool):
            for r in range(RELS):
                i = pool.memset(RV[:, r:r + 1], float(r + 2))
            i.then_inc(rv_set, 1)
            def fetch(g, q):
                if g < NG:
                    if g >= 2 and q == 0:
                        pool.wait_ge(full, g - 1)
                    for c in two:
                        gather(pool, k, GT * g + q, c, G[g % 2][c][:, q, :], gathered[g % 2])

            def roots(it, n, p):
                root(pool, k, mv[p], flat(rstd[p][:, :, :]), lns, 6 * it + n)

            for g in two:
                for q in range(GT):
                    fetch(g, q)
            for it in range(NG // 2):
                g = 2 * it + 2
                for p in two:
                    roots(it, p + 1, p)
                for q in range(GT):
                    fetch(g, q)
                roots(it, 3, 0)
                roots(it, 4, 0)
                for q in range(GT):
                    fetch(g + 1, q)
                roots(it, 5, 1)
                roots(it, 6, 1)

        @block.sync
        def _(sp):
            for n, name in enumerate(("b_fwd", "bg_fwd", "b_bwd", "bg_bwd")):
                sp.dma_start(relrows[:, n * P:(n + 1) * P], ins["L1_gnn_" + name]).then_inc(rows_packed, 16)
            sp.wait_ge(rows_packed, 64)
            with if_general(sp):
                def group(g):
                    def rel(r):
                        wait_from(sp, g_used, (g * RELS + r) * GT if not isinstance(g, int) or not isinstance(r, int)
                                  else (g * RELS + r) * GT)
                        sp.dma_start(BB[:, :, :, :].rearrange("p a b c -> p (a b c)"),
                                     relrows[bass.ds(r, 1), :].to_broadcast([P, 4 * P])).then_inc(g_bias, 16)
                    turns(sp, RELS, rel)
                turns(sp, NG, group)

        @block.tensor
        def _(pe):
            def turn_over(p, sem_in, v, done):
                pe.wait_ge(sem_in, v)
                for s in range(2):
                    for q in range(GT):
                        i = pe.transpose(TRh[p][:, s, q * P:(q + 1) * P], tok[p][:, s, q, :], ident[:, :])
                i.then_inc(done, 1)

            def general(g, p):
                with if_general(pe):
                    pe.wait_ge(g_clip, g + 1)
                    for q in range(GT):
                        i = pe.transpose(GBh[:, q * P:(q + 1) * P], AC[:, q, :], ident[:, :])
                    i.then_inc(g_ps, 1)
                    pe.wait_ge(g_at, g + 1)
                    for q in range(GT):
                        wait_from(pe, g_hg, GT * g + q)
                        passes(pe, GB[:, :].rearrange("p (a b) -> p a b", a=2), lambda s: xT[p][:, s, q * P:(q + 1) * P],
                               lambda s: WREL[:, 1:3, s, :], True, True).then_inc(g_hg_ps, 1)

                    def rel(r):
                        for q in range(GT):
                            pe.wait_ge(g_ops, (g * RELS + r) * GT + q + 1)
                            for d in two:
                                for s in two:
                                    i = pe.matmul(RL[p][:, q * P:(q + 1) * P], HOT[:, d, :], VS[:, s, d, :],
                                                  start=False, stop=True, skip_group_check=True)
                            i.then_inc(g_used, 1)
                    turns(pe, RELS, rel)

            def pair(it):
                for p in two:
                    g = 2 * it + p
                    turn_over(p, lo_a, g + 1, a_ps)
                for p in two:
                    g = 2 * it + p
                    pe.wait_ge(a_sb, g + 1)
                    for q in range(GT):
                        v = q // 2
                        if q % 2 == 0:
                            wait_from(pe, val_sb, 2 * g + v - 1)
                        o = Vv[v][:, q % 2, :, :].rearrange("p s d -> p (s d)")
                        for s in range(2):
                            pe.matmul(o, k["ones16"][:, :], k["relbias"][:, s, :], start=(q % 2 == 0 and s == 0),
                                      stop=False, skip_group_check=True)
                        i = passes(pe, o, lambda s: xT[p][:, s, q * P:(q + 1) * P], lambda s: WREL[:, 0, s, :],
                                   False, True)
                        if q % 2:
                            i.then_inc(v_ps, 1)
                for p in two:
                    g = 2 * it + p
                    pe.wait_ge(v_lo, g + 1)
                    for q in range(GT):
                        for s in range(2):
                            i = pe.matmul(RL[p][:, q * P:(q + 1) * P], tile_of(MASK, GT * g + q), vs[p][:, s, q, :],
                                          start=(q == 0 and s == 0), stop=True, skip_group_check=True)
                    i.then_inc(g_direct, 1)
                    general(g, p)
                    pe.wait_ge(g_direct, g + 1)
                    pe.transpose(SC[:, 256:320].bitcast(F16), ident[:, :], ident[:, :]).then_inc(rel_ps, 1)
                for p in two:
                    turn_over(p, lo_b, 2 * it + p + 1, b_ps)
                for p in two:
                    g = 2 * it + p
                    pe.wait_ge(b_sb, g + 1)
                    wait_from(pe, score, g)
                    for q in range(GT):
                        i = passes(pe, SC[:, q * E:(q + 1) * E], lambda s: xT[p][:, s, q * P:(q + 1) * P],
                                   lambda s: WGATE[:, 1, s, :], q == 0, True)
                    i.then_inc(score_ps, 1)
            turns(pe, NG // 2, pair)

        @block.scalar
        def _(act):
            def hi(p, src, done, v, done_hi):
                act.wait_ge(done, v)
                act.activation(flat(tok[p][:, 0, :, :]), flat(src[p][:, :, :]), ACT.Copy, scale=AS).then_inc(done_hi, 1)

            def general(g, p):
                with if_general(act):
                    def rel(r):
                        for q in range(GT):
                            act.wait_ge(g_sum, (g * RELS + r) * GT + q + 1)
                            act.activation(SIG[:, :, :], SUM[:, :, 1, :], ACT.Sigmoid).then_inc(g_sig, 1)
                    turns(act, RELS, rel)

            def pair(it):
                for p in two:
                    hi(p, norm, lns[4], 3 * (2 * it + p) + 1 if False else 6 * it + p + 1, hi_a)
                for p in two:
                    g = 2 * it + p
                    act.wait_ge(a_ps, g + 1)
                    act.activation(flat(xT[p][:, :, :]), flat(TRh[p]), ACT.Copy).then_inc(a_sb, 1)
                for p in two:
                    g = 2 * it + p
                    for v in two:
                        act.wait_ge(v_ps, 2 * g + v + 1)
                        act.activation(sg[p][:, 2 * v:2 * v + 2, :], Vv[v][:, :, 1, :], ACT.Sigmoid, scale=1 / PS)\
                            .then_inc(sg_sb, 1)
                    act.wait_ge(val_sb, 2 * g + 2)
                    act.activation(flat(vs[p][:, 0, :, :]), flat(val[p][:, :, :]), ACT.Copy).then_inc(v_hi, 1)
                for p in two:
                    g = 2 * it + p
                    general(g, p)
                    act.wait_ge(rel_ps, g + 1)
                    act.activation(flat(sg[p][:, :, :]), RL[p][:, :], ACT.Relu, scale=1 / WS).then_inc(rel_sb, 1)
                for p in two:
                    hi(p, norm, lns[4], 6 * it + 2 * p + 3, hi_b)
                for p in two:
                    g = 2 * it + p
                    act.wait_ge(b_ps, g + 1)
                    act.activation(flat(xT[p][:, :, :]), flat(TRh[p]), ACT.Copy).then_inc(b_sb, 1)
                    act.wait_ge(lns[4], 6 * it + 2 * p + 4)
                    act.activation(tiles_of(ROWS, GT * g, GT)[:, :, 0:P], norm2[p][:, :, :], ACT.Copy, scale=AS)\
                        .then_inc(hi_c, 1)
            turns(act, NG // 2, pair)

        @block.vector
        def _(dve):
            def lo(out, src, in1):
                return dve.scalar_tensor_tensor(out=out, in0=src, scalar=AS, in1=in1, op0=ALU.mult, op1=ALU.subtract)

            def general(g, p):
                with if_general(dve):
                    wait_from(dve, g_used, g * RELS * GT)
                    dve.memset(AC[:, :, :], 0.0).then_inc(g_zero, 1)
                    dve.wait_ge(g_zero, g + 1)
                    for h in two:
                        part = slice(h * NODES, (h + 1) * NODES)
                        i = dve.tensor_scalar(AC[part, :, part], tiles_of(ADJ, GT * g, GT)[part, :, :], 0, RELS + 2,
                                              ALU.max, ALU.min)
                    i.then_inc(g_clip, 1)
                    dve.wait_ge(g_ps, g + 1)
                    dve.tensor_copy(flat(AT[:, :, :]), GBh).then_inc(g_at, 1)
                    for q in range(GT):
                        dve.wait_ge(g_hg_ps, GT * g + q + 1)
                        dve.tensor_scalar(HG[:, q, :, :, :].rearrange("p a b c -> p (a b c)"), GB[:, :], 1 / PS, None,
                                          ALU.mult).then_inc(g_hg, 1)
                    dve.wait_ge(g_hg, GT * g + GT)
                    dve.wait_ge(rv_set, 1)

                    def rel(r):
                        dve.wait_ge(g_bias, 16 * (g * RELS + r + 1))
                        for q in range(GT):
                            m = (g * RELS + r) * GT + q
                            dve.tensor_tensor(SUM[:, :, :, :].rearrange("p a b c -> p (a b c)"),
                                              HG[:, q, :, :, :].rearrange("p a b c -> p (a b c)"),
                                              BB[:, :, :, :].rearrange("p a b c -> p (a b c)"), ALU.add).then_inc(g_sum, 1)
                            dve.wait_ge(g_sig, m + 1)
                            dve.scalar_tensor_tensor(out=VG[:, :, :], in0=SUM[:, :, 0, :], scalar=WS, in1=SIG[:, :, :],
                                                     op0=ALU.mult, op1=ALU.mult).then_inc(g_val, 1)
                            wait_from(dve, g_used, m)
                            dve.tensor_scalar(HOT[:, 0, :], AT[:, q, :], RV[:, bass.ds(r, 1)], None, ALU.is_equal)
                            dve.tensor_scalar(HOT[:, 1, :], AC[:, q, :], RV[:, bass.ds(r, 1)], None, ALU.is_equal)
                            dve.wait_ge(g_val, m + 1)
                            dve.tensor_copy(VS[:, 0, :, :], VG[:, :, :]).then_inc(g_hi, 1)
                            dve.wait_ge(g_hi, m + 1)
                            dve.tensor_tensor(VS[:, 1, :, :], VG[:, :, :], VS[:, 0, :, :], ALU.subtract)\
                                .then_inc(g_ops, 1)
                    turns(dve, RELS, rel)

            def pair(it):
                for p in two:
                    g = 2 * it + p
                    dve.wait_ge(gathered[p], 16 * 2 * GT * (it + 1))
                    mix(dve, k, gathered, G[p], GT * g, None, half, full, g + 1)
                    normalise(dve, k, lambda q: tile_of(X, GT * g + q), lambda q: norm[p][:, q, :],
                              st[p], mv[p], flat(rstd[p][:, :, :]), lns, 6 * it + p + 1)
                for p in two:
                    dve.wait_ge(hi_a, 2 * it + p + 1)
                    lo(flat(tok[p][:, 1, :, :]), flat(norm[p][:, :, :]), flat(tok[p][:, 0, :, :])).then_inc(lo_a, 1)
                for p in two:
                    g = 2 * it + p
                    for v in two:
                        dve.wait_ge(sg_sb, 2 * g + v + 1)
                        dve.scalar_tensor_tensor(out=val[p][:, 2 * v:2 * v + 2, :], in0=Vv[v][:, :, 0, :], scalar=1 / AS,
                                                 in1=sg[p][:, 2 * v:2 * v + 2, :], op0=ALU.mult, op1=ALU.mult)\
                            .then_inc(val_sb, 1)
                for p in two:
                    dve.wait_ge(v_hi, 2 * it + p + 1)
                    dve.tensor_tensor(flat(vs[p][:, 1, :, :]), flat(val[p][:, :, :]), flat(vs[p][:, 0, :, :]),
                                      ALU.subtract).then_inc(v_lo, 1)
                for p in two:
                    general(2 * it + p, p)
                for p in two:
                    g = 2 * it + p
                    xg = flat(tiles_of(X, GT * g, GT))
                    dve.wait_ge(rel_sb, g + 1)
                    dve.tensor_tensor(xg, xg, flat(sg[p][:, :, :]), ALU.add).then_inc(x_rel, 1)
                    dve.wait_ge(x_rel, g + 1)
                    normalise(dve, k, lambda q: tile_of(X, GT * g + q), lambda q: norm[p][:, q, :],
                              st[p], mv[p], flat(rstd[p][:, :, :]), lns, 6 * it + 2 * p + 3)
                    dve.wait_ge(lns[4], 6 * it + 2 * p + 3)
                    normalise(dve, k, lambda q: norm[p][:, q, :], lambda q: norm2[p][:, q, :],
                              st[p], mv[p], flat(rstd[p][:, :, :]), lns, 6 * it + 2 * p + 4)
                    dve.wait_ge(hi_b, g + 1)
                    lo(flat(tok[p][:, 1, :, :]), flat(norm[p][:, :, :]), flat(tok[p][:, 0, :, :])).then_inc(lo_b, 1)
                for p in two:
                    g = 2 * it + p
                    dve.wait_ge(hi_c, g + 1)
                    rows = tiles_of(ROWS, GT * g, GT)
                    lo(rows[:, :, P:2 * P], norm2[p][:, :, :], rows[:, :, 0:P]).then_inc(lo_c, 1)
                    dve.wait_ge(score_ps, g + 1)
                    dve.tensor_tensor(tiles_of(S, GT * g, GT), SC[:, 0:GT * E].rearrange("p (q e) -> p q e", e=E),
                                      k["gate_b"][:, 1:2, :].to_broadcast([P, GT, E]), ALU.add).then_inc(score, 1)
            turns(dve, NG // 2, pair)


def combine(nc, k):
    NG, X = k["NG"], k["X"]
    RG = 4
    with ExitStack() as ctx:
        def sem(name):
            return ctx.enter_context(nc.semaphore("d_" + name))
        G = [[ctx.enter_context(nc.sbuf_tensor(f"d_G{p}{c}", [P, GT, P], F32)) for c in range(2)] for p in range(RG)]
        gathered = [sem(f"gathered{p}") for p in range(RG)]
        half, full, stored = sem("half"), sem("full"), sem("stored")
        block = ctx.enter_context(nc.Block())

        @block.gpsimd
        def _(pool):
            for g in range(NG):
                if g >= RG:
                    pool.wait_ge(full, g - RG + 1)
                for q in range(GT):
                    for c in range(2):
                        gather(pool, k, GT * g + q, c, G[g % RG][c][:, q, :], gathered[g % RG])

        @block.vector
        def _(dve):
            def four(it):
                for p in range(RG):
                    g = RG * it + p
                    dve.wait_ge(gathered[p], 16 * 2 * GT * (it + 1))
                    mix(dve, k, gathered, G[p], GT * g, None, half, full, g + 1)
            turns(dve, NG // RG, four)

        @block.sync
        def _(sp):
            def group(g):
                sp.wait_ge(full, g + 1)
                sp.dma_start(k["out_v"][:, bass.ds(GT * g, GT), :], tiles_of(X, GT * g, GT)).then_inc(stored, 16)
            turns(sp, NG, group)
            sp.wait_ge(stored, 16 * NG)


_UNUSED = ("nodemask",)


def kernel(**inputs):
    import numpy as _np
    import concourse.bacc as _bacc
    from concourse import mybir as _mybir
    from concourse.bass_utils import run_bass_kernel_spmd as _run

    nc = _bacc.Bacc("TRN2", target_bir_lowering=False, num_devices=1)
    arrays, args = {}, {}
    for name in inputs:
        if name in _UNUSED:
            continue
        a = _np.ascontiguousarray(inputs[name])
        arrays[f"in_{name}_dram"] = a
        args[name] = nc.dram_tensor(f"in_{name}_dram", a.shape, _mybir.dt.from_np(a.dtype), kind="ExternalInput").ap()
    shape = inputs["x"].shape
    out = nc.dram_tensor("out_dram", shape, _mybir.dt.from_np(_np.dtype("float32")), kind="ExternalOutput").ap()
    program(nc, args, out)
    r = _run(nc, [arrays], core_ids=[0])
    return r.results[0]["out_dram"]
```

```python
from contextlib import ExitStack

import concourse.bass as bass
from concourse import mybir

F32 = mybir.dt.float32
F16 = mybir.dt.float16
I32 = mybir.dt.int32
ALU = mybir.AluOpType
ACT = mybir.ActivationFunctionType
AX_X = mybir.AxisListType.X

P = 128
NODES = 64
E = 8
HID = 512
CH = HID // P
LAYERS = 3
GT = 4
GW = GT * P
BLK = 512
RING = 3
RELS = 39
AS = 16.0
WS = 64.0
PS = AS * WS
EPS = 1e-5
BIG = 3.0e38


def flat(ap):
    return ap.rearrange("p a b -> p (a b)")


def wait_from(eng, sem, value):
    if not isinstance(value, int) or value > 0:
        eng.wait_ge(sem, value)


def turns(eng, n, step):
    step(0)
    with eng.Fori(1, n) as i:
        step(i)


def program(nc, ins, out):
    TOK = ins["x"].shape[0] * NODES
    NT = TOK // P
    NG = NT // GT
    NBLK = 2 * TOK // BLK + E - 1
    NBLK += -NBLK % RING
    NZERO = NBLK * BLK // (2 * P)
    PAIRS = NG // 2
    x_v = ins["x"].rearrange("(t g) n d -> (g n) t d", g=2)
    out_v = out.rearrange("(t g) n d -> (g n) t d", g=2)
    adj_v = ins["adj"].rearrange("(t g) s n -> (g s) t n", g=2)

    with ExitStack() as ctx:
        def sb(name, shape, dt, c=ctx):
            return c.enter_context(nc.sbuf_tensor(name, shape, dt))

        slots = nc.dram_tensor("slots", [NBLK * BLK, 2 * P], F16).ap()
        kept = [nc.dram_tensor(f"kept{m}", [P, 2 * E * HID], F16).ap() for m in range(2)]
        results = nc.dram_tensor("results", [NBLK * BLK, P], F32).ap()

        X = sb("X", [P, NT, P], F32)
        ADJ = sb("ADJ", [P, NT, NODES], I32)
        MASK = sb("MASK", [P, NT, P], F16)
        W1 = sb("W1", [P, 2, E * HID], F16)
        W2 = sb("W2", [P, 2, E * CH * P], F16)
        ROWS = sb("ROWS", [P, NT, 2 * P], F16)
        ident = sb("ident", [P, P], F16)
        identf = sb("identf", [P, P], F32)
        before = sb("before", [P, P], F16)
        ones = sb("ones", [P, P], F16)
        ones16 = sb("ones16", [1, P], F16)
        hold = sb("hold", [P, 1], F32)
        mhalf = sb("mhalf", [P, GT], F32)
        revidx = sb("revidx", [P, E], F32)
        WHH = sb("WHH", [P, 2, 3 * P], F16)
        WIH = sb("WIH", [P, LAYERS, 2, 3 * P], F16)
        WREL = sb("WREL", [P, 3, 2, 2 * P], F16)
        WGATE = sb("WGATE", [P, 2, 2, E], F16)
        VT = sb("VT", [P, 96], F32)
        gru_b = sb("gru_b", [P, 5], F32)
        b2rows = sb("b2rows", [1, 2, 2, E * P], F16)
        relbias = sb("relbias", [1, 2, 2 * P], F16)
        gate_b = sb("gate_b", [P, 2, E], F32)
        S = sb("S", [P, NT, E], F32)
        prob = sb("prob", [P, 2, NT], F32)
        pos = sb("pos", [P, 2, NT], I32)
        owner = sb("owner", [P, NBLK], I32)
        general = sb("general", [P, 1], I32)

        C_B1A, C_B1B, C_LNG, C_LNB, C_IH, C_HH, C_WG = 0, 32, 64, 72, 80, 83, 86
        NV = C_WG + E

        banks = [ctx.enter_context(nc.psum_tensor(f"bank{i}", [P, 512], F32)) for i in range(8)]

        dma_sems = [ctx.enter_context(nc.semaphore(f"indexed{i}")) for i in range(8)]

        zeroed = ctx.enter_context(nc.semaphore("slots_zeroed"))

        phase(nc, setup, ins, locals())
        phase(nc, first_norm, locals())
        phase(nc, gated_graph, locals())
        phase(nc, router, locals())
        phase(nc, route, locals(), "1")
        phase(nc, scatter_weights, ins, locals(), dma_sems[0])
        phase(nc, experts, locals(), "1", ACT.Relu, C_B1A, 0)
        phase(nc, relational, ins, locals())
        phase(nc, route, locals(), "2")
        phase(nc, scatter_reload, locals(), dma_sems[1])
        phase(nc, experts, locals(), "2", ACT.Gelu, C_B1B, 1)
        combine(nc, locals())


def phase(nc, run, *args):
    had = list(nc.free_semaphores)
    run(nc, *args)
    used = sorted(had[:had.index(nc.free_semaphores[0])])
    if not used:
        return
    with nc.Block() as block:
        @block.gpsimd
        def _(pool):
            first = used[0]
            for a, b in zip(used, used[1:] + [None]):
                if b != a + 1:
                    pool.sem_clear(range(first, a + 1))
                    first = b


def setup(nc, ins, k):
    X, ADJ, MASK = k["X"], k["ADJ"], k["MASK"]
    banks, VT, NT, NBLK = k["banks"], k["VT"], k["NT"], k["NBLK"]
    ident, identf = k["ident"], k["identf"]
    with ExitStack() as ctx:
        def sb(name, shape, dt):
            return ctx.enter_context(nc.sbuf_tensor(name, shape, dt))

        def sem(name):
            return ctx.enter_context(nc.semaphore(name))

        V = sb("V", [P, P], F32)
        SM = sb("SM", [P, 15, P], F32)
        ST = sb("ST", [P, 12, P], F32)
        b2f = sb("b2f", [1, 2, E * P], F32)
        rbf = sb("rbf", [1, 2 * P], F32)
        wr = sb("wr", [P, E], F32)
        gbf = sb("gbf", [P, 2, E], F32)
        zero = k["W1"][:, 0, 0:4 * P]
        prod = sb("prod", [P, 6, 3 * P], F32)

        loaded = sem("small_loaded")
        x_loaded = sem("x_loaded")
        adj_loaded = sem("adj_loaded")
        zeroed = k["zeroed"]
        consts = sem("consts")
        pchain, vchain = sem("pool_chain"), sem("dve_chain")
        small_ps, small_sb = sem("small_ps"), sem("small_sb")
        mask_zero = sem("mask_zero")

        nsmall = [0]
        block = ctx.enter_context(nc.Block())
        slots = k["slots"]

        @block.sync
        def _(sp):
            def small(dst, src):
                sp.dma_start(dst, src).then_inc(loaded, 16)
                nsmall[0] += 16
            rows = lambda a: a.rearrange("e (c p) -> (e c) p", p=P)
            small(V[0:32, :], rows(ins["L0_ffn_b1"]))
            small(V[32:64, :], rows(ins["L1_ffn_b1"]))
            small(V[64:72, :], ins["L1_ffn_ln_g"])
            small(V[72:80, :], ins["L1_ffn_ln_b"])
            small(V[80:83, :], ins["L0_gnn_b_ih"].rearrange("(c p) -> c p", p=P))
            small(V[83:86, :], ins["L0_gnn_b_hh"].rearrange("(c p) -> c p", p=P))
            small(V[86:94, :], ins["L0_ffn_Wg"])
            small(SM[:, 0:3, :], ins["L0_gnn_w_ih"].rearrange("(c p) d -> p c d", p=P))
            small(SM[:, 3:6, :], ins["L0_gnn_w_hh"].rearrange("(c p) d -> p c d", p=P))
            small(SM[:, 6:9, :], ins["L0_gnn_weight"].rearrange("l d e -> d l e"))
            for n, w in enumerate(("loop", "fwd", "bwd")):
                small(SM[:, 9 + n, :], ins[f"L1_gnn_W_{w}"])
                small(SM[:, 12 + n, :], ins[f"L1_gnn_Wg_{w}"])
            small(b2f[:, 0, :], ins["L0_ffn_b2"].rearrange("(a e) d -> a (e d)", a=1))
            small(b2f[:, 1, :], ins["L1_ffn_b2"].rearrange("(a e) d -> a (e d)", a=1))
            small(rbf[:, 0:P], ins["L1_gnn_b_loop"])
            small(rbf[:, P:2 * P], ins["L1_gnn_bg_loop"])
            small(wr[:, :], ins["L1_ffn_Wr"])
            small(gbf[:, 0, :], ins["L0_ffn_bg"].rearrange("(a e) -> a e", a=1).to_broadcast([P, E]))
            small(gbf[:, 1, :], ins["L1_ffn_br"].rearrange("(a e) -> a e", a=1).to_broadcast([P, E]))
            sp.dma_start(X[:, :, :], k["x_v"]).then_inc(x_loaded, 16)
            sp.wait_ge(x_loaded, 16)

        NSMALL = nsmall[0]

        @block.gpsimd
        def _(pool):
            pool.memset(zero, 0.0).then_inc(pchain, 1)
            pool.memset(ident[:, :], 0.0).then_inc(pchain, 1)
            pool.memset(identf[:, :], 0.0).then_inc(pchain, 1)
            pool.memset(k["before"][:, :], 0.0).then_inc(pchain, 1)
            pool.memset(k["ones"][:, :], 1.0)
            pool.memset(k["mhalf"][:, :], -0.5)
            pool.memset(k["ones16"][:, :], AS).then_inc(consts, 1)
            pool.wait_ge(pchain, 4)
            for m in (ident, identf):
                pool.affine_select(out=m[:, :], in_=m[:, :], compare_op=ALU.not_equal, fill=1.0, base=0,
                                   pattern=[[-1, P]], channel_multiplier=1).then_inc(consts, 1)
            pool.affine_select(out=k["before"][:, :], in_=k["before"][:, :], compare_op=ALU.is_ge, fill=1.0,
                               base=0, pattern=[[-1, P]], channel_multiplier=1).then_inc(consts, 1)
            for e in range(E):
                pool.memset(k["revidx"][:, e:e + 1], float(E - e)).then_inc(pchain, 1)
            pool.memset(MASK[:, :, :], 0.0).then_inc(mask_zero, 1)

        @block.scalar
        def _(act):
            act.dma_start(ADJ[:, :, :], k["adj_v"]).then_inc(adj_loaded, 16)
            act.wait_ge(pchain, 1)
            zrows = slots.rearrange("(n p r) c -> n p (r c)", p=P, r=2)
            for n in range(zrows.shape[0]):
                act.dma_start(zrows[n], zero).then_inc(zeroed, 16)

        @block.tensor
        def _(pe):
            pe.wait_ge(consts, 4)
            pe.wait_ge(loaded, NSMALL)
            pe.wait_ge(vchain, 1)
            pe.transpose(banks[0][:, 0:k["NV"]], V[0:k["NV"], :], identf[0:k["NV"], 0:k["NV"]]).then_inc(small_ps, 1)
            for n, src in enumerate([0, 1, 2, 3, 4, 5, 6, 7, 8, 12, 13, 14]):
                pe.transpose(banks[1 + n // 4][:, n % 4 * P:(n % 4 + 1) * P], SM[:, src, :],
                             identf[:, :]).then_inc(small_ps, 1)
            pe.wait_ge(small_sb, 4)
            for l in range(LAYERS):
                pe.matmul(banks[l][:, 0:3 * P], ST[:, 6 + l, :], flat(ST[:, 0:3, :]),
                          start=True, stop=True).then_inc(small_ps, 1)
            pe.wait_ge(small_sb, 7)
            for n in range(3):
                pe.matmul(banks[n][:, 0:P], SM[:, 9 + n, :], ST[:, 9 + n, :], start=True, stop=True)
                pe.transpose(banks[n][:, P:2 * P], SM[:, 9 + n, :], identf[:, :]).then_inc(small_ps, 1)

        @block.vector
        def _(dve):
            done = [0]

            def link(i):
                done[0] += 1
                i.then_inc(vchain, 1)
                dve.wait_ge(vchain, done[0])

            def split(hi, lo, src, scale):
                link(dve.tensor_scalar(hi, src, scale, None, ALU.mult))
                dve.scalar_tensor_tensor(out=lo, in0=src, scalar=scale, in1=hi, op0=ALU.mult, op1=ALU.subtract)

            link(dve.memset(k["general"][:, :], 0))
            dve.wait_ge(loaded, NSMALL)
            for m in range(2):
                split(k["b2rows"][:, m, 0, :], k["b2rows"][:, m, 1, :], b2f[:, m, :], WS)
            split(k["relbias"][:, 0, :], k["relbias"][:, 1, :], rbf[:, :], WS)
            split(k["WGATE"][:, 1, 0, :], k["WGATE"][:, 1, 1, :], wr[:, :], WS)
            dve.tensor_scalar(flat(k["gate_b"][:, :, :]), flat(gbf[:, :, :]), PS, None, ALU.mult)
            dve.wait_ge(small_ps, 1)
            dve.tensor_copy(VT[:, 0:k["NV"]], banks[0][:, 0:k["NV"]]).then_inc(small_sb, 1)
            for n in range(3):
                dve.wait_ge(small_ps, 5 + 4 * n)
                dve.tensor_copy(flat(ST[:, 4 * n:4 * n + 4, :]), banks[1 + n][:, :]).then_inc(small_sb, 1)
            dve.wait_ge(small_sb, 4)
            dve.tensor_tensor(k["gru_b"][:, 0:2], VT[:, k["C_IH"]:k["C_IH"] + 2], VT[:, k["C_HH"]:k["C_HH"] + 2], ALU.add)
            dve.tensor_scalar(k["gru_b"][:, 3:4], VT[:, k["C_HH"] + 2:k["C_HH"] + 3], PS, None, ALU.mult)
            link(dve.tensor_copy(k["gru_b"][:, 2:3], VT[:, k["C_IH"] + 2:k["C_IH"] + 3]))
            dve.tensor_scalar(k["gru_b"][:, 4:5], k["gru_b"][:, 1:2], -1.0, None, ALU.mult)
            split(k["WGATE"][:, 0, 0, :], k["WGATE"][:, 0, 1, :], VT[:, k["C_WG"]:k["C_WG"] + E], WS)
            split(k["WHH"][:, 0, :], k["WHH"][:, 1, :], flat(ST[:, 3:6, :]), WS)
            for l in range(LAYERS):
                dve.wait_ge(small_ps, 14 + l)
                dve.tensor_copy(prod[:, l, :], banks[l][:, 0:3 * P]).then_inc(small_sb, 1)
            dve.wait_ge(small_sb, 7)
            for l in range(LAYERS):
                split(k["WIH"][:, l, 0, :], k["WIH"][:, l, 1, :], prod[:, l, :], WS)
            for n in range(3):
                dve.wait_ge(small_ps, 17 + n)
                link(dve.tensor_copy(prod[:, 3 + n, P:2 * P], banks[n][:, 0:P]))
                link(dve.tensor_copy(prod[:, 3 + n, 0:P], banks[n][:, P:2 * P]))
                split(k["WREL"][:, n, 0, :], k["WREL"][:, n, 1, :], prod[:, 3 + n, 0:2 * P], WS)
            dve.wait_ge(adj_loaded, 16)
            dve.wait_ge(mask_zero, 1)
            for h in range(2):
                part = slice(h * NODES, (h + 1) * NODES)
                dve.tensor_scalar(MASK[part, :, part], ADJ[part, :, :], 0, None, ALU.not_equal)


def tile_of(buf, t):
    return flat(buf[:, bass.ds(t, 1), :])


def tiles_of(buf, t, n):
    return buf[:, bass.ds(t, n), :]


def passes(pe, out, lhs, rhs, start, stop):
    pe.matmul(out, lhs(0), rhs(0), start=start, stop=False, skip_group_check=True)
    pe.matmul(out, lhs(0), rhs(1), start=False, stop=False, skip_group_check=True)
    return pe.matmul(out, lhs(1), rhs(0), start=False, stop=stop, skip_group_check=True)


def part_norm(dve, k, x_of, st, mv, sems, n):
    stats_done, aggr_done, var_done = sems[0:3]
    dve.memset(k["hold"][:, :], 0.0)
    for q in range(GT):
        i = dve.bn_stats(st[:, q, :], x_of(q))
    i.then_inc(stats_done, 1)
    dve.wait_ge(stats_done, n)
    dve.memset(k["hold"][:, :], 0.0)
    for q in range(GT):
        i = dve.bn_aggr(mv[:, q, :], st[:, q, :])
    i.then_inc(aggr_done, 1)
    dve.wait_ge(aggr_done, n)
    dve.tensor_scalar(mv[:, :, 1], mv[:, :, 1], EPS, None, ALU.add).then_inc(var_done, 1)


def root(pool, k, mv, rstd, sems, n):
    pool.wait_ge(sems[2], n)
    pool.tensor_tensor(rstd[:, :], mv[:, :, 1], k["mhalf"][:, :], ALU.pow).then_inc(sems[3], 1)


def finish_norm(dve, x_of, out_of, mv, rstd, sems, n):
    dve.wait_ge(sems[3], n)
    for q in range(GT):
        i = dve.tensor_scalar(out_of(q), x_of(q), mv[:, q, 0:1], rstd[:, q:q + 1], ALU.subtract, ALU.mult)
    i.then_inc(sems[4], 1)


def lo_part(dve, out, src, hi):
    return dve.scalar_tensor_tensor(out=out, in0=src, scalar=AS, in1=hi, op0=ALU.mult, op1=ALU.subtract)


def staggered(eng, n, ring, stages):
    deepest = max(d for d, _ in stages)
    first = -(-(deepest + ring) // ring)

    def step(s, j):
        for d, do in stages:
            if not isinstance(s, int) or 0 <= s - d < n:
                do(s - d, (j - d) % ring)
    for s in range(min(first * ring, n + deepest)):
        step(s, s % ring)
    if first < n // ring:
        with eng.Fori(first, n // ring) as i:
            for j in range(ring):
                step(ring * i + j, j)
    for s in range(max(first, n // ring) * ring, n + deepest):
        step(s, s % ring)


def first_norm(nc, k):
    X, ROWS, NG = k["X"], k["ROWS"], k["NG"]
    with ExitStack() as ctx:
        def sb(name, shape):
            return [ctx.enter_context(nc.sbuf_tensor(f"n_{name}{p}", shape, F32)) for p in range(2)]
        norm, st, mv, rstd = sb("norm", [P, GT, P]), sb("st", [P, GT, 6]), sb("mv", [P, GT, 2]), sb("rstd", [P, GT])
        lns = [ctx.enter_context(nc.semaphore("n_" + n)) for n in ("stats", "aggr", "var", "rstd", "norm")]
        hi, lo = (ctx.enter_context(nc.semaphore("n_" + n)) for n in ("hi", "lo"))
        block = ctx.enter_context(nc.Block())

        @block.vector
        def _(dve):
            def stats(g, p):
                part_norm(dve, k, lambda q: tile_of(X, GT * g + q), st[p], mv[p], lns, g + 1)

            def norms(g, p):
                wait_from(dve, hi, g - 1)
                finish_norm(dve, lambda q: tile_of(X, GT * g + q), lambda q: norm[p][:, q, :], mv[p], rstd[p], lns, g + 1)

            def los(g, p):
                dve.wait_ge(hi, g + 1)
                rows = tiles_of(ROWS, GT * g, GT)
                lo_part(dve, rows[:, :, P:2 * P], norm[p][:, :, :], rows[:, :, 0:P]).then_inc(lo, 1)
            staggered(dve, NG, 2, [(0, stats), (2, los), (1, norms)])

        @block.scalar
        def _(act):
            def his(g, p):
                act.wait_ge(lns[4], g + 1)
                act.activation(tiles_of(ROWS, GT * g, GT)[:, :, 0:P], norm[p][:, :, :], ACT.Copy, scale=AS).then_inc(hi, 1)
            staggered(act, NG, 2, [(0, his)])

        @block.gpsimd
        def _(pool):
            staggered(pool, NG, 2, [(0, lambda g, p: root(pool, k, mv[p], rstd[p], lns, g + 1))])


def gated_graph(nc, k):
    X, MASK, ROWS, WHH, WIH = k["X"], k["MASK"], k["ROWS"], k["WHH"], k["WIH"]
    ident, gru_b, banks, PAIRS = k["ident"], k["gru_b"], k["banks"], k["PAIRS"]
    with ExitStack() as ctx:
        def sb(name, shape, dt):
            return ctx.enter_context(nc.sbuf_tensor(name, shape, dt))

        def sem(name):
            return ctx.enter_context(nc.semaphore("a_" + name))

        two = range(2)
        tok = [sb(f"a_tok{p}", [P, 2, GT, P], F16) for p in two]
        hT = [sb(f"a_hT{p}", [P, 2, GW], F16) for p in two]
        H = [sb(f"a_H{p}", [P, GW], F32) for p in two]
        agg = [sb(f"a_agg{p}", [P, 2, GW], F16) for p in two]
        R = [sb(f"a_R{p}", [P, GW], F32) for p in two]
        Z = [sb(f"a_Z{p}", [P, GW], F32) for p in two]
        Y = [sb(f"a_Y{p}", [P, GW], F32) for p in two]
        N = [sb(f"a_N{p}", [P, GW], F32) for p in two]
        T = [sb(f"a_T{p}", [P, GW], F32) for p in two]

        start_ps, start_hi, start_lo, start_H, end_ps, x_half, x_new = (
            sem(n) for n in ("start_ps", "start_hi", "start_lo", "start_H", "end_ps", "x_half", "x_new"))
        agg_ps, agg_hi, agg_lo, r_ps, z_ps, n_ps, r_sb, z_sb, y_sb = (
            sem(n) for n in ("agg_ps", "agg_hi", "agg_lo", "r_ps", "z_ps", "n_ps", "r_sb", "z_sb", "y_sb"))
        t1, t2, n_sb, u_sb, zh_sb, h_new, h_hi, h_lo = (
            sem(n) for n in ("t1", "t2", "n_sb", "u_sb", "zh_sb", "h_new", "h_hi", "h_lo"))
        tok_ps, tok_sb = sem("tok_ps"), sem("tok_sb")
        AG, TR = banks[0:2], banks[2:4]
        BR, BZ, BH, BN = banks[4:8]
        halves = lambda b: b[:, :].bitcast(F16).rearrange("p (s n) -> p s n", s=2)
        TRh, AGh = [halves(b) for b in TR], [halves(b) for b in AG]

        block = ctx.enter_context(nc.Block())

        @block.tensor
        def _(pe):
            def h_parts(n, p):
                wait_from(pe, r_sb, n)
                passes(pe, BR[:, :], lambda s: WHH[:, s, 0:P], lambda s: hT[p][:, s, :], True, False)
                wait_from(pe, y_sb, n)
                passes(pe, BZ[:, :], lambda s: WHH[:, s, P:2 * P], lambda s: hT[p][:, s, :], True, False)
                wait_from(pe, t1, n)
                passes(pe, BH[:, :], lambda s: WHH[:, s, 2 * P:], lambda s: hT[p][:, s, :], True, True)

            def agg_parts(n, l, p):
                pe.wait_ge(agg_lo, n + 1)
                passes(pe, BR[:, :], lambda s: WIH[:, l, s, 0:P], lambda s: agg[p][:, s, :], False, True)\
                    .then_inc(r_ps, 1)
                wait_from(pe, t2, n)
                passes(pe, BN[:, :], lambda s: WIH[:, l, s, 2 * P:], lambda s: agg[p][:, s, :], True, True)\
                    .then_inc(n_ps, 1)
                passes(pe, BZ[:, :], lambda s: WIH[:, l, s, P:2 * P], lambda s: agg[p][:, s, :], False, True)\
                    .then_inc(z_ps, 1)

            def aggregate(g, l, p):
                for q in range(GT):
                    for s in range(2):
                        h = tok[p][:, s, q, :] if l else tile_of(ROWS, GT * g + q)[:, s * P:(s + 1) * P]
                        i = pe.matmul(AG[p][:, q * P:(q + 1) * P], h, tile_of(MASK, GT * g + q),
                                      start=(q == 0 and s == 0), stop=(s == 1), skip_group_check=True)
                i.then_inc(agg_ps, 1)

            def turn_over(dst, p):
                for s in range(2):
                    for q in range(GT):
                        i = pe.transpose(dst[:, s, q * P:(q + 1) * P], hT[p][:, s, q * P:(q + 1) * P], ident[:, :])
                return i

            def start(g, p):
                for q in range(GT):
                    for s in range(2):
                        i = pe.matmul(TR[p][:, q * P:(q + 1) * P], tile_of(ROWS, GT * g + q)[:, s * P:(s + 1) * P],
                                      ident[:, :], start=(q == 0 and s == 0), stop=(s == 1), skip_group_check=True)
                i.then_inc(start_ps, 1)

            def end(it, p):
                pe.wait_ge(h_lo, 6 * it + 5 + p)
                turn_over(AGh[p], p).then_inc(end_ps, 1)

            def pair(it):
                for l in range(LAYERS):
                    n = 6 * it + 2 * l
                    for p in two:
                        g = 2 * it + p
                        if l:
                            pe.wait_ge(h_lo, n + p - 1)
                            turn_over(TRh[p], p).then_inc(tok_ps, 1)
                        else:
                            if not isinstance(it, int) or it > 0:
                                end(it - 1, p)
                            start(g, p)
                        if p == 0:
                            if l == 0:
                                pe.wait_ge(start_lo, g + 1)
                            h_parts(n, 0)
                        if l:
                            pe.wait_ge(tok_sb, 4 * it + 2 * (l - 1) + p + 1)
                        else:
                            wait_from(pe, x_new, g - 1)
                        aggregate(g, l, p)
                    agg_parts(n, l, 0)
                    if l == 0:
                        pe.wait_ge(start_lo, 2 * it + 2)
                    h_parts(n + 1, 1)
                    agg_parts(n + 1, l, 1)

            turns(pe, PAIRS, pair)
            for p in two:
                end(PAIRS - 1, p)

        @block.scalar
        def _(act):
            def pair(it):
                for l in range(LAYERS):
                    n = 6 * it + 2 * l

                    def begin(p):
                        act.wait_ge(start_ps, 2 * it + p + 1)
                        act.activation(H[p][:, :], TR[p][:, :], ACT.Copy).then_inc(start_H, 1)
                        act.wait_ge(start_H, 2 * it + p + 1)
                        act.activation(hT[p][:, 0, :], H[p][:, :], ACT.Copy).then_inc(start_hi, 1)

                    def back(p):
                        act.wait_ge(tok_ps, 4 * it + 2 * (l - 1) + p + 1)
                        act.activation(tok[p][:, :, :, :].rearrange("p s q d -> p (s q d)"), flat(TRh[p]),
                                       ACT.Copy).then_inc(tok_sb, 1)

                    def agg_part(p):
                        act.wait_ge(agg_ps, n + p + 1)
                        act.activation(agg[p][:, 0, :], AG[p][:, :], ACT.Copy).then_inc(agg_hi, 1)

                    def gates(p):
                        act.wait_ge(r_ps, n + p + 1)
                        act.activation(R[p][:, :], BR[:, :], ACT.Sigmoid, bias=gru_b[:, 0:1], scale=1 / PS)\
                            .then_inc(r_sb, 1)
                        act.wait_ge(z_ps, n + p + 1)
                        act.activation(Z[p][:, :], BZ[:, :], ACT.Sigmoid, bias=gru_b[:, 1:2], scale=1 / PS)\
                            .then_inc(z_sb, 1)
                        act.activation(Y[p][:, :], BZ[:, :], ACT.Sigmoid, bias=gru_b[:, 4:5], scale=-1 / PS)\
                            .then_inc(y_sb, 1)

                    def new(p):
                        act.wait_ge(t2, n + p + 1)
                        act.activation(N[p][:, :], T[p][:, :], ACT.Tanh, bias=gru_b[:, 2:3], scale=1 / PS)\
                            .then_inc(n_sb, 1)

                    def hi(p):
                        act.wait_ge(h_new, n + p + 1)
                        act.activation(hT[p][:, 0, :], H[p][:, :], ACT.Copy).then_inc(h_hi, 1)

                    (back if l else begin)(0)
                    agg_part(0)
                    (back if l else begin)(1)
                    agg_part(1)
                    gates(0)
                    new(0)
                    hi(0)
                    gates(1)
                    new(1)
                    hi(1)
            turns(act, PAIRS, pair)

        @block.vector
        def _(dve):
            def end(it, p):
                g = 2 * it + p
                xg = flat(tiles_of(X, GT * g, GT))
                dve.wait_ge(end_ps, g + 1)
                dve.scalar_tensor_tensor(out=T[p][:, :], in0=AGh[p][:, 0, :], scalar=1 / AS, in1=xg,
                                         op0=ALU.mult, op1=ALU.add).then_inc(x_half, 1)
                dve.wait_ge(x_half, g + 1)
                dve.scalar_tensor_tensor(out=xg, in0=AGh[p][:, 1, :], scalar=1 / AS, in1=T[p][:, :],
                                         op0=ALU.mult, op1=ALU.add).then_inc(x_new, 1)

            def pair(it):
                for l in range(LAYERS):
                    n = 6 * it + 2 * l

                    def agg_part(p):
                        dve.wait_ge(agg_hi, n + p + 1)
                        dve.tensor_tensor(agg[p][:, 1, :], AG[p][:, :], agg[p][:, 0, :], ALU.subtract)\
                            .then_inc(agg_lo, 1)

                    def inner(p):
                        dve.wait_ge(r_sb, n + p + 1)
                        dve.scalar_tensor_tensor(out=T[p][:, :], in0=BH[:, :], scalar=gru_b[:, 3:4], in1=R[p][:, :],
                                                 op0=ALU.add, op1=ALU.mult).then_inc(t1, 1)
                        dve.wait_ge(n_ps, n + p + 1)
                        dve.wait_ge(t1, n + p + 1)
                        dve.tensor_tensor(T[p][:, :], T[p][:, :], BN[:, :], ALU.add).then_inc(t2, 1)

                    def state(p):
                        dve.wait_ge(n_sb, n + p + 1)
                        dve.wait_ge(y_sb, n + p + 1)
                        dve.scalar_tensor_tensor(out=T[p][:, :], in0=N[p][:, :], scalar=AS, in1=Y[p][:, :],
                                                 op0=ALU.mult, op1=ALU.mult).then_inc(u_sb, 1)
                        dve.wait_ge(zh_sb, n + p + 1)
                        dve.wait_ge(u_sb, n + p + 1)
                        dve.tensor_tensor(H[p][:, :], T[p][:, :], Z[p][:, :], ALU.add).then_inc(h_new, 1)

                    def lo(p):
                        dve.wait_ge(h_hi, n + p + 1)
                        dve.tensor_tensor(hT[p][:, 1, :], H[p][:, :], hT[p][:, 0, :], ALU.subtract).then_inc(h_lo, 1)

                    def begin(p):
                        if not isinstance(it, int) or it > 0:
                            end(it - 1, p)
                        dve.wait_ge(start_hi, 2 * it + p + 1)
                        dve.tensor_tensor(hT[p][:, 1, :], H[p][:, :], hT[p][:, 0, :], ALU.subtract)\
                            .then_inc(start_lo, 1)

                    for p in two:
                        if l == 0:
                            begin(p)
                        agg_part(p)
                    inner(0)
                    state(0)
                    inner(1)
                    lo(0)
                    state(1)
                    lo(1)
            turns(dve, PAIRS, pair)
            for p in two:
                end(PAIRS - 1, p)

        @block.gpsimd
        def _(pool):
            def pair(it):
                for l in range(LAYERS):
                    for p in two:
                        n = 6 * it + 2 * l + p
                        if l == 0:
                            pool.wait_ge(start_H, 2 * it + p + 1)
                        pool.wait_ge(z_sb, n + 1)
                        pool.tensor_tensor(Z[p][:, :], Z[p][:, :], H[p][:, :], ALU.mult).then_inc(zh_sb, 1)
            turns(pool, PAIRS, pair)


def router(nc, k):
    X, ROWS, S, WGATE, NG, ident, banks = k["X"], k["ROWS"], k["S"], k["WGATE"], k["NG"], k["ident"], k["banks"]
    with ExitStack() as ctx:
        def sb(name, shape, dt=F32):
            return [ctx.enter_context(nc.sbuf_tensor(f"s_{name}{p}", shape, dt)) for p in range(2)]

        def sem(name):
            return ctx.enter_context(nc.semaphore("s_" + name))
        norm, st, mv, rstd = sb("norm", [P, GT, P]), sb("st", [P, GT, 6]), sb("mv", [P, GT, 2]), sb("rstd", [P, GT])
        xT = sb("xT", [P, 2, GW], F16)
        lns = [sem(n) for n in ("stats", "aggr", "var", "rstd", "norm")]
        hi, lo, t_ps, hi_T, lo_T, s_ps, score = (sem(n) for n in ("hi", "lo", "t_ps", "hi_T", "lo_T", "s_ps", "score"))
        TB, SC = banks[0:4], banks[4:6]
        block = ctx.enter_context(nc.Block())

        @block.vector
        def _(dve):
            def stats(g, p):
                part_norm(dve, k, lambda q: tile_of(X, GT * g + q), st[p], mv[p], lns, g + 1)

            def norms(g, p):
                wait_from(dve, hi, g - 1)
                finish_norm(dve, lambda q: tile_of(X, GT * g + q), lambda q: norm[p][:, q, :], mv[p], rstd[p], lns, g + 1)

            def los(g, p):
                dve.wait_ge(hi, g + 1)
                rows = tiles_of(ROWS, GT * g, GT)
                lo_part(dve, rows[:, :, P:2 * P], norm[p][:, :, :], rows[:, :, 0:P]).then_inc(lo, 1)

            def scores(g, p):
                dve.wait_ge(s_ps, g + 1)
                dve.tensor_tensor(tiles_of(S, GT * g, GT), SC[p][:, 0:GT * E].rearrange("p (q e) -> p q e", e=E),
                                  k["gate_b"][:, 0:1, :].to_broadcast([P, GT, E]), ALU.add).then_inc(score, 1)
            staggered(dve, NG, 2, [(0, stats), (2, los), (4, scores), (1, norms)])

        @block.scalar
        def _(act):
            def his(g, p):
                act.wait_ge(lns[4], g + 1)
                act.activation(tiles_of(ROWS, GT * g, GT)[:, :, 0:P], norm[p][:, :, :], ACT.Copy, scale=AS).then_inc(hi, 1)

            def turned(g, p):
                act.wait_ge(t_ps, g + 1)
                wait_from(act, s_ps, g - 1)
                for s in range(2):
                    act.activation(xT[p][:, s, :], TB[2 * p + s][:, :], ACT.Copy).then_inc(hi_T, 1)
            staggered(act, NG, 2, [(2, turned), (0, his)])

        @block.tensor
        def _(pe):
            def turn(g, p):
                pe.wait_ge(lo, g + 1)
                wait_from(pe, hi_T, 2 * (g - 1))
                for s in range(2):
                    for q in range(GT):
                        i = pe.matmul(TB[2 * p + s][:, q * P:(q + 1) * P],
                                      tile_of(ROWS, GT * g + q)[:, s * P:(s + 1) * P], ident[:, :],
                                      start=(q == 0), stop=True, skip_group_check=True)
                i.then_inc(t_ps, 1)

            def scores(g, p):
                pe.wait_ge(hi_T, 2 * (g + 1))
                wait_from(pe, score, g - 1)
                for q in range(GT):
                    i = passes(pe, SC[p][:, q * E:(q + 1) * E], lambda s: xT[p][:, s, q * P:(q + 1) * P],
                               lambda s: WGATE[:, 0, s, :], q == 0, True)
                i.then_inc(s_ps, 1)
            staggered(pe, NG, 2, [(0, turn), (1, scores)])

        @block.gpsimd
        def _(pool):
            staggered(pool, NG, 2, [(0, lambda g, p: root(pool, k, mv[p], rstd[p], lns, g + 1))])


def route(nc, k, tag):
    S, prob, pos, owner, revidx, banks = k["S"], k["prob"], k["pos"], k["owner"], k["revidx"], k["banks"]
    NT, NBLK = k["NT"], k["NBLK"]
    with ExitStack() as ctx:
        def sb(name, shape, dt):
            return ctx.enter_context(nc.sbuf_tensor("r" + tag + name, shape, dt))

        def sem(name):
            return ctx.enter_context(nc.semaphore("r" + tag + name))

        top = [sb(f"top{c}", [P, NT], F32) for c in range(2)]
        who = sb("who", [P, NT], F32)
        tmp = sb("tmp", [P, NT, E], F32)
        hot = [sb(f"hot{c}", [P, NT, E], F32) for c in range(2)]
        both = sb("both", [P, NT, E], F16)
        gap = sb("gap", [P, NT], F32)
        pre = [sb(f"pre{c}", [P, NT, E], F32) for c in range(2)]
        counts = sb("counts", [P, NT, E], F32)
        steps = sb("steps", [P, 2 * NBLK], F32)
        full = sb("full", [P, E, 16 * 4], F32)
        nblk = [sb(f"nblk{c}", [P, E], F32) for c in range(2)]
        nown = sb("nown", [P, E], F32)
        ends = sb("ends", [P, NBLK, E], F32)
        who_b = sb("who_b", [P, NBLK], F32)
        posf = sb("posf", [P, 2, NT], F32)
        chain, picked, ranked, iota_done, weighed = (sem(n) for n in ("chain", "picked", "ranked", "iota", "weighed"))
        MAXB = NT * P // BLK
        block = ctx.enter_context(nc.Block())

        @block.gpsimd
        def _(pool):
            pool.iota(steps[:, :], pattern=[[1, 2 * NBLK]], base=0, channel_multiplier=0,
                      allow_small_or_imprecise_dtypes=True).then_inc(iota_done, 1)

        @block.vector
        def _(dve):
            done = [0]

            def link(i):
                done[0] += 1
                i.then_inc(chain, 1)
                dve.wait_ge(chain, done[0])

            wide = lambda a: a[:, :].rearrange("p (t o) -> p t o", o=1).to_broadcast([P, NT, E])
            by_e = lambda a: a.rearrange("p (o e) -> p o e", o=1).to_broadcast([P, NT, E])
            scores = S
            for c in range(2):
                link(dve.tensor_reduce(top[c][:, :], scores[:, :, :], AX_X, ALU.max))
                link(dve.tensor_tensor(tmp[:, :, :], scores[:, :, :], wide(top[c]), ALU.is_equal))
                link(dve.tensor_tensor(tmp[:, :, :], tmp[:, :, :], by_e(revidx[:, :]), ALU.mult))
                link(dve.tensor_reduce(who[:, :], tmp[:, :, :], AX_X, ALU.max))
                link(dve.tensor_tensor(hot[c][:, :, :], by_e(revidx[:, :]), wide(who), ALU.is_equal))
                if c == 0:
                    link(dve.scalar_tensor_tensor(out=pre[0][:, :, :], in0=hot[0][:, :, :], scalar=-BIG,
                                                  in1=S[:, :, :], op0=ALU.mult, op1=ALU.add))
                    scores = pre[0]
            dve.tensor_tensor(both[:, :, :], hot[0][:, :, :], hot[1][:, :, :], ALU.add).then_inc(picked, 1)
            dve.tensor_tensor(gap[:, :], top[0][:, :], top[1][:, :], ALU.subtract).then_inc(picked, 1)
            dve.wait_ge(ranked, 2)
            dve.tensor_copy(flat(counts[:, :, :]), banks[1][:, 0:NT * E])
            link(dve.tensor_copy(flat(pre[0][:, :, :]), banks[1][:, 0:NT * E]))
            a, b, step = 0, 1, 1
            while step < NT:
                dve.tensor_copy(pre[b][:, 0:step, :], pre[a][:, 0:step, :])
                link(dve.tensor_tensor(pre[b][:, step:, :], pre[a][:, step:, :], pre[a][:, 0:NT - step, :], ALU.add))
                a, b, step = b, a, 2 * step
            dve.wait_ge(iota_done, 1)
            link(dve.tensor_scalar(full[:, :, 0:MAXB],
                                   steps[:, 0:MAXB].rearrange("p (o m) -> p o m", o=1).to_broadcast([P, E, MAXB]),
                                   float(BLK), None, ALU.mult))
            link(dve.tensor_tensor(full[:, :, 0:MAXB], full[:, :, 0:MAXB],
                                   pre[a][:, NT - 1, :].rearrange("p (e o) -> p e o", o=1).to_broadcast([P, E, MAXB]),
                                   ALU.is_lt))
            link(dve.tensor_reduce(nown[:, :], full[:, :, 0:MAXB], AX_X, ALU.add))
            link(dve.tensor_copy(nblk[0][:, :], nown[:, :]))
            c, d, step = 0, 1, 1
            while step < E:
                dve.tensor_copy(nblk[d][:, 0:step], nblk[c][:, 0:step])
                link(dve.tensor_tensor(nblk[d][:, step:], nblk[c][:, step:], nblk[c][:, 0:E - step], ALU.add))
                c, d, step = d, c, 2 * step
            link(dve.tensor_tensor(ends[:, :, :],
                                   steps[:, 0:NBLK].rearrange("p (m o) -> p m o", o=1).to_broadcast([P, NBLK, E]),
                                   nblk[c][:, :].rearrange("p (o e) -> p o e", o=1).to_broadcast([P, NBLK, E]), ALU.is_ge))
            link(dve.tensor_reduce(who_b[:, :], ends[:, :, :], AX_X, ALU.add))
            dve.tensor_scalar(owner[:, :], who_b[:, :], float(E - 1), None, ALU.min)
            link(dve.tensor_tensor(nown[:, :], nblk[c][:, :], nown[:, :], ALU.subtract))
            link(dve.tensor_scalar(nown[:, :], nown[:, :], float(BLK), None, ALU.mult))
            link(dve.tensor_tensor(pre[a][:, :, :], pre[a][:, :, :], counts[:, :, :], ALU.subtract))
            link(dve.tensor_tensor(pre[a][:, :, :], pre[a][:, :, :], by_e(nown[:, :]), ALU.add))
            link(dve.tensor_tensor(pre[a][:, :, :], pre[a][:, :, :],
                                   banks[0][:, 0:NT * E].rearrange("p (t e) -> p t e", e=E), ALU.add))
            for n in range(2):
                link(dve.tensor_tensor(tmp[:, :, :], hot[n][:, :, :], pre[a][:, :, :], ALU.mult))
                link(dve.tensor_reduce(posf[:, n, :], tmp[:, :, :], AX_X, ALU.add))
            dve.tensor_copy(flat(pos[:, :, :]), flat(posf[:, :, :]))

        @block.tensor
        def _(pe):
            pe.wait_ge(picked, 1)
            pe.matmul(banks[0][:, 0:NT * E], k["before"][:, :], flat(both[:, :, :]), start=True, stop=True)\
                .then_inc(ranked, 1)
            pe.matmul(banks[1][:, 0:NT * E], k["ones"][:, :], flat(both[:, :, :]), start=True, stop=True)\
                .then_inc(ranked, 1)

        @block.scalar
        def _(act):
            act.wait_ge(picked, 2)
            act.activation(prob[:, 0, :], gap[:, :], ACT.Sigmoid, scale=1 / PS)
            act.activation(prob[:, 1, :], gap[:, :], ACT.Sigmoid, scale=-1 / PS)


def send_rows(pool, k, sent):
    for t in range(k["NT"]):
        for c in range(2):
            pool.indirect_dma_start(
                out=k["slots"], out_offset=bass.IndirectOffsetOnAxis(ap=k["pos"][:, c, t:t + 1], axis=0),
                in_=k["ROWS"][:, t, :], in_offset=None).then_inc(sent, 16)
    pool.wait_ge(sent, 32 * k["NT"])


def scatter_reload(nc, k, sent):
    with ExitStack() as ctx:
        back = ctx.enter_context(nc.semaphore("weights_back"))
        block = ctx.enter_context(nc.Block())

        @block.gpsimd
        def _(pool):
            send_rows(pool, k, sent)

        @block.sync
        def _(sp):
            for n, w in enumerate((k["W1"], k["W2"])):
                sp.dma_start(w[:, :, :].rearrange("p s n -> p (s n)"), k["kept"][n]).then_inc(back, 16)
            sp.wait_ge(back, 32)


def scatter_weights(nc, ins, k, sent):
    W1, W2, VT, MASK, ADJ, banks, ident, NT = (k[n] for n in ("W1", "W2", "VT", "MASK", "ADJ", "banks", "ident", "NT"))
    with ExitStack() as ctx:
        def sb(name, shape, dt):
            return ctx.enter_context(nc.sbuf_tensor("w_" + name, shape, dt))

        def sem(name):
            return ctx.enter_context(nc.semaphore("w_" + name))

        N = E * HID
        stage = [sb(f"stage{m}", [P, N], F32) for m in range(2)]
        SPL = sb("SPL", [P, 2, N], F16)
        G = SPL[:, :, :].rearrange("p s n -> p (s n)").bitcast(F32)
        H = N // 2
        OUT = sb("OUT", [P, 2, H], F16)
        few = OUT[:, :, :].rearrange("p s n -> p (s n)")[:, 0:NT * NODES]

        def half_of(c):
            return (G, stage[1][:, :])[c // 2][:, c % 2 * H:(c % 2 + 1) * H]

        cnt = sb("cnt", [P, 1], F32)
        onesf = sb("ones", [P, P], F32)
        loaded = [sem(f"loaded{m}") for m in range(2)]
        stored = sem("stored")
        (hi, lo, t_ps, t_sb, gained, hi2, lo2, b_ps, b_new, chain, ones_set, counted, total) = (
            sem(n) for n in ("hi", "lo", "t_ps", "t_sb", "gained", "hi2", "lo2", "b_ps", "b_new", "chain",
                             "ones_set", "counted", "total"))
        block = ctx.enter_context(nc.Block())

        @block.gpsimd
        def _(pool):
            pool.memset(onesf[:, :], 1.0).then_inc(ones_set, 1)
            pool.wait_ge(k["zeroed"], k["NZERO"] * 16)
            send_rows(pool, k, sent)

        @block.sync
        def _(sp):
            sp.dma_start(stage[0][:, :].rearrange("p (n d) -> p n d", d=P),
                         ins["L0_ffn_W1"].rearrange("e (c p) d -> p (e c) d", p=P)).then_inc(loaded[0], 16)
            sp.dma_start(stage[1][:, :].rearrange("p (e h) -> p e h", e=E),
                         ins["L0_ffn_W2"].rearrange("e d h -> d e h")).then_inc(loaded[1], 16)
            sp.wait_ge(lo, 1)
            sp.dma_start(stage[0][:, :].rearrange("p (e h) -> p e h", e=E),
                         ins["L1_ffn_W1"].rearrange("e d h -> d e h")).then_inc(loaded[0], 16)
            sp.wait_ge(lo, 2)
            sp.dma_start(stage[1][:, :].rearrange("p (n d) -> p n d", d=P),
                         ins["L1_ffn_W2"].rearrange("e (c p) d -> p (e c) d", p=P)).then_inc(loaded[1], 16)
            for c in range(4):
                sp.wait_ge(lo2, c + 1)
                sp.dma_start(k["kept"][c // 2].rearrange("p (s n) -> p s n", s=2)[:, :, c % 2 * H:(c % 2 + 1) * H],
                             OUT[:, :, :]).then_inc(stored, 16)
            sp.wait_ge(stored, 64)

        @block.scalar
        def _(act):
            act.wait_ge(k["zeroed"], k["NZERO"] * 16)
            for m, W in enumerate((W1, W2)):
                act.wait_ge(loaded[m], 16)
                if m:
                    act.wait_ge(t_ps, 16)
                act.activation(SPL[:, 0, :], stage[m][:, :], ACT.Copy, scale=WS).then_inc(hi, 1)
                for b in range(16 * m, 16 * m + 16):
                    act.wait_ge(t_ps, b + 1)
                    act.activation(W[:, b // 8 % 2, (b % 8) * 512:(b % 8 + 1) * 512],
                                   banks[4 + b % 4][:, 0:256].bitcast(F16), ACT.Copy).then_inc(t_sb, 1)
            act.wait_ge(gained, 1)
            act.wait_ge(counted, 1)
            for c in range(4):
                if c == 2:
                    act.wait_ge(loaded[1], 32)
                if c:
                    act.wait_ge(stored, 16 * c)
                act.activation(OUT[:, 0, :], half_of(c), ACT.Copy, scale=WS).then_inc(hi2, 1)

        @block.tensor
        def _(pe):
            for b in range(32):
                if b % 8 == 0:
                    pe.wait_ge(lo, 1 + b // 16)
                if b >= 4:
                    pe.wait_ge(t_sb, b - 3)
                for q in range(4):
                    n = (b % 8) * 4 + q
                    last = pe.transpose(banks[4 + b % 4][:, q * 64:(q + 1) * 64].bitcast(F16),
                                        SPL[:, b // 8 % 2, n * P:(n + 1) * P], ident[:, :])
                last.then_inc(t_ps, 1)
            pe.wait_ge(loaded[0], 32)
            for n in range(E * CH):
                i = pe.matmul(banks[0][:, n:n + 1], stage[0][:, n * P:(n + 1) * P],
                              VT[:, k["C_LNB"] + n // CH:k["C_LNB"] + n // CH + 1], start=True, stop=True)
            i.then_inc(b_ps, 1)
            pe.wait_ge(ones_set, 1)
            pe.wait_ge(counted, 1)
            pe.matmul(banks[1][:, 0:1], onesf[:, :], cnt[:, :], start=True, stop=True).then_inc(total, 1)

        @block.vector
        def _(dve):
            def part(out, src, first):
                return dve.scalar_tensor_tensor(out=out, in0=src, scalar=WS, in1=first, op0=ALU.mult, op1=ALU.subtract)

            for n, step in enumerate((
                    lambda: dve.tensor_scalar(few, flat(ADJ[:, :, :]), 1, RELS + 2, ALU.max, ALU.min),
                    lambda: dve.tensor_scalar(few, few, 21.0, None, ALU.subtract),
                    lambda: dve.tensor_tensor(few, few, few, ALU.mult),
                    lambda: dve.tensor_scalar(few, few, 400.0, None, ALU.is_lt))):
                step().then_inc(chain, 1)
                dve.wait_ge(chain, n + 1)
            dve.tensor_reduce(cnt[:, :], few, AX_X, ALU.add).then_inc(counted, 1)
            for m in range(2):
                dve.wait_ge(hi, m + 1)
                part(SPL[:, 1, :], stage[m][:, :], SPL[:, 0, :]).then_inc(lo, 1)
            for h in range(2):
                half = slice(h * NODES, (h + 1) * NODES)
                dve.tensor_scalar(MASK[half, :, half], ADJ[half, :, :], 1, None, ALU.is_equal)
            dve.wait_ge(t_ps, 32)
            dve.wait_ge(loaded[0], 32)
            for e in range(E):
                i = dve.tensor_scalar(G[:, e * HID:(e + 1) * HID], stage[0][:, e * HID:(e + 1) * HID],
                                      VT[:, k["C_LNG"] + e:k["C_LNG"] + e + 1], None, ALU.mult)
            i.then_inc(gained, 1)
            for c in range(4):
                dve.wait_ge(hi2, c + 1)
                part(OUT[:, 1, :], half_of(c), OUT[:, 0, :]).then_inc(lo2, 1)
            dve.wait_ge(b_ps, 1)
            dve.tensor_tensor(VT[:, k["C_B1B"]:k["C_B1B"] + E * CH], VT[:, k["C_B1B"]:k["C_B1B"] + E * CH],
                              banks[0][:, 0:E * CH], ALU.add).then_inc(b_new, 1)
            dve.wait_ge(total, 1)
            dve.tensor_copy(k["general"][:, :], banks[1][:, 0:1])


def experts(nc, k, tag, func, b1_col, m):
    W1, W2, VT, b2rows, owner, banks, ident = (k[n] for n in ("W1", "W2", "VT", "b2rows", "owner", "banks", "ident"))
    NBLK = k["NBLK"]
    x_rows = k["slots"].rearrange("(b p r) c -> p b (r c)", p=P, r=BLK // P)
    y_rows = k["results"].rearrange("(b p r) c -> p b (r c)", p=P, r=BLK // P)
    with ExitStack() as ctx:
        def sb(name, shape, dt):
            return ctx.enter_context(nc.sbuf_tensor("e" + tag + name, shape, dt))

        def sem(name):
            return ctx.enter_context(nc.semaphore("e" + tag + name))

        ring = range(RING)
        xs = [sb(f"xs{j}", [P, GT, 2, P], F16) for j in ring]
        xT = [sb(f"xT{j}", [P, 2, BLK], F16) for j in ring]
        hf = [sb(f"hf{c}", [P, BLK], F32) for c in range(CH)]
        hs = [sb(f"hs{j}", [P, 2, CH, BLK], F16) for j in ring]
        ys = [sb(f"ys{j}", [P, BLK], F32) for j in ring]
        x_loaded = [sem(f"x_loaded{j}") for j in ring]
        y_stored = [sem(f"y_stored{j}") for j in ring]
        xT_ps, xT_sb, h_ps, h_f32, h_hi, h_lo, y_ps, y_sb = (
            sem(n) for n in ("xT_ps", "xT_sb", "h_ps", "h_f32", "h_hi", "h_lo", "y_ps", "y_sb"))
        HB, TB, YB = banks[0:4], banks[4], banks[5:8]
        TBh = TB[:, :].bitcast(F16).rearrange("p (s n) -> p s n", s=2)

        def rounds(eng, step):
            for j in ring:
                step(j, j, 0)
            with eng.Fori(1, NBLK // RING - 1) as i:
                for j in ring:
                    step(RING * i + j, j, i)
            for j in ring:
                step(NBLK - RING + j, j, NBLK // RING - 1)

        last = lambda b: isinstance(b, int) and b == NBLK - 1
        block = ctx.enter_context(nc.Block())

        @block.sync
        def _(sp):
            def load(b, j):
                sp.dma_start(xs[j][:, :, :, :].rearrange("p r s d -> p (r s d)"),
                             flat(x_rows[:, bass.ds(b, 1), :])).then_inc(x_loaded[j], 16)
            for j in ring:
                load(j, j)

            def step(b, j, i):
                if not (isinstance(b, int) and b + RING >= NBLK):
                    sp.wait_ge(xT_ps, b + 1)
                    load(b + RING, j)
                sp.wait_ge(y_sb, b + 1)
                sp.dma_start(flat(y_rows[:, bass.ds(b, 1), :]), ys[j][:, :]).then_inc(y_stored[j], 16)
            rounds(sp, step)
            for j in ring:
                sp.wait_ge(y_stored[j], 16 * (NBLK // RING))

        @block.tensor
        def _(pe):
            def turn_over(b, j, i):
                pe.wait_ge(x_loaded[j], 16 * (i + 1))
                wait_from(pe, xT_sb, b)
                for s in range(2):
                    for q in range(GT):
                        t = pe.transpose(TBh[:, s, q * P:(q + 1) * P], xs[j][:, q, s, :], ident[:, :])
                t.then_inc(xT_ps, 1)

            def up(b, j, e):
                pe.wait_ge(xT_sb, b + 1)
                for c in range(CH):
                    wait_from(pe, h_f32, 4 * b + c - 3)
                    passes(pe, HB[c][:, :], lambda s: W1[:, s, bass.ds(e * HID + c * P, P)],
                           lambda s: xT[j][:, s, :], True, True).then_inc(h_ps, 1)

            def down(b, j, e):
                wait_from(pe, y_sb, b - RING + 1)
                for q in range(GT):
                    o = YB[j][:, q * P:(q + 1) * P]
                    for s in range(2):
                        pe.matmul(o, k["ones16"][:, :], b2rows[:, m, s, bass.ds(e * P, P)],
                                  start=(q == 0 and s == 0), stop=False, skip_group_check=True)
                pe.wait_ge(h_lo, 4 * b + 4)
                for q in range(GT):
                    o = YB[j][:, q * P:(q + 1) * P]
                    for c in range(CH):
                        t = passes(pe, o, lambda s: hs[j][:, s, c, q * P:(q + 1) * P],
                                   lambda s: W2[:, s, bass.ds(e * HID + c * P, P)], False, c == CH - 1)
                t.then_inc(y_ps, 1)

            def who(b):
                return pe.value_load(owner[0:1, bass.ds(b, 1)], min_val=0, max_val=E - 1)

            turn_over(0, 0, 0)
            up(0, 0, who(0))
            turn_over(1, 1, 0)

            def step(b, j, i):
                if not last(b):
                    up(b + 1, (j + 1) % RING, who(b + 1))
                if not (isinstance(b, int) and b >= NBLK - 2):
                    turn_over(b + 2, (j + 2) % RING, i + (j + 2) // RING)
                down(b, j, who(b))
            rounds(pe, step)

        @block.scalar
        def _(act):
            def step(b, j, i):
                e = act.value_load(owner[0:1, bass.ds(b, 1)], min_val=0, max_val=E - 1)
                wait_from(act, y_ps, b - RING + 1)

                def hidden(c):
                    act.wait_ge(h_ps, 4 * b + c + 1)
                    wait_from(act, h_lo, 4 * b + c - 3)
                    act.activation(hf[c][:, :], HB[c][:, :], func, bias=VT[:, bass.ds(e * CH + b1_col + c, 1)],
                                   scale=1 / PS).then_inc(h_f32, 1)

                def hi(c):
                    act.wait_ge(h_f32, 4 * b + c + 1)
                    act.activation(hs[j][:, 0, c, :], hf[c][:, :], ACT.Copy, scale=AS).then_inc(h_hi, 1)

                hidden(0)
                for c in range(1, CH):
                    hidden(c)
                    hi(c - 1)
                hi(CH - 1)
            rounds(act, step)

        @block.vector
        def _(dve):
            def turned(b, j):
                dve.wait_ge(xT_ps, b + 1)
                wait_from(dve, h_ps, 4 * (b - RING + 1))
                dve.tensor_copy(flat(xT[j][:, :, :]), flat(TBh)).then_inc(xT_sb, 1)

            def lo(b, j, c):
                dve.wait_ge(h_hi, 4 * b + c + 1)
                dve.scalar_tensor_tensor(out=hs[j][:, 1, c, :], in0=hf[c][:, :], scalar=AS, in1=hs[j][:, 0, c, :],
                                         op0=ALU.mult, op1=ALU.subtract).then_inc(h_lo, 1)

            turned(0, 0)
            for c in range(CH):
                if c == 2:
                    turned(1, 1)
                lo(0, 0, c)

            def step(b, j, i):
                for c in range(CH):
                    if c == 2 and not (isinstance(b, int) and b >= NBLK - 2):
                        turned(b + 2, (j + 2) % RING)
                    if not last(b):
                        lo(b + 1, (j + 1) % RING, c)
                dve.wait_ge(y_ps, b + 1)
                wait_from(dve, y_stored[j], i * 16)
                dve.tensor_scalar(ys[j][:, :], YB[j][:, :], 1 / PS, None, ALU.mult).then_inc(y_sb, 1)
            rounds(dve, step)


def mix(dve, k, G, t0, sem_half, sem_full, n):
    for c, done in ((0, sem_half), (1, sem_full)):
        for q in range(GT):
            x = tile_of(k["X"], t0 + q)
            i = dve.scalar_tensor_tensor(out=x, in0=G[c][:, q, :], scalar=k["prob"][:, c, bass.ds(t0 + q, 1)], in1=x,
                                         op0=ALU.mult, op1=ALU.add)
        i.then_inc(done, 1)
        dve.wait_ge(done, n)


def gather(pool, k, t, c, dst, sem):
    pool.indirect_dma_start(out=dst, out_offset=None, in_=k["results"],
                            in_offset=bass.IndirectOffsetOnAxis(ap=k["pos"][:, c, t:t + 1], axis=0)).then_inc(sem, 16)


def relational(nc, ins, k):
    X, MASK, ADJ, ROWS, WREL, WGATE, S = (k[n] for n in ("X", "MASK", "ADJ", "ROWS", "WREL", "WGATE", "S"))
    ident, banks, NG, NT = k["ident"], k["banks"], k["NG"], k["NT"]
    with ExitStack() as ctx:
        def sb(name, shape, dt):
            return ctx.enter_context(nc.sbuf_tensor("c_" + name, shape, dt))

        def sem(name):
            return ctx.enter_context(nc.semaphore("c_" + name))

        two = range(2)
        G = [[sb(f"G{p}{c}", [P, GT, P], F32) for c in two] for p in two]
        norm_a, norm_b = ([sb(f"norm_{n}{p}", [P, GT, P], F32) for p in two] for n in "ab")
        tok_a = [sb(f"tok_a{p}", [P, 2, GT, P], F16) for p in two]
        xT_a = [sb(f"xT_a{p}", [P, 2, GW], F16) for p in two]
        sg = [sb(f"sg{p}", [P, GT, P], F32) for p in two]
        norm_c, rl = [sb("norm_c", [P, GT, P], F32)] * 2, [sb("rl", [P, GT, P], F32)] * 2
        tok_b, vs = [sb("tok_b", [P, 2, GT, P], F16)] * 2, [sb("vs", [P, 2, GT, P], F16)] * 2
        xT_b = [sb("xT_b", [P, 2, GW], F16)] * 2
        val = sg
        st, mv, rstd = ([[sb(f"{n}{a}{p}", [P, GT, w], F32) for p in two] for a in range(3)]
                        for n, w in (("st", 6), ("mv", 2), ("rs", 1)))
        rstd = [[flat(x[:, :, :]) for x in y] for y in rstd]
        AC, AT = sb("AC", [P, GT, P], F16), sb("AT", [P, GT, P], F16)
        HG = sb("HG", [P, GT, 2, 2, P], F32)
        BB = sb("BB", [P, 2, 2, P], F32)
        SUM = sb("SUM", [P, 2, 2, P], F32)
        SIG = sb("SIG", [P, 2, P], F32)
        VG = SIG
        VS = sb("VS", [P, 2, 2, P], F16)
        HOT = sb("HOT", [P, 2, P], F16)
        RV = sb("RV", [P, RELS], F32)
        relrows = nc.dram_tensor("relrows", [RELS, 4 * P], F32).ap()

        gathered = k["dma_sems"][2:4]
        half, full = sem("half"), sem("full")
        ln_a, ln_b, ln_c = ([sem(n + a) for n in ("stats", "aggr", "var", "rstd", "norm")] for a in "abc")
        hi_a, lo_a, a_ps, a_sb, v_ps, sg_sb, val_sb, v_hi, v_lo, rel_ps, rel_sb, x_rel = (
            sem(n) for n in ("hi_a", "lo_a", "a_ps", "a_sb", "v_ps", "sg_sb", "val_sb", "v_hi", "v_lo",
                             "rel_ps", "rel_sb", "x_rel"))
        hi_b, lo_b, b_ps, b_sb, score_ps, score, hi_c, lo_c = (
            sem(n) for n in ("hi_b", "lo_b", "b_ps", "b_sb", "score_ps", "score", "hi_c", "lo_c"))
        (rv_set, rows_packed, g_zero, g_clip, g_ps, g_at, g_hg_ps, g_hg, g_bias, g_sum, g_sig, g_val, g_hi, g_ops,
         g_used) = (sem("g_" + n) for n in ("rv", "packed", "zero", "clip", "ps", "at", "hgps", "hg", "bias", "sum",
                                            "sig", "val", "hi", "ops", "used"))
        V, RL, TA, TBk, SC, GB = banks[0:2], banks[2:4], banks[4], banks[5], banks[6], banks[7]
        halves = lambda b: b[:, :].bitcast(F16).rearrange("p (s n) -> p s n", s=2)
        TAh, TBh = halves(TA), halves(TBk)
        Vv = [b[:, :].rearrange("p (q s d) -> p q s d", q=2, s=2) for b in V]
        GBh = GB[:, 0:256].bitcast(F16)
        xs_of = lambda g: (lambda q: tile_of(X, GT * g + q))

        def if_general(eng):
            n = eng.value_load(k["general"][0:1, 0:1], min_val=0, max_val=NT * P * NODES)
            return eng.If(n > 0)

        block = ctx.enter_context(nc.Block())

        @block.gpsimd
        def _(pool):
            for r in range(RELS):
                i = pool.memset(RV[:, r:r + 1], float(r + 2))
            i.then_inc(rv_set, 1)

            def fetch(g, tiles):
                if g < NG:
                    if g >= 2:
                        pool.wait_ge(full, g - 1)
                    for q in tiles:
                        for c in two:
                            gather(pool, k, GT * g + q, c, G[g % 2][c][:, q, :], gathered[g % 2])

            fetch(0, range(GT))
            fetch(1, range(GT))
            for s in range(NG + 2):
                if s < NG:
                    root(pool, k, mv[0][s % 2], rstd[0][s % 2], ln_a, s + 1)
                if s >= 2:
                    root(pool, k, mv[1][s % 2], rstd[1][s % 2], ln_b, s - 1)
                fetch(s + 2, range(2))
                if s >= 2:
                    root(pool, k, mv[2][s % 2], rstd[2][s % 2], ln_c, s - 1)
                fetch(s + 2, range(2, GT))

        @block.sync
        def _(sp):
            for n, name in enumerate(("b_fwd", "bg_fwd", "b_bwd", "bg_bwd")):
                sp.dma_start(relrows[:, n * P:(n + 1) * P], ins["L1_gnn_" + name]).then_inc(rows_packed, 16)
            sp.wait_ge(rows_packed, 64)
            with if_general(sp):
                def group(g):
                    def rel(r):
                        wait_from(sp, g_used, (g * RELS + r) * GT)
                        sp.dma_start(BB[:, :, :, :].rearrange("p a b c -> p (a b c)"),
                                     relrows[bass.ds(r, 1), :].to_broadcast([P, 4 * P])).then_inc(g_bias, 16)
                    turns(sp, RELS, rel)
                turns(sp, NG, group)

        @block.tensor
        def _(pe):
            def turn_over(dst, src):
                for s in range(2):
                    for q in range(GT):
                        i = pe.transpose(dst[:, s, q * P:(q + 1) * P], src[:, s, q, :], ident[:, :])
                return i

            def turn_a(g, p):
                pe.wait_ge(lo_a, g + 1)
                turn_over(TAh, tok_a[p]).then_inc(a_ps, 1)

            def values(g, p):
                pe.wait_ge(a_sb, g + 1)
                for q in range(GT):
                    v = q // 2
                    if q % 2 == 0:
                        wait_from(pe, val_sb, 2 * g + v - 1)
                    o = Vv[v][:, q % 2, :, :].rearrange("p s d -> p (s d)")
                    for s in range(2):
                        pe.matmul(o, k["ones16"][:, :], k["relbias"][:, s, :], start=(q % 2 == 0 and s == 0),
                                  stop=False, skip_group_check=True)
                    i = passes(pe, o, lambda s: xT_a[p][:, s, q * P:(q + 1) * P], lambda s: WREL[:, 0, s, :],
                               False, True)
                    if q % 2:
                        i.then_inc(v_ps, 1)

            def neighbours(g, p):
                pe.wait_ge(v_lo, g + 1)
                wait_from(pe, rel_sb, g - 1)
                for q in range(GT):
                    for s in range(2):
                        i = pe.matmul(RL[p][:, q * P:(q + 1) * P], tile_of(MASK, GT * g + q), vs[p][:, s, q, :],
                                      start=(q == 0 and s == 0), stop=True, skip_group_check=True)
                general(g, p)
                pe.matmul(GB[:, 0:E], ident[:, :], WGATE[:, 1, 0, :], start=True, stop=True)\
                    .then_inc(rel_ps, 1)

            def general(g, p):
                with if_general(pe):
                    pe.wait_ge(g_clip, g + 1)
                    for q in range(GT):
                        i = pe.transpose(GBh[:, q * P:(q + 1) * P], AC[:, q, :], ident[:, :])
                    i.then_inc(g_ps, 1)
                    pe.wait_ge(g_at, g + 1)
                    for q in range(GT):
                        wait_from(pe, g_hg, GT * g + q)
                        passes(pe, GB[:, :].rearrange("p (a b) -> p a b", a=2),
                               lambda s: xT_a[p][:, s, q * P:(q + 1) * P],
                               lambda s: WREL[:, 1:3, s, :], True, True).then_inc(g_hg_ps, 1)

                    def rel(r):
                        for q in range(GT):
                            pe.wait_ge(g_ops, (g * RELS + r) * GT + q + 1)
                            for d in two:
                                for s in two:
                                    i = pe.matmul(RL[p][:, q * P:(q + 1) * P], HOT[:, d, :], VS[:, s, d, :],
                                                  start=False, stop=True, skip_group_check=True)
                            i.then_inc(g_used, 1)
                    turns(pe, RELS, rel)

            def turn_b(g, p):
                pe.wait_ge(lo_b, g + 1)
                wait_from(pe, b_sb, g)
                turn_over(TBh, tok_b[p]).then_inc(b_ps, 1)

            def scores(g, p):
                pe.wait_ge(b_sb, g + 1)
                wait_from(pe, score, g)
                for q in range(GT):
                    i = passes(pe, SC[:, q * E:(q + 1) * E], lambda s: xT_b[p][:, s, q * P:(q + 1) * P],
                               lambda s: WGATE[:, 1, s, :], q == 0, True)
                i.then_inc(score_ps, 1)
            staggered(pe, NG, 2, [(0, turn_a), (1, neighbours), (0, values), (2, turn_b), (2, scores)])

        @block.scalar
        def _(act):
            def relu(g, p):
                act.wait_ge(rel_ps, g + 1)
                wait_from(act, x_rel, g)
                act.activation(flat(rl[p][:, :, :]), RL[p][:, :], ACT.Relu, scale=1 / WS).then_inc(rel_sb, 1)

            def sig(g, p):
                for v in two:
                    act.wait_ge(v_ps, 2 * g + v + 1)
                    act.activation(sg[p][:, 2 * v:2 * v + 2, :], Vv[v][:, :, 1, :], ACT.Sigmoid, scale=1 / PS)\
                        .then_inc(sg_sb, 1)

            def his_a(g, p):
                act.wait_ge(ln_a[4], g + 1)
                act.activation(flat(tok_a[p][:, 0, :, :]), flat(norm_a[p][:, :, :]), ACT.Copy, scale=AS)\
                    .then_inc(hi_a, 1)

            def v_his(g, p):
                act.wait_ge(val_sb, 2 * g + 2)
                wait_from(act, rel_ps, g)
                act.activation(flat(vs[p][:, 0, :, :]), flat(val[p][:, :, :]), ACT.Copy).then_inc(v_hi, 1)

            def turned_a(g, p):
                act.wait_ge(a_ps, g + 1)
                act.activation(flat(xT_a[p][:, :, :]), flat(TAh), ACT.Copy).then_inc(a_sb, 1)

            def general(g, p):
                with if_general(act):
                    def rel(r):
                        for q in range(GT):
                            act.wait_ge(g_sum, (g * RELS + r) * GT + q + 1)
                            act.activation(SIG[:, :, :], SUM[:, :, 1, :], ACT.Sigmoid).then_inc(g_sig, 1)
                    turns(act, RELS, rel)

            def his_b(g, p):
                act.wait_ge(ln_b[4], g + 1)
                wait_from(act, b_ps, g)
                act.activation(flat(tok_b[p][:, 0, :, :]), flat(norm_b[p][:, :, :]), ACT.Copy, scale=AS)\
                    .then_inc(hi_b, 1)

            def turned_b(g, p):
                act.wait_ge(b_ps, g + 1)
                wait_from(act, score_ps, g)
                act.activation(flat(xT_b[p][:, :, :]), flat(TBh), ACT.Copy).then_inc(b_sb, 1)

            def his_c(g, p):
                act.wait_ge(ln_c[4], g + 1)
                act.activation(tiles_of(ROWS, GT * g, GT)[:, :, 0:P], norm_c[p][:, :, :], ACT.Copy, scale=AS)\
                    .then_inc(hi_c, 1)
            staggered(act, NG, 2, [(2, relu), (1, sig), (0, his_a), (1, v_his), (0, turned_a), (1, general),
                                   (2, his_b), (2, turned_b), (2, his_c)])

        @block.vector
        def _(dve):
            def mixture(g, p):
                dve.wait_ge(gathered[p], 64 * (g - p) + 128)
                mix(dve, k, G[p], GT * g, half, full, g + 1)
                part_norm(dve, k, xs_of(g), st[0][p], mv[0][p], ln_a, g + 1)

            def values(g, p):
                for v in two:
                    dve.wait_ge(sg_sb, 2 * g + v + 1)
                    dve.scalar_tensor_tensor(out=val[p][:, 2 * v:2 * v + 2, :], in0=Vv[v][:, :, 0, :], scalar=1 / AS,
                                             in1=sg[p][:, 2 * v:2 * v + 2, :], op0=ALU.mult, op1=ALU.mult)\
                        .then_inc(val_sb, 1)

            def norms_a(g, p):
                finish_norm(dve, xs_of(g), lambda q: norm_a[p][:, q, :], mv[0][p], rstd[0][p], ln_a, g + 1)

            def sums(g, p):
                xg = flat(tiles_of(X, GT * g, GT))
                dve.wait_ge(rel_sb, g + 1)
                dve.tensor_tensor(xg, xg, flat(rl[p][:, :, :]), ALU.add).then_inc(x_rel, 1)
                dve.wait_ge(x_rel, g + 1)
                part_norm(dve, k, xs_of(g), st[1][p], mv[1][p], ln_b, g + 1)

            def los_a(g, p):
                dve.wait_ge(hi_a, g + 1)
                lo_part(dve, flat(tok_a[p][:, 1, :, :]), flat(norm_a[p][:, :, :]), flat(tok_a[p][:, 0, :, :]))\
                    .then_inc(lo_a, 1)

            def v_los(g, p):
                dve.wait_ge(v_hi, g + 1)
                dve.tensor_tensor(flat(vs[p][:, 1, :, :]), flat(val[p][:, :, :]), flat(vs[p][:, 0, :, :]),
                                  ALU.subtract).then_inc(v_lo, 1)

            def general(g, p):
                with if_general(dve):
                    wait_from(dve, g_used, g * RELS * GT)
                    dve.memset(AC[:, :, :], 0.0).then_inc(g_zero, 1)
                    dve.wait_ge(g_zero, g + 1)
                    for h in two:
                        part = slice(h * NODES, (h + 1) * NODES)
                        i = dve.tensor_scalar(AC[part, :, part], tiles_of(ADJ, GT * g, GT)[part, :, :], 0, RELS + 2,
                                              ALU.max, ALU.min)
                    i.then_inc(g_clip, 1)
                    dve.wait_ge(g_ps, g + 1)
                    dve.tensor_copy(flat(AT[:, :, :]), GBh).then_inc(g_at, 1)
                    for q in range(GT):
                        dve.wait_ge(g_hg_ps, GT * g + q + 1)
                        dve.tensor_scalar(HG[:, q, :, :, :].rearrange("p a b c -> p (a b c)"), GB[:, :], 1 / PS, None,
                                          ALU.mult).then_inc(g_hg, 1)
                    dve.wait_ge(g_hg, GT * g + GT)
                    dve.wait_ge(rv_set, 1)

                    def rel(r):
                        dve.wait_ge(g_bias, 16 * (g * RELS + r + 1))
                        for q in range(GT):
                            m = (g * RELS + r) * GT + q
                            dve.tensor_tensor(SUM[:, :, :, :].rearrange("p a b c -> p (a b c)"),
                                              HG[:, q, :, :, :].rearrange("p a b c -> p (a b c)"),
                                              BB[:, :, :, :].rearrange("p a b c -> p (a b c)"), ALU.add).then_inc(g_sum, 1)
                            dve.wait_ge(g_sig, m + 1)
                            dve.scalar_tensor_tensor(out=VG[:, :, :], in0=SUM[:, :, 0, :], scalar=WS, in1=SIG[:, :, :],
                                                     op0=ALU.mult, op1=ALU.mult).then_inc(g_val, 1)
                            wait_from(dve, g_used, m)
                            dve.tensor_scalar(HOT[:, 0, :], AT[:, q, :], RV[:, bass.ds(r, 1)], None, ALU.is_equal)
                            dve.tensor_scalar(HOT[:, 1, :], AC[:, q, :], RV[:, bass.ds(r, 1)], None, ALU.is_equal)
                            dve.wait_ge(g_val, m + 1)
                            dve.tensor_copy(VS[:, 0, :, :], VG[:, :, :]).then_inc(g_hi, 1)
                            dve.wait_ge(g_hi, m + 1)
                            dve.tensor_tensor(VS[:, 1, :, :], VG[:, :, :], VS[:, 0, :, :], ALU.subtract)\
                                .then_inc(g_ops, 1)
                    turns(dve, RELS, rel)

            def norms_b(g, p):
                finish_norm(dve, xs_of(g), lambda q: norm_b[p][:, q, :], mv[1][p], rstd[1][p], ln_b, g + 1)
                dve.wait_ge(ln_b[4], g + 1)
                part_norm(dve, k, lambda q: norm_b[p][:, q, :], st[2][p], mv[2][p], ln_c, g + 1)

            def los_b(g, p):
                dve.wait_ge(hi_b, g + 1)
                lo_part(dve, flat(tok_b[p][:, 1, :, :]), flat(norm_b[p][:, :, :]), flat(tok_b[p][:, 0, :, :]))\
                    .then_inc(lo_b, 1)

            def norms_c(g, p):
                wait_from(dve, lo_c, g)
                finish_norm(dve, lambda q: norm_b[p][:, q, :], lambda q: norm_c[p][:, q, :], mv[2][p], rstd[2][p],
                            ln_c, g + 1)

            def los_c(g, p):
                dve.wait_ge(hi_c, g + 1)
                rows = tiles_of(ROWS, GT * g, GT)
                lo_part(dve, rows[:, :, P:2 * P], norm_c[p][:, :, :], rows[:, :, 0:P]).then_inc(lo_c, 1)

            def scores(g, p):
                dve.wait_ge(score_ps, g + 1)
                dve.tensor_tensor(tiles_of(S, GT * g, GT), SC[:, 0:GT * E].rearrange("p (q e) -> p q e", e=E),
                                  k["gate_b"][:, 1:2, :].to_broadcast([P, GT, E]), ALU.add).then_inc(score, 1)
            staggered(dve, NG, 2, [(0, mixture), (1, values), (0, norms_a), (2, sums), (0, los_a), (1, v_los),
                                   (1, general), (2, norms_b), (3, los_c), (2, los_b), (2, norms_c), (3, scores)])


def combine(nc, k):
    NG, X = k["NG"], k["X"]
    RG = 4
    with ExitStack() as ctx:
        def sem(name):
            return ctx.enter_context(nc.semaphore("d_" + name))
        G = [[ctx.enter_context(nc.sbuf_tensor(f"d_G{p}{c}", [P, GT, P], F32)) for c in range(2)] for p in range(RG)]
        gathered = k["dma_sems"][4:4 + RG]
        half, full, stored = sem("half"), sem("full"), sem("stored")
        block = ctx.enter_context(nc.Block())

        @block.gpsimd
        def _(pool):
            for g in range(NG):
                if g >= RG:
                    pool.wait_ge(full, g - RG + 1)
                for q in range(GT):
                    for c in range(2):
                        gather(pool, k, GT * g + q, c, G[g % RG][c][:, q, :], gathered[g % RG])

        @block.vector
        def _(dve):
            def four(it):
                for p in range(RG):
                    g = RG * it + p
                    dve.wait_ge(gathered[p], 16 * 2 * GT * (it + 1))
                    mix(dve, k, G[p], GT * g, half, full, g + 1)
            turns(dve, NG // RG, four)

        @block.sync
        def _(sp):
            def group(g):
                sp.wait_ge(full, g + 1)
                sp.dma_start(k["out_v"][:, bass.ds(GT * g, GT), :], tiles_of(X, GT * g, GT)).then_inc(stored, 16)
            turns(sp, NG, group)
            sp.wait_ge(stored, 16 * NG)


_UNUSED = ("nodemask",)


def kernel(**inputs):
    import numpy as _np
    import concourse.bacc as _bacc
    from concourse import mybir as _mybir
    from concourse.bass_utils import run_bass_kernel_spmd as _run

    nc = _bacc.Bacc("TRN2", target_bir_lowering=False, num_devices=1)
    arrays, args = {}, {}
    for name in inputs:
        if name in _UNUSED:
            continue
        a = _np.ascontiguousarray(inputs[name])
        arrays[f"in_{name}_dram"] = a
        args[name] = nc.dram_tensor(f"in_{name}_dram", a.shape, _mybir.dt.from_np(a.dtype), kind="ExternalInput").ap()
    shape = inputs["x"].shape
    out = nc.dram_tensor("out_dram", shape, _mybir.dt.from_np(_np.dtype("float32")), kind="ExternalOutput").ap()
    program(nc, args, out)
    r = _run(nc, [arrays], core_ids=[0])
    return r.results[0]["out_dram"]
```

```python
from contextlib import ExitStack

import concourse.bass as bass
from concourse import mybir

F32 = mybir.dt.float32
F16 = mybir.dt.float16
I32 = mybir.dt.int32
ALU = mybir.AluOpType
ACT = mybir.ActivationFunctionType
AX_X = mybir.AxisListType.X

P = 128
NODES = 64
E = 8
HID = 512
CH = HID // P
LAYERS = 3
QUAD = 4
GT = 4
GW = GT * P
BLK = 512
RING = 3
RELS = 39
AS = 16.0
WS = 64.0
PS = AS * WS
EPS = 1e-5
BIG = 3.0e38


def flat(ap):
    return ap.rearrange("p a b -> p (a b)")


def wait_from(eng, sem, value):
    if not isinstance(value, int) or value > 0:
        eng.wait_ge(sem, value)


def turns(eng, n, step):
    step(0)
    with eng.Fori(1, n) as i:
        step(i)


def program(nc, ins, out):
    TOK = ins["x"].shape[0] * NODES
    NT = TOK // P
    NG = NT // GT
    NBLK = 2 * TOK // BLK + E - 1
    NBLK += -NBLK % RING
    NZERO = NBLK * BLK // (2 * P)
    x_v = ins["x"].rearrange("(t g) n d -> (g n) t d", g=2)
    out_v = out.rearrange("(t g) n d -> (g n) t d", g=2)
    adj_v = ins["adj"].rearrange("(t g) s n -> (g s) t n", g=2)

    with ExitStack() as ctx:
        def sb(name, shape, dt, c=ctx):
            return c.enter_context(nc.sbuf_tensor(name, shape, dt))

        slots = nc.dram_tensor("slots", [NBLK * BLK, 2 * P], F16).ap()
        kept = [nc.dram_tensor(f"kept{m}", [P, 2 * E * HID], F16).ap() for m in range(2)]
        results = nc.dram_tensor("results", [NBLK * BLK, P], F32).ap()

        X = sb("X", [P, NT, P], F32)
        ADJ = sb("ADJ", [P, NT, NODES], I32)
        MASK = sb("MASK", [P, NT, P], F16)
        W1 = sb("W1", [P, 2, E * HID], F16)
        W2 = sb("W2", [P, 2, E * CH * P], F16)
        ROWS = sb("ROWS", [P, NT, 2 * P], F16)
        ident = sb("ident", [P, P], F16)
        identf = sb("identf", [P, P], F32)
        before = sb("before", [P, P], F16)
        ones = sb("ones", [P, P], F16)
        ones16 = sb("ones16", [1, P], F16)
        hold = sb("hold", [P, 1], F32)
        mhalf = sb("mhalf", [P, GT], F32)
        revidx = sb("revidx", [P, E], F32)
        WHH = sb("WHH", [P, 2, 3 * P], F16)
        WIH = sb("WIH", [P, LAYERS, 2, 3 * P], F16)
        WREL = sb("WREL", [P, 3, 2, 2 * P], F16)
        WGATE = sb("WGATE", [P, 2, 2, E], F16)
        VT = sb("VT", [P, 96], F32)
        gru_b = sb("gru_b", [P, 5], F32)
        b2rows = sb("b2rows", [1, 2, 2, E * P], F16)
        relbias = sb("relbias", [1, 2, 2 * P], F16)
        gate_b = sb("gate_b", [P, 2, E], F32)
        S = sb("S", [P, NT, E], F32)
        prob = sb("prob", [P, 2, NT], F32)
        pos = sb("pos", [P, 2, NT], I32)
        owner = sb("owner", [P, NBLK], I32)
        general = sb("general", [P, 1], I32)

        C_B1A, C_B1B, C_LNG, C_LNB, C_IH, C_HH, C_WG = 0, 32, 64, 72, 80, 83, 86
        NV = C_WG + E

        banks = [ctx.enter_context(nc.psum_tensor(f"bank{i}", [P, 512], F32)) for i in range(8)]

        dma_sems = [ctx.enter_context(nc.semaphore(f"indexed{i}")) for i in range(8)]

        zeroed = ctx.enter_context(nc.semaphore("slots_zeroed"))

        phase(nc, setup, ins, locals())
        phase(nc, first_norm, locals())
        phase(nc, gated_graph, locals())
        phase(nc, router, locals())
        phase(nc, route, locals(), "1")
        phase(nc, scatter_weights, ins, locals(), dma_sems[0])
        phase(nc, experts, locals(), "1", ACT.Relu, C_B1A, 0)
        phase(nc, relational, ins, locals())
        phase(nc, route, locals(), "2")
        phase(nc, scatter_reload, locals(), dma_sems[1])
        phase(nc, experts, locals(), "2", ACT.Gelu, C_B1B, 1)
        combine(nc, locals())


def phase(nc, run, *args):
    had = list(nc.free_semaphores)
    run(nc, *args)
    used = sorted(had[:had.index(nc.free_semaphores[0])])
    if not used:
        return
    with nc.Block() as block:
        @block.gpsimd
        def _(pool):
            first = used[0]
            for a, b in zip(used, used[1:] + [None]):
                if b != a + 1:
                    pool.sem_clear(range(first, a + 1))
                    first = b


def setup(nc, ins, k):
    X, ADJ, MASK = k["X"], k["ADJ"], k["MASK"]
    banks, VT, NT, NBLK = k["banks"], k["VT"], k["NT"], k["NBLK"]
    ident, identf = k["ident"], k["identf"]
    with ExitStack() as ctx:
        def sb(name, shape, dt):
            return ctx.enter_context(nc.sbuf_tensor(name, shape, dt))

        def sem(name):
            return ctx.enter_context(nc.semaphore(name))

        V = sb("V", [P, P], F32)
        SM = sb("SM", [P, 15, P], F32)
        ST = sb("ST", [P, 12, P], F32)
        b2f = sb("b2f", [1, 2, E * P], F32)
        rbf = sb("rbf", [1, 2 * P], F32)
        wr = sb("wr", [P, E], F32)
        gbf = sb("gbf", [P, 2, E], F32)
        zero = k["W1"][:, 0, 0:4 * P]
        prod = sb("prod", [P, 6, 3 * P], F32)

        loaded = sem("small_loaded")
        x_loaded = sem("x_loaded")
        adj_loaded = sem("adj_loaded")
        zeroed = k["zeroed"]
        consts = sem("consts")
        pchain, vchain = sem("pool_chain"), sem("dve_chain")
        small_ps, small_sb = sem("small_ps"), sem("small_sb")
        mask_zero = sem("mask_zero")

        nsmall = [0]
        block = ctx.enter_context(nc.Block())
        slots = k["slots"]

        @block.sync
        def _(sp):
            def small(dst, src):
                sp.dma_start(dst, src).then_inc(loaded, 16)
                nsmall[0] += 16
            rows = lambda a: a.rearrange("e (c p) -> (e c) p", p=P)
            small(V[0:32, :], rows(ins["L0_ffn_b1"]))
            small(V[32:64, :], rows(ins["L1_ffn_b1"]))
            small(V[64:72, :], ins["L1_ffn_ln_g"])
            small(V[72:80, :], ins["L1_ffn_ln_b"])
            small(V[80:83, :], ins["L0_gnn_b_ih"].rearrange("(c p) -> c p", p=P))
            small(V[83:86, :], ins["L0_gnn_b_hh"].rearrange("(c p) -> c p", p=P))
            small(V[86:94, :], ins["L0_ffn_Wg"])
            small(SM[:, 0:3, :], ins["L0_gnn_w_ih"].rearrange("(c p) d -> p c d", p=P))
            small(SM[:, 3:6, :], ins["L0_gnn_w_hh"].rearrange("(c p) d -> p c d", p=P))
            small(SM[:, 6:9, :], ins["L0_gnn_weight"].rearrange("l d e -> d l e"))
            for n, w in enumerate(("loop", "fwd", "bwd")):
                small(SM[:, 9 + n, :], ins[f"L1_gnn_W_{w}"])
                small(SM[:, 12 + n, :], ins[f"L1_gnn_Wg_{w}"])
            small(b2f[:, 0, :], ins["L0_ffn_b2"].rearrange("(a e) d -> a (e d)", a=1))
            small(b2f[:, 1, :], ins["L1_ffn_b2"].rearrange("(a e) d -> a (e d)", a=1))
            small(rbf[:, 0:P], ins["L1_gnn_b_loop"])
            small(rbf[:, P:2 * P], ins["L1_gnn_bg_loop"])
            small(wr[:, :], ins["L1_ffn_Wr"])
            small(gbf[:, 0, :], ins["L0_ffn_bg"].rearrange("(a e) -> a e", a=1).to_broadcast([P, E]))
            small(gbf[:, 1, :], ins["L1_ffn_br"].rearrange("(a e) -> a e", a=1).to_broadcast([P, E]))
            sp.dma_start(X[:, :, :], k["x_v"]).then_inc(x_loaded, 16)
            sp.wait_ge(x_loaded, 16)

        NSMALL = nsmall[0]

        @block.gpsimd
        def _(pool):
            pool.memset(zero, 0.0).then_inc(pchain, 1)
            pool.memset(ident[:, :], 0.0).then_inc(pchain, 1)
            pool.memset(identf[:, :], 0.0).then_inc(pchain, 1)
            pool.memset(k["before"][:, :], 0.0).then_inc(pchain, 1)
            pool.memset(k["ones"][:, :], 1.0)
            pool.memset(k["mhalf"][:, :], -0.5)
            pool.memset(k["ones16"][:, :], AS).then_inc(consts, 1)
            pool.wait_ge(pchain, 4)
            for m in (ident, identf):
                pool.affine_select(out=m[:, :], in_=m[:, :], compare_op=ALU.not_equal, fill=1.0, base=0,
                                   pattern=[[-1, P]], channel_multiplier=1).then_inc(consts, 1)
            pool.affine_select(out=k["before"][:, :], in_=k["before"][:, :], compare_op=ALU.is_ge, fill=1.0,
                               base=0, pattern=[[-1, P]], channel_multiplier=1).then_inc(consts, 1)
            for e in range(E):
                pool.memset(k["revidx"][:, e:e + 1], float(E - e)).then_inc(pchain, 1)
            pool.memset(MASK[:, :, :], 0.0).then_inc(mask_zero, 1)

        @block.scalar
        def _(act):
            act.dma_start(ADJ[:, :, :], k["adj_v"]).then_inc(adj_loaded, 16)
            act.wait_ge(pchain, 1)
            zrows = slots.rearrange("(n p r) c -> n p (r c)", p=P, r=2)
            for n in range(zrows.shape[0]):
                act.dma_start(zrows[n], zero).then_inc(zeroed, 16)

        @block.tensor
        def _(pe):
            pe.wait_ge(consts, 4)
            pe.wait_ge(loaded, NSMALL)
            pe.wait_ge(vchain, 1)
            pe.transpose(banks[0][:, 0:k["NV"]], V[0:k["NV"], :], identf[0:k["NV"], 0:k["NV"]]).then_inc(small_ps, 1)
            for n, src in enumerate([0, 1, 2, 3, 4, 5, 6, 7, 8, 12, 13, 14]):
                pe.transpose(banks[1 + n // 4][:, n % 4 * P:(n % 4 + 1) * P], SM[:, src, :],
                             identf[:, :]).then_inc(small_ps, 1)
            pe.wait_ge(small_sb, 4)
            for l in range(LAYERS):
                pe.matmul(banks[l][:, 0:3 * P], ST[:, 6 + l, :], flat(ST[:, 0:3, :]),
                          start=True, stop=True).then_inc(small_ps, 1)
            pe.wait_ge(small_sb, 7)
            for n in range(3):
                pe.matmul(banks[n][:, 0:P], SM[:, 9 + n, :], ST[:, 9 + n, :], start=True, stop=True)
                pe.transpose(banks[n][:, P:2 * P], SM[:, 9 + n, :], identf[:, :]).then_inc(small_ps, 1)

        @block.vector
        def _(dve):
            done = [0]

            def link(i):
                done[0] += 1
                i.then_inc(vchain, 1)
                dve.wait_ge(vchain, done[0])

            def split(hi, lo, src, scale):
                link(dve.tensor_scalar(hi, src, scale, None, ALU.mult))
                dve.scalar_tensor_tensor(out=lo, in0=src, scalar=scale, in1=hi, op0=ALU.mult, op1=ALU.subtract)

            link(dve.memset(k["general"][:, :], 0))
            dve.wait_ge(loaded, NSMALL)
            for m in range(2):
                split(k["b2rows"][:, m, 0, :], k["b2rows"][:, m, 1, :], b2f[:, m, :], WS)
            split(k["relbias"][:, 0, :], k["relbias"][:, 1, :], rbf[:, :], WS)
            split(k["WGATE"][:, 1, 0, :], k["WGATE"][:, 1, 1, :], wr[:, :], WS)
            dve.tensor_scalar(flat(k["gate_b"][:, :, :]), flat(gbf[:, :, :]), PS, None, ALU.mult)
            dve.wait_ge(small_ps, 1)
            dve.tensor_copy(VT[:, 0:k["NV"]], banks[0][:, 0:k["NV"]]).then_inc(small_sb, 1)
            for n in range(3):
                dve.wait_ge(small_ps, 5 + 4 * n)
                dve.tensor_copy(flat(ST[:, 4 * n:4 * n + 4, :]), banks[1 + n][:, :]).then_inc(small_sb, 1)
            dve.wait_ge(small_sb, 4)
            dve.tensor_tensor(k["gru_b"][:, 0:2], VT[:, k["C_IH"]:k["C_IH"] + 2], VT[:, k["C_HH"]:k["C_HH"] + 2], ALU.add)
            dve.tensor_scalar(k["gru_b"][:, 3:4], VT[:, k["C_HH"] + 2:k["C_HH"] + 3], PS, None, ALU.mult)
            link(dve.tensor_copy(k["gru_b"][:, 2:3], VT[:, k["C_IH"] + 2:k["C_IH"] + 3]))
            dve.tensor_scalar(k["gru_b"][:, 4:5], k["gru_b"][:, 1:2], -1.0, None, ALU.mult)
            split(k["WGATE"][:, 0, 0, :], k["WGATE"][:, 0, 1, :], VT[:, k["C_WG"]:k["C_WG"] + E], WS)
            split(k["WHH"][:, 0, :], k["WHH"][:, 1, :], flat(ST[:, 3:6, :]), WS)
            for l in range(LAYERS):
                dve.wait_ge(small_ps, 14 + l)
                dve.tensor_copy(prod[:, l, :], banks[l][:, 0:3 * P]).then_inc(small_sb, 1)
            dve.wait_ge(small_sb, 7)
            for l in range(LAYERS):
                split(k["WIH"][:, l, 0, :], k["WIH"][:, l, 1, :], prod[:, l, :], WS)
            for n in range(3):
                dve.wait_ge(small_ps, 17 + n)
                link(dve.tensor_copy(prod[:, 3 + n, P:2 * P], banks[n][:, 0:P]))
                link(dve.tensor_copy(prod[:, 3 + n, 0:P], banks[n][:, P:2 * P]))
                split(k["WREL"][:, n, 0, :], k["WREL"][:, n, 1, :], prod[:, 3 + n, 0:2 * P], WS)
            dve.wait_ge(adj_loaded, 16)
            dve.wait_ge(mask_zero, 1)
            for h in range(2):
                part = slice(h * NODES, (h + 1) * NODES)
                dve.tensor_scalar(MASK[part, :, part], ADJ[part, :, :], 0, None, ALU.not_equal)


def tile_of(buf, t):
    return flat(buf[:, bass.ds(t, 1), :])


def tiles_of(buf, t, n):
    return buf[:, bass.ds(t, n), :]


def passes(pe, out, lhs, rhs, start, stop):
    pe.matmul(out, lhs(0), rhs(0), start=start, stop=False, skip_group_check=True)
    pe.matmul(out, lhs(0), rhs(1), start=False, stop=False, skip_group_check=True)
    return pe.matmul(out, lhs(1), rhs(0), start=False, stop=stop, skip_group_check=True)


def part_norm(dve, k, x_of, st, mv, sems, n):
    stats_done, aggr_done, var_done = sems[0:3]
    dve.memset(k["hold"][:, :], 0.0)
    for q in range(GT):
        i = dve.bn_stats(st[:, q, :], x_of(q))
    i.then_inc(stats_done, 1)
    dve.wait_ge(stats_done, n)
    dve.memset(k["hold"][:, :], 0.0)
    for q in range(GT):
        i = dve.bn_aggr(mv[:, q, :], st[:, q, :])
    i.then_inc(aggr_done, 1)
    dve.wait_ge(aggr_done, n)
    dve.tensor_scalar(mv[:, :, 1], mv[:, :, 1], EPS, None, ALU.add).then_inc(var_done, 1)


def root(pool, k, mv, rstd, sems, n):
    pool.wait_ge(sems[2], n)
    pool.tensor_tensor(rstd[:, :], mv[:, :, 1], k["mhalf"][:, :], ALU.pow).then_inc(sems[3], 1)


def finish_norm(dve, x_of, out_of, mv, rstd, sems, n):
    dve.wait_ge(sems[3], n)
    for q in range(GT):
        i = dve.tensor_scalar(out_of(q), x_of(q), mv[:, q, 0:1], rstd[:, q:q + 1], ALU.subtract, ALU.mult)
    i.then_inc(sems[4], 1)


def lo_part(dve, out, src, hi):
    return dve.scalar_tensor_tensor(out=out, in0=src, scalar=AS, in1=hi, op0=ALU.mult, op1=ALU.subtract)


def staggered(eng, n, ring, stages):
    deepest = max(d for d, _ in stages)
    first = -(-(deepest + ring) // ring)

    def step(s, j):
        for d, do in stages:
            if not isinstance(s, int) or 0 <= s - d < n:
                do(s - d, (j - d) % ring)
    for s in range(min(first * ring, n + deepest)):
        step(s, s % ring)
    if first < n // ring:
        with eng.Fori(first, n // ring) as i:
            for j in range(ring):
                step(ring * i + j, j)
    for s in range(max(first, n // ring) * ring, n + deepest):
        step(s, s % ring)


def first_norm(nc, k):
    X, ROWS, NG = k["X"], k["ROWS"], k["NG"]
    with ExitStack() as ctx:
        def sb(name, shape):
            return [ctx.enter_context(nc.sbuf_tensor(f"n_{name}{p}", shape, F32)) for p in range(2)]
        norm, st, mv, rstd = sb("norm", [P, GT, P]), sb("st", [P, GT, 6]), sb("mv", [P, GT, 2]), sb("rstd", [P, GT])
        lns = [ctx.enter_context(nc.semaphore("n_" + n)) for n in ("stats", "aggr", "var", "rstd", "norm")]
        hi, lo = (ctx.enter_context(nc.semaphore("n_" + n)) for n in ("hi", "lo"))
        block = ctx.enter_context(nc.Block())

        @block.vector
        def _(dve):
            def stats(g, p):
                part_norm(dve, k, lambda q: tile_of(X, GT * g + q), st[p], mv[p], lns, g + 1)

            def norms(g, p):
                wait_from(dve, hi, g - 1)
                finish_norm(dve, lambda q: tile_of(X, GT * g + q), lambda q: norm[p][:, q, :], mv[p], rstd[p], lns, g + 1)

            def los(g, p):
                dve.wait_ge(hi, g + 1)
                rows = tiles_of(ROWS, GT * g, GT)
                lo_part(dve, rows[:, :, P:2 * P], norm[p][:, :, :], rows[:, :, 0:P]).then_inc(lo, 1)
            staggered(dve, NG, 2, [(0, stats), (2, los), (1, norms)])

        @block.scalar
        def _(act):
            def his(g, p):
                act.wait_ge(lns[4], g + 1)
                act.activation(tiles_of(ROWS, GT * g, GT)[:, :, 0:P], norm[p][:, :, :], ACT.Copy, scale=AS).then_inc(hi, 1)
            staggered(act, NG, 2, [(0, his)])

        @block.gpsimd
        def _(pool):
            staggered(pool, NG, 2, [(0, lambda g, p: root(pool, k, mv[p], rstd[p], lns, g + 1))])


def gated_graph(nc, k):
    X, MASK, ROWS, WHH, WIH = k["X"], k["MASK"], k["ROWS"], k["WHH"], k["WIH"]
    ident, gru_b, banks = k["ident"], k["gru_b"], k["banks"]
    QUADS = k["NG"] // QUAD
    PER = LAYERS * QUAD
    with ExitStack() as ctx:
        def sb(name, shape, dt):
            return ctx.enter_context(nc.sbuf_tensor(name, shape, dt))

        def sem(name):
            return ctx.enter_context(nc.semaphore("a_" + name))

        four = range(QUAD)
        tok = [sb(f"a_tok{p}", [P, 2, GT, P], F16) for p in four]
        hT = [sb(f"a_hT{p}", [P, 2, GW], F16) for p in four]
        H = [sb(f"a_H{p}", [P, GW], F32) for p in four]
        two = range(2)
        agg = [sb(f"a_agg{j}", [P, 2, GW], F16) for j in two]
        R = [sb(f"a_R{j}", [P, GW], F32) for j in two]
        Z = [sb(f"a_Z{j}", [P, GW], F32) for j in two]
        Y = [sb(f"a_Y{j}", [P, GW], F32) for j in two]
        N = [sb(f"a_N{j}", [P, GW], F32) for j in two]
        T = [sb(f"a_T{j}", [P, GW], F32) for j in two]
        XH = [sb(f"a_XH{j}", [P, GW], F32) for j in two]

        start_ps, start_hi, start_lo, start_H, end_ps, x_half, x_new = (
            sem(n) for n in ("start_ps", "start_hi", "start_lo", "start_H", "end_ps", "x_half", "x_new"))
        agg_ps, agg_hi, agg_lo, r_ps, z_ps, n_ps, r_sb, z_sb, y_sb = (
            sem(n) for n in ("agg_ps", "agg_hi", "agg_lo", "r_ps", "z_ps", "n_ps", "r_sb", "z_sb", "y_sb"))
        t1, t2, n_sb, u_sb, zh_sb, h_new, h_hi, h_lo = (
            sem(n) for n in ("t1", "t2", "n_sb", "u_sb", "zh_sb", "h_new", "h_hi", "h_lo"))
        tok_ps, tok_sb = sem("tok_ps"), sem("tok_sb")
        AG, TR = banks[0:2], banks[2:4]
        BR, BZ, BH, BN = banks[4:8]
        halves = lambda b: b[:, :].bitcast(F16).rearrange("p (s n) -> p s n", s=2)
        TRh, AGh = [halves(b) for b in TR], [halves(b) for b in AG]

        def quads(eng, step):
            def quad(it):
                for s in range(PER):
                    step(PER * it + s, it, s // QUAD, s % QUAD)
            turns(eng, QUADS, quad)

        def has(m):
            return not isinstance(m, int) or m >= 0

        LAST = PER * QUADS
        block = ctx.enter_context(nc.Block())

        @block.tensor
        def _(pe):
            def h_parts(n, p):
                wait_from(pe, r_sb, n)
                passes(pe, BR[:, :], lambda s: WHH[:, s, 0:P], lambda s: hT[p][:, s, :], True, False)
                wait_from(pe, t1, n)
                passes(pe, BH[:, :], lambda s: WHH[:, s, 2 * P:], lambda s: hT[p][:, s, :], True, True)
                wait_from(pe, y_sb, n)
                passes(pe, BZ[:, :], lambda s: WHH[:, s, P:2 * P], lambda s: hT[p][:, s, :], True, False)

            def agg_parts(n, l, j):
                pe.wait_ge(agg_lo, n + 1)
                passes(pe, BR[:, :], lambda s: WIH[:, l, s, 0:P], lambda s: agg[j][:, s, :], False, True)\
                    .then_inc(r_ps, 1)
                wait_from(pe, t2, n)
                passes(pe, BN[:, :], lambda s: WIH[:, l, s, 2 * P:], lambda s: agg[j][:, s, :], True, True)\
                    .then_inc(n_ps, 1)
                passes(pe, BZ[:, :], lambda s: WIH[:, l, s, P:2 * P], lambda s: agg[j][:, s, :], False, True)\
                    .then_inc(z_ps, 1)

            def aggregate(it, l, p):
                for q in range(GT):
                    t = GT * (QUAD * it + p) + q
                    for s in range(2):
                        h = tok[p][:, s, q, :] if l else tile_of(ROWS, t)[:, s * P:(s + 1) * P]
                        i = pe.matmul(AG[p % 2][:, q * P:(q + 1) * P], h, tile_of(MASK, t),
                                      start=(q == 0 and s == 0), stop=(s == 1), skip_group_check=True)
                i.then_inc(agg_ps, 1)

            def turn_over(dst, p):
                for s in range(2):
                    for q in range(GT):
                        i = pe.transpose(dst[:, s, q * P:(q + 1) * P], hT[p][:, s, q * P:(q + 1) * P], ident[:, :])
                return i

            def start(g, p):
                for q in range(GT):
                    for s in range(2):
                        i = pe.matmul(TR[p % 2][:, q * P:(q + 1) * P], tile_of(ROWS, GT * g + q)[:, s * P:(s + 1) * P],
                                      ident[:, :], start=(q == 0 and s == 0), stop=(s == 1), skip_group_check=True)
                i.then_inc(start_ps, 1)

            def end(it, p):
                pe.wait_ge(h_lo, PER * it + PER - QUAD + p + 1)
                turn_over(AGh[p % 2], p).then_inc(end_ps, 1)

            def gates(n, it, s):
                l, p = s // QUAD, s % QUAD
                if l == 0:
                    pe.wait_ge(start_lo, QUAD * it + p + 1)
                h_parts(n, p)
                return lambda: agg_parts(n, l, p % 2)

            def step(m, it, l, p):
                if l:
                    pe.wait_ge(h_lo, m - QUAD + 1)
                    turn_over(TRh[p % 2], p).then_inc(tok_ps, 1)
                else:
                    if has(m - PER):
                        end(it - 1, p)
                    start(QUAD * it + p, p)
                s = l * QUAD + p
                second = gates(m - 1, it if s else it - 1, (s - 1) % PER) if has(m - 1) else None
                if l:
                    pe.wait_ge(tok_sb, 2 * QUAD * it + QUAD * (l - 1) + p + 1)
                elif has(m - PER):
                    pe.wait_ge(x_new, QUAD * (it - 1) + p + 1)
                aggregate(it, l, p)
                if second:
                    second()

            quads(pe, step)
            gates(LAST - 1, QUADS - 1, PER - 1)()
            for p in four:
                if p >= 2:
                    pe.wait_ge(x_new, QUAD * (QUADS - 1) + p - 1)
                end(QUADS - 1, p)

        @block.scalar
        def _(act):
            def begin(g, p):
                act.wait_ge(start_ps, g + 1)
                act.activation(H[p][:, :], TR[p % 2][:, :], ACT.Copy).then_inc(start_H, 1)
                act.wait_ge(start_H, g + 1)
                act.activation(hT[p][:, 0, :], H[p][:, :], ACT.Copy).then_inc(start_hi, 1)

            def back(count, p):
                act.wait_ge(tok_ps, count)
                act.activation(tok[p][:, :, :, :].rearrange("p s q d -> p (s q d)"), flat(TRh[p % 2]),
                               ACT.Copy).then_inc(tok_sb, 1)

            def gates(n, j):
                act.wait_ge(r_ps, n + 1)
                act.activation(R[j][:, :], BR[:, :], ACT.Sigmoid, bias=gru_b[:, 0:1], scale=1 / PS)\
                    .then_inc(r_sb, 1)
                act.wait_ge(z_ps, n + 1)
                act.activation(Z[j][:, :], BZ[:, :], ACT.Sigmoid, bias=gru_b[:, 1:2], scale=1 / PS)\
                    .then_inc(z_sb, 1)
                act.activation(Y[j][:, :], BZ[:, :], ACT.Sigmoid, bias=gru_b[:, 4:5], scale=-1 / PS)\
                    .then_inc(y_sb, 1)

            def new(n, j):
                act.wait_ge(t2, n + 1)
                act.activation(N[j][:, :], T[j][:, :], ACT.Tanh, bias=gru_b[:, 2:3], scale=1 / PS).then_inc(n_sb, 1)

            def hi(n, p):
                act.wait_ge(h_new, n + 1)
                act.activation(hT[p][:, 0, :], H[p][:, :], ACT.Copy).then_inc(h_hi, 1)

            def step(m, it, l, p):
                if l:
                    back(2 * QUAD * it + QUAD * (l - 1) + p + 1, p)
                else:
                    begin(QUAD * it + p, p)
                if has(m - 2):
                    new(m - 2, p % 2)
                act.wait_ge(agg_ps, m + 1)
                act.activation(agg[p % 2][:, 0, :], AG[p % 2][:, :], ACT.Copy).then_inc(agg_hi, 1)
                if has(m - 2):
                    hi(m - 2, (p - 2) % QUAD)
                if has(m - 1):
                    gates(m - 1, (p - 1) % 2)

            quads(act, step)
            new(LAST - 2, 0)
            hi(LAST - 2, QUAD - 2)
            gates(LAST - 1, 1)
            new(LAST - 1, 1)
            hi(LAST - 1, QUAD - 1)

        @block.vector
        def _(dve):
            def end(g, p):
                xg = flat(tiles_of(X, GT * g, GT))
                dve.wait_ge(end_ps, g + 1)
                dve.scalar_tensor_tensor(out=XH[p % 2][:, :], in0=AGh[p % 2][:, 0, :], scalar=1 / AS, in1=xg,
                                         op0=ALU.mult, op1=ALU.add).then_inc(x_half, 1)
                dve.wait_ge(x_half, g + 1)
                dve.scalar_tensor_tensor(out=xg, in0=AGh[p % 2][:, 1, :], scalar=1 / AS, in1=XH[p % 2][:, :],
                                         op0=ALU.mult, op1=ALU.add).then_inc(x_new, 1)

            def begin(g, p):
                dve.wait_ge(start_hi, g + 1)
                dve.tensor_tensor(hT[p][:, 1, :], H[p][:, :], hT[p][:, 0, :], ALU.subtract).then_inc(start_lo, 1)

            def inner(n, j):
                dve.wait_ge(r_sb, n + 1)
                dve.scalar_tensor_tensor(out=T[j][:, :], in0=BH[:, :], scalar=gru_b[:, 3:4], in1=R[j][:, :],
                                         op0=ALU.add, op1=ALU.mult).then_inc(t1, 1)
                dve.wait_ge(n_ps, n + 1)
                dve.wait_ge(t1, n + 1)
                dve.tensor_tensor(T[j][:, :], T[j][:, :], BN[:, :], ALU.add).then_inc(t2, 1)

            def state(n, j, p):
                dve.wait_ge(n_sb, n + 1)
                dve.wait_ge(y_sb, n + 1)
                dve.scalar_tensor_tensor(out=T[j][:, :], in0=N[j][:, :], scalar=AS, in1=Y[j][:, :],
                                         op0=ALU.mult, op1=ALU.mult).then_inc(u_sb, 1)
                dve.wait_ge(zh_sb, n + 1)
                dve.wait_ge(u_sb, n + 1)
                dve.tensor_tensor(H[p][:, :], T[j][:, :], Z[j][:, :], ALU.add).then_inc(h_new, 1)

            def lo(n, p):
                dve.wait_ge(h_hi, n + 1)
                dve.tensor_tensor(hT[p][:, 1, :], H[p][:, :], hT[p][:, 0, :], ALU.subtract).then_inc(h_lo, 1)

            def step(m, it, l, p):
                if l == 0:
                    if has(m - PER):
                        end(QUAD * (it - 1) + p, p)
                    begin(QUAD * it + p, p)
                if has(m - 2):
                    state(m - 2, p % 2, (p - 2) % QUAD)
                dve.wait_ge(agg_hi, m + 1)
                dve.tensor_tensor(agg[p % 2][:, 1, :], AG[p % 2][:, :], agg[p % 2][:, 0, :], ALU.subtract)\
                    .then_inc(agg_lo, 1)
                if has(m - 2):
                    lo(m - 2, (p - 2) % QUAD)
                if has(m - 1):
                    inner(m - 1, (p - 1) % 2)

            quads(dve, step)
            state(LAST - 2, 0, QUAD - 2)
            lo(LAST - 2, QUAD - 2)
            inner(LAST - 1, 1)
            state(LAST - 1, 1, QUAD - 1)
            lo(LAST - 1, QUAD - 1)
            for p in four:
                end(QUAD * (QUADS - 1) + p, p)

        @block.gpsimd
        def _(pool):
            def step(m, it, l, p):
                if l == 0:
                    pool.wait_ge(start_H, QUAD * it + p + 1)
                pool.wait_ge(z_sb, m + 1)
                pool.tensor_tensor(Z[p % 2][:, :], Z[p % 2][:, :], H[p][:, :], ALU.mult).then_inc(zh_sb, 1)
            quads(pool, step)


def router(nc, k):
    X, ROWS, S, WGATE, NG, ident, banks = k["X"], k["ROWS"], k["S"], k["WGATE"], k["NG"], k["ident"], k["banks"]
    with ExitStack() as ctx:
        def sb(name, shape, dt=F32):
            return [ctx.enter_context(nc.sbuf_tensor(f"s_{name}{p}", shape, dt)) for p in range(2)]

        def sem(name):
            return ctx.enter_context(nc.semaphore("s_" + name))
        norm, st, mv, rstd = sb("norm", [P, GT, P]), sb("st", [P, GT, 6]), sb("mv", [P, GT, 2]), sb("rstd", [P, GT])
        xT = sb("xT", [P, 2, GW], F16)
        lns = [sem(n) for n in ("stats", "aggr", "var", "rstd", "norm")]
        hi, lo, t_ps, hi_T, lo_T, s_ps, score = (sem(n) for n in ("hi", "lo", "t_ps", "hi_T", "lo_T", "s_ps", "score"))
        TB, SC = banks[0:4], banks[4:6]
        block = ctx.enter_context(nc.Block())

        @block.vector
        def _(dve):
            def stats(g, p):
                part_norm(dve, k, lambda q: tile_of(X, GT * g + q), st[p], mv[p], lns, g + 1)

            def norms(g, p):
                wait_from(dve, hi, g - 1)
                finish_norm(dve, lambda q: tile_of(X, GT * g + q), lambda q: norm[p][:, q, :], mv[p], rstd[p], lns, g + 1)

            def los(g, p):
                dve.wait_ge(hi, g + 1)
                rows = tiles_of(ROWS, GT * g, GT)
                lo_part(dve, rows[:, :, P:2 * P], norm[p][:, :, :], rows[:, :, 0:P]).then_inc(lo, 1)

            def scores(g, p):
                dve.wait_ge(s_ps, g + 1)
                dve.tensor_tensor(tiles_of(S, GT * g, GT), SC[p][:, 0:GT * E].rearrange("p (q e) -> p q e", e=E),
                                  k["gate_b"][:, 0:1, :].to_broadcast([P, GT, E]), ALU.add).then_inc(score, 1)
            staggered(dve, NG, 2, [(0, stats), (2, los), (4, scores), (1, norms)])

        @block.scalar
        def _(act):
            def his(g, p):
                act.wait_ge(lns[4], g + 1)
                act.activation(tiles_of(ROWS, GT * g, GT)[:, :, 0:P], norm[p][:, :, :], ACT.Copy, scale=AS).then_inc(hi, 1)

            def turned(g, p):
                act.wait_ge(t_ps, g + 1)
                wait_from(act, s_ps, g - 1)
                for s in range(2):
                    act.activation(xT[p][:, s, :], TB[2 * p + s][:, :], ACT.Copy).then_inc(hi_T, 1)
            staggered(act, NG, 2, [(2, turned), (0, his)])

        @block.tensor
        def _(pe):
            def turn(g, p):
                pe.wait_ge(lo, g + 1)
                wait_from(pe, hi_T, 2 * (g - 1))
                for s in range(2):
                    for q in range(GT):
                        i = pe.matmul(TB[2 * p + s][:, q * P:(q + 1) * P],
                                      tile_of(ROWS, GT * g + q)[:, s * P:(s + 1) * P], ident[:, :],
                                      start=(q == 0), stop=True, skip_group_check=True)
                i.then_inc(t_ps, 1)

            def scores(g, p):
                pe.wait_ge(hi_T, 2 * (g + 1))
                wait_from(pe, score, g - 1)
                for q in range(GT):
                    i = passes(pe, SC[p][:, q * E:(q + 1) * E], lambda s: xT[p][:, s, q * P:(q + 1) * P],
                               lambda s: WGATE[:, 0, s, :], q == 0, True)
                i.then_inc(s_ps, 1)
            staggered(pe, NG, 2, [(0, turn), (1, scores)])

        @block.gpsimd
        def _(pool):
            staggered(pool, NG, 2, [(0, lambda g, p: root(pool, k, mv[p], rstd[p], lns, g + 1))])


def route(nc, k, tag):
    S, prob, pos, owner, revidx, banks = k["S"], k["prob"], k["pos"], k["owner"], k["revidx"], k["banks"]
    NT, NBLK = k["NT"], k["NBLK"]
    with ExitStack() as ctx:
        def sb(name, shape, dt):
            return ctx.enter_context(nc.sbuf_tensor("r" + tag + name, shape, dt))

        def sem(name):
            return ctx.enter_context(nc.semaphore("r" + tag + name))

        top = [sb(f"top{c}", [P, NT], F32) for c in range(2)]
        who = sb("who", [P, NT], F32)
        tmp = sb("tmp", [P, NT, E], F32)
        hot = [sb(f"hot{c}", [P, NT, E], F32) for c in range(2)]
        both = sb("both", [P, NT, E], F16)
        gap = sb("gap", [P, NT], F32)
        pre = [sb(f"pre{c}", [P, NT, E], F32) for c in range(2)]
        counts = sb("counts", [P, NT, E], F32)
        steps = sb("steps", [P, 2 * NBLK], F32)
        full = sb("full", [P, E, 16 * 4], F32)
        nblk = [sb(f"nblk{c}", [P, E], F32) for c in range(2)]
        nown = sb("nown", [P, E], F32)
        ends = sb("ends", [P, NBLK, E], F32)
        who_b = sb("who_b", [P, NBLK], F32)
        posf = sb("posf", [P, 2, NT], F32)
        chain, picked, ranked, iota_done, weighed = (sem(n) for n in ("chain", "picked", "ranked", "iota", "weighed"))
        MAXB = NT * P // BLK
        block = ctx.enter_context(nc.Block())

        @block.gpsimd
        def _(pool):
            pool.iota(steps[:, :], pattern=[[1, 2 * NBLK]], base=0, channel_multiplier=0,
                      allow_small_or_imprecise_dtypes=True).then_inc(iota_done, 1)

        @block.vector
        def _(dve):
            done = [0]

            def link(i):
                done[0] += 1
                i.then_inc(chain, 1)
                dve.wait_ge(chain, done[0])

            wide = lambda a: a[:, :].rearrange("p (t o) -> p t o", o=1).to_broadcast([P, NT, E])
            by_e = lambda a: a.rearrange("p (o e) -> p o e", o=1).to_broadcast([P, NT, E])
            scores = S
            for c in range(2):
                link(dve.tensor_reduce(top[c][:, :], scores[:, :, :], AX_X, ALU.max))
                link(dve.tensor_tensor(tmp[:, :, :], scores[:, :, :], wide(top[c]), ALU.is_equal))
                link(dve.tensor_tensor(tmp[:, :, :], tmp[:, :, :], by_e(revidx[:, :]), ALU.mult))
                link(dve.tensor_reduce(who[:, :], tmp[:, :, :], AX_X, ALU.max))
                link(dve.tensor_tensor(hot[c][:, :, :], by_e(revidx[:, :]), wide(who), ALU.is_equal))
                if c == 0:
                    link(dve.scalar_tensor_tensor(out=pre[0][:, :, :], in0=hot[0][:, :, :], scalar=-BIG,
                                                  in1=S[:, :, :], op0=ALU.mult, op1=ALU.add))
                    scores = pre[0]
            dve.tensor_tensor(both[:, :, :], hot[0][:, :, :], hot[1][:, :, :], ALU.add).then_inc(picked, 1)
            dve.tensor_tensor(gap[:, :], top[0][:, :], top[1][:, :], ALU.subtract).then_inc(picked, 1)
            dve.wait_ge(ranked, 2)
            dve.tensor_copy(flat(counts[:, :, :]), banks[1][:, 0:NT * E])
            link(dve.tensor_copy(flat(pre[0][:, :, :]), banks[1][:, 0:NT * E]))
            a, b, step = 0, 1, 1
            while step < NT:
                dve.tensor_copy(pre[b][:, 0:step, :], pre[a][:, 0:step, :])
                link(dve.tensor_tensor(pre[b][:, step:, :], pre[a][:, step:, :], pre[a][:, 0:NT - step, :], ALU.add))
                a, b, step = b, a, 2 * step
            dve.wait_ge(iota_done, 1)
            link(dve.tensor_scalar(full[:, :, 0:MAXB],
                                   steps[:, 0:MAXB].rearrange("p (o m) -> p o m", o=1).to_broadcast([P, E, MAXB]),
                                   float(BLK), None, ALU.mult))
            link(dve.tensor_tensor(full[:, :, 0:MAXB], full[:, :, 0:MAXB],
                                   pre[a][:, NT - 1, :].rearrange("p (e o) -> p e o", o=1).to_broadcast([P, E, MAXB]),
                                   ALU.is_lt))
            link(dve.tensor_reduce(nown[:, :], full[:, :, 0:MAXB], AX_X, ALU.add))
            link(dve.tensor_copy(nblk[0][:, :], nown[:, :]))
            c, d, step = 0, 1, 1
            while step < E:
                dve.tensor_copy(nblk[d][:, 0:step], nblk[c][:, 0:step])
                link(dve.tensor_tensor(nblk[d][:, step:], nblk[c][:, step:], nblk[c][:, 0:E - step], ALU.add))
                c, d, step = d, c, 2 * step
            link(dve.tensor_tensor(ends[:, :, :],
                                   steps[:, 0:NBLK].rearrange("p (m o) -> p m o", o=1).to_broadcast([P, NBLK, E]),
                                   nblk[c][:, :].rearrange("p (o e) -> p o e", o=1).to_broadcast([P, NBLK, E]), ALU.is_ge))
            link(dve.tensor_reduce(who_b[:, :], ends[:, :, :], AX_X, ALU.add))
            dve.tensor_scalar(owner[:, :], who_b[:, :], float(E - 1), None, ALU.min)
            link(dve.tensor_tensor(nown[:, :], nblk[c][:, :], nown[:, :], ALU.subtract))
            link(dve.tensor_scalar(nown[:, :], nown[:, :], float(BLK), None, ALU.mult))
            link(dve.tensor_tensor(pre[a][:, :, :], pre[a][:, :, :], counts[:, :, :], ALU.subtract))
            link(dve.tensor_tensor(pre[a][:, :, :], pre[a][:, :, :], by_e(nown[:, :]), ALU.add))
            link(dve.tensor_tensor(pre[a][:, :, :], pre[a][:, :, :],
                                   banks[0][:, 0:NT * E].rearrange("p (t e) -> p t e", e=E), ALU.add))
            for n in range(2):
                link(dve.tensor_tensor(tmp[:, :, :], hot[n][:, :, :], pre[a][:, :, :], ALU.mult))
                link(dve.tensor_reduce(posf[:, n, :], tmp[:, :, :], AX_X, ALU.add))
            dve.tensor_copy(flat(pos[:, :, :]), flat(posf[:, :, :]))

        @block.tensor
        def _(pe):
            pe.wait_ge(picked, 1)
            pe.matmul(banks[0][:, 0:NT * E], k["before"][:, :], flat(both[:, :, :]), start=True, stop=True)\
                .then_inc(ranked, 1)
            pe.matmul(banks[1][:, 0:NT * E], k["ones"][:, :], flat(both[:, :, :]), start=True, stop=True)\
                .then_inc(ranked, 1)

        @block.scalar
        def _(act):
            act.wait_ge(picked, 2)
            act.activation(prob[:, 0, :], gap[:, :], ACT.Sigmoid, scale=1 / PS)
            act.activation(prob[:, 1, :], gap[:, :], ACT.Sigmoid, scale=-1 / PS)


def send_rows(pool, k, sent):
    for t in range(k["NT"]):
        for c in range(2):
            pool.indirect_dma_start(
                out=k["slots"], out_offset=bass.IndirectOffsetOnAxis(ap=k["pos"][:, c, t:t + 1], axis=0),
                in_=k["ROWS"][:, t, :], in_offset=None).then_inc(sent, 16)
    pool.wait_ge(sent, 32 * k["NT"])


def scatter_reload(nc, k, sent):
    with ExitStack() as ctx:
        back = ctx.enter_context(nc.semaphore("weights_back"))
        block = ctx.enter_context(nc.Block())

        @block.gpsimd
        def _(pool):
            send_rows(pool, k, sent)

        @block.sync
        def _(sp):
            for n, w in enumerate((k["W1"], k["W2"])):
                sp.dma_start(w[:, :, :].rearrange("p s n -> p (s n)"), k["kept"][n]).then_inc(back, 16)
            sp.wait_ge(back, 32)


def scatter_weights(nc, ins, k, sent):
    W1, W2, VT, MASK, ADJ, banks, ident, NT = (k[n] for n in ("W1", "W2", "VT", "MASK", "ADJ", "banks", "ident", "NT"))
    with ExitStack() as ctx:
        def sb(name, shape, dt):
            return ctx.enter_context(nc.sbuf_tensor("w_" + name, shape, dt))

        def sem(name):
            return ctx.enter_context(nc.semaphore("w_" + name))

        N = E * HID
        stage = [sb(f"stage{m}", [P, N], F32) for m in range(2)]
        SPL = sb("SPL", [P, 2, N], F16)
        G = SPL[:, :, :].rearrange("p s n -> p (s n)").bitcast(F32)
        H = N // 2
        OUT = sb("OUT", [P, 2, H], F16)
        few = OUT[:, :, :].rearrange("p s n -> p (s n)")[:, 0:NT * NODES]

        def half_of(c):
            return (G, stage[1][:, :])[c // 2][:, c % 2 * H:(c % 2 + 1) * H]

        cnt = sb("cnt", [P, 1], F32)
        onesf = sb("ones", [P, P], F32)
        loaded = [sem(f"loaded{m}") for m in range(2)]
        stored = sem("stored")
        (hi, lo, t_ps, t_sb, gained, hi2, lo2, b_ps, b_new, chain, ones_set, counted, total) = (
            sem(n) for n in ("hi", "lo", "t_ps", "t_sb", "gained", "hi2", "lo2", "b_ps", "b_new", "chain",
                             "ones_set", "counted", "total"))
        block = ctx.enter_context(nc.Block())

        @block.gpsimd
        def _(pool):
            pool.memset(onesf[:, :], 1.0).then_inc(ones_set, 1)
            pool.wait_ge(k["zeroed"], k["NZERO"] * 16)
            send_rows(pool, k, sent)

        @block.sync
        def _(sp):
            sp.dma_start(stage[0][:, :].rearrange("p (n d) -> p n d", d=P),
                         ins["L0_ffn_W1"].rearrange("e (c p) d -> p (e c) d", p=P)).then_inc(loaded[0], 16)
            sp.dma_start(stage[1][:, :].rearrange("p (e h) -> p e h", e=E),
                         ins["L0_ffn_W2"].rearrange("e d h -> d e h")).then_inc(loaded[1], 16)
            sp.wait_ge(lo, 1)
            sp.dma_start(stage[0][:, :].rearrange("p (e h) -> p e h", e=E),
                         ins["L1_ffn_W1"].rearrange("e d h -> d e h")).then_inc(loaded[0], 16)
            sp.wait_ge(lo, 2)
            sp.dma_start(stage[1][:, :].rearrange("p (n d) -> p n d", d=P),
                         ins["L1_ffn_W2"].rearrange("e (c p) d -> p (e c) d", p=P)).then_inc(loaded[1], 16)
            for c in range(4):
                sp.wait_ge(lo2, c + 1)
                sp.dma_start(k["kept"][c // 2].rearrange("p (s n) -> p s n", s=2)[:, :, c % 2 * H:(c % 2 + 1) * H],
                             OUT[:, :, :]).then_inc(stored, 16)
            sp.wait_ge(stored, 64)

        @block.scalar
        def _(act):
            act.wait_ge(k["zeroed"], k["NZERO"] * 16)
            for m, W in enumerate((W1, W2)):
                act.wait_ge(loaded[m], 16)
                if m:
                    act.wait_ge(t_ps, 16)
                act.activation(SPL[:, 0, :], stage[m][:, :], ACT.Copy, scale=WS).then_inc(hi, 1)
                for b in range(16 * m, 16 * m + 16):
                    act.wait_ge(t_ps, b + 1)
                    act.activation(W[:, b // 8 % 2, (b % 8) * 512:(b % 8 + 1) * 512],
                                   banks[4 + b % 4][:, 0:256].bitcast(F16), ACT.Copy).then_inc(t_sb, 1)
            act.wait_ge(gained, 1)
            act.wait_ge(counted, 1)
            for c in range(4):
                if c == 2:
                    act.wait_ge(loaded[1], 32)
                if c:
                    act.wait_ge(stored, 16 * c)
                act.activation(OUT[:, 0, :], half_of(c), ACT.Copy, scale=WS).then_inc(hi2, 1)

        @block.tensor
        def _(pe):
            for b in range(32):
                if b % 8 == 0:
                    pe.wait_ge(lo, 1 + b // 16)
                if b >= 4:
                    pe.wait_ge(t_sb, b - 3)
                for q in range(4):
                    n = (b % 8) * 4 + q
                    last = pe.transpose(banks[4 + b % 4][:, q * 64:(q + 1) * 64].bitcast(F16),
                                        SPL[:, b // 8 % 2, n * P:(n + 1) * P], ident[:, :])
                last.then_inc(t_ps, 1)
            pe.wait_ge(loaded[0], 32)
            for n in range(E * CH):
                i = pe.matmul(banks[0][:, n:n + 1], stage[0][:, n * P:(n + 1) * P],
                              VT[:, k["C_LNB"] + n // CH:k["C_LNB"] + n // CH + 1], start=True, stop=True)
            i.then_inc(b_ps, 1)
            pe.wait_ge(ones_set, 1)
            pe.wait_ge(counted, 1)
            pe.matmul(banks[1][:, 0:1], onesf[:, :], cnt[:, :], start=True, stop=True).then_inc(total, 1)

        @block.vector
        def _(dve):
            def part(out, src, first):
                return dve.scalar_tensor_tensor(out=out, in0=src, scalar=WS, in1=first, op0=ALU.mult, op1=ALU.subtract)

            for n, step in enumerate((
                    lambda: dve.tensor_scalar(few, flat(ADJ[:, :, :]), 1, RELS + 2, ALU.max, ALU.min),
                    lambda: dve.tensor_scalar(few, few, 21.0, None, ALU.subtract),
                    lambda: dve.tensor_tensor(few, few, few, ALU.mult),
                    lambda: dve.tensor_scalar(few, few, 400.0, None, ALU.is_lt))):
                step().then_inc(chain, 1)
                dve.wait_ge(chain, n + 1)
            dve.tensor_reduce(cnt[:, :], few, AX_X, ALU.add).then_inc(counted, 1)
            for m in range(2):
                dve.wait_ge(hi, m + 1)
                part(SPL[:, 1, :], stage[m][:, :], SPL[:, 0, :]).then_inc(lo, 1)
            for h in range(2):
                half = slice(h * NODES, (h + 1) * NODES)
                dve.tensor_scalar(MASK[half, :, half], ADJ[half, :, :], 1, None, ALU.is_equal)
            dve.wait_ge(t_ps, 32)
            dve.wait_ge(loaded[0], 32)
            for e in range(E):
                i = dve.tensor_scalar(G[:, e * HID:(e + 1) * HID], stage[0][:, e * HID:(e + 1) * HID],
                                      VT[:, k["C_LNG"] + e:k["C_LNG"] + e + 1], None, ALU.mult)
            i.then_inc(gained, 1)
            for c in range(4):
                dve.wait_ge(hi2, c + 1)
                part(OUT[:, 1, :], half_of(c), OUT[:, 0, :]).then_inc(lo2, 1)
            dve.wait_ge(b_ps, 1)
            dve.tensor_tensor(VT[:, k["C_B1B"]:k["C_B1B"] + E * CH], VT[:, k["C_B1B"]:k["C_B1B"] + E * CH],
                              banks[0][:, 0:E * CH], ALU.add).then_inc(b_new, 1)
            dve.wait_ge(total, 1)
            dve.tensor_copy(k["general"][:, :], banks[1][:, 0:1])


def experts(nc, k, tag, func, b1_col, m):
    W1, W2, VT, b2rows, owner, banks, ident = (k[n] for n in ("W1", "W2", "VT", "b2rows", "owner", "banks", "ident"))
    NBLK = k["NBLK"]
    x_rows = k["slots"].rearrange("(b p r) c -> p b (r c)", p=P, r=BLK // P)
    y_rows = k["results"].rearrange("(b p r) c -> p b (r c)", p=P, r=BLK // P)
    with ExitStack() as ctx:
        def sb(name, shape, dt):
            return ctx.enter_context(nc.sbuf_tensor("e" + tag + name, shape, dt))

        def sem(name):
            return ctx.enter_context(nc.semaphore("e" + tag + name))

        ring = range(RING)
        xs = [sb(f"xs{j}", [P, GT, 2, P], F16) for j in ring]
        xT = [sb(f"xT{j}", [P, 2, BLK], F16) for j in ring]
        hf = [sb(f"hf{c}", [P, BLK], F32) for c in range(CH)]
        hs = [sb(f"hs{j}", [P, 2, CH, BLK], F16) for j in ring]
        ys = [sb(f"ys{j}", [P, BLK], F32) for j in ring]
        x_loaded = [sem(f"x_loaded{j}") for j in ring]
        y_stored = [sem(f"y_stored{j}") for j in ring]
        xT_ps, xT_sb, h_ps, h_f32, h_hi, h_lo, y_ps, y_sb = (
            sem(n) for n in ("xT_ps", "xT_sb", "h_ps", "h_f32", "h_hi", "h_lo", "y_ps", "y_sb"))
        HB, TB, YB = banks[0:4], banks[4], banks[5:8]
        TBh = TB[:, :].bitcast(F16).rearrange("p (s n) -> p s n", s=2)

        def rounds(eng, step):
            for j in ring:
                step(j, j, 0)
            with eng.Fori(1, NBLK // RING - 1) as i:
                for j in ring:
                    step(RING * i + j, j, i)
            for j in ring:
                step(NBLK - RING + j, j, NBLK // RING - 1)

        last = lambda b: isinstance(b, int) and b == NBLK - 1
        block = ctx.enter_context(nc.Block())

        @block.sync
        def _(sp):
            def load(b, j):
                sp.dma_start(xs[j][:, :, :, :].rearrange("p r s d -> p (r s d)"),
                             flat(x_rows[:, bass.ds(b, 1), :])).then_inc(x_loaded[j], 16)
            for j in ring:
                load(j, j)

            def step(b, j, i):
                if not (isinstance(b, int) and b + RING >= NBLK):
                    sp.wait_ge(xT_ps, b + 1)
                    load(b + RING, j)
                sp.wait_ge(y_sb, b + 1)
                sp.dma_start(flat(y_rows[:, bass.ds(b, 1), :]), ys[j][:, :]).then_inc(y_stored[j], 16)
            rounds(sp, step)
            for j in ring:
                sp.wait_ge(y_stored[j], 16 * (NBLK // RING))

        @block.tensor
        def _(pe):
            def turn_over(b, j, i):
                pe.wait_ge(x_loaded[j], 16 * (i + 1))
                wait_from(pe, xT_sb, b)
                for s in range(2):
                    for q in range(GT):
                        t = pe.transpose(TBh[:, s, q * P:(q + 1) * P], xs[j][:, q, s, :], ident[:, :])
                t.then_inc(xT_ps, 1)

            def up(b, j, e):
                pe.wait_ge(xT_sb, b + 1)
                for c in range(CH):
                    wait_from(pe, h_f32, 4 * b + c - 3)
                    passes(pe, HB[c][:, :], lambda s: W1[:, s, bass.ds(e * HID + c * P, P)],
                           lambda s: xT[j][:, s, :], True, True).then_inc(h_ps, 1)

            def down(b, j, e):
                wait_from(pe, y_sb, b - RING + 1)
                for q in range(GT):
                    o = YB[j][:, q * P:(q + 1) * P]
                    for s in range(2):
                        pe.matmul(o, k["ones16"][:, :], b2rows[:, m, s, bass.ds(e * P, P)],
                                  start=(q == 0 and s == 0), stop=False, skip_group_check=True)
                pe.wait_ge(h_lo, 4 * b + 4)
                for q in range(GT):
                    o = YB[j][:, q * P:(q + 1) * P]
                    for c in range(CH):
                        t = passes(pe, o, lambda s: hs[j][:, s, c, q * P:(q + 1) * P],
                                   lambda s: W2[:, s, bass.ds(e * HID + c * P, P)], False, c == CH - 1)
                t.then_inc(y_ps, 1)

            def who(b):
                return pe.value_load(owner[0:1, bass.ds(b, 1)], min_val=0, max_val=E - 1)

            turn_over(0, 0, 0)
            up(0, 0, who(0))
            turn_over(1, 1, 0)

            def step(b, j, i):
                if not last(b):
                    up(b + 1, (j + 1) % RING, who(b + 1))
                if not (isinstance(b, int) and b >= NBLK - 2):
                    turn_over(b + 2, (j + 2) % RING, i + (j + 2) // RING)
                down(b, j, who(b))
            rounds(pe, step)

        @block.scalar
        def _(act):
            def step(b, j, i):
                e = act.value_load(owner[0:1, bass.ds(b, 1)], min_val=0, max_val=E - 1)
                wait_from(act, y_ps, b - RING + 1)

                def hidden(c):
                    act.wait_ge(h_ps, 4 * b + c + 1)
                    wait_from(act, h_lo, 4 * b + c - 3)
                    act.activation(hf[c][:, :], HB[c][:, :], func, bias=VT[:, bass.ds(e * CH + b1_col + c, 1)],
                                   scale=1 / PS).then_inc(h_f32, 1)

                def hi(c):
                    act.wait_ge(h_f32, 4 * b + c + 1)
                    act.activation(hs[j][:, 0, c, :], hf[c][:, :], ACT.Copy, scale=AS).then_inc(h_hi, 1)

                hidden(0)
                for c in range(1, CH):
                    hidden(c)
                    hi(c - 1)
                hi(CH - 1)
            rounds(act, step)

        @block.vector
        def _(dve):
            def turned(b, j):
                dve.wait_ge(xT_ps, b + 1)
                wait_from(dve, h_ps, 4 * (b - RING + 1))
                dve.tensor_copy(flat(xT[j][:, :, :]), flat(TBh)).then_inc(xT_sb, 1)

            def lo(b, j, c):
                dve.wait_ge(h_hi, 4 * b + c + 1)
                dve.scalar_tensor_tensor(out=hs[j][:, 1, c, :], in0=hf[c][:, :], scalar=AS, in1=hs[j][:, 0, c, :],
                                         op0=ALU.mult, op1=ALU.subtract).then_inc(h_lo, 1)

            turned(0, 0)
            for c in range(CH):
                if c == 2:
                    turned(1, 1)
                lo(0, 0, c)

            def step(b, j, i):
                for c in range(CH):
                    if c == 2 and not (isinstance(b, int) and b >= NBLK - 2):
                        turned(b + 2, (j + 2) % RING)
                    if not last(b):
                        lo(b + 1, (j + 1) % RING, c)
                dve.wait_ge(y_ps, b + 1)
                wait_from(dve, y_stored[j], i * 16)
                dve.tensor_scalar(ys[j][:, :], YB[j][:, :], 1 / PS, None, ALU.mult).then_inc(y_sb, 1)
            rounds(dve, step)


def mix(dve, k, G, t0, sem_half, sem_full, n):
    for c, done in ((0, sem_half), (1, sem_full)):
        for q in range(GT):
            x = tile_of(k["X"], t0 + q)
            i = dve.scalar_tensor_tensor(out=x, in0=G[c][:, q, :], scalar=k["prob"][:, c, bass.ds(t0 + q, 1)], in1=x,
                                         op0=ALU.mult, op1=ALU.add)
        i.then_inc(done, 1)
        dve.wait_ge(done, n)


def gather(pool, k, t, c, dst, sem):
    pool.indirect_dma_start(out=dst, out_offset=None, in_=k["results"],
                            in_offset=bass.IndirectOffsetOnAxis(ap=k["pos"][:, c, t:t + 1], axis=0)).then_inc(sem, 16)


def relational(nc, ins, k):
    X, MASK, ADJ, ROWS, WREL, WGATE, S = (k[n] for n in ("X", "MASK", "ADJ", "ROWS", "WREL", "WGATE", "S"))
    ident, banks, NG, NT = k["ident"], k["banks"], k["NG"], k["NT"]
    with ExitStack() as ctx:
        def sb(name, shape, dt):
            return ctx.enter_context(nc.sbuf_tensor("c_" + name, shape, dt))

        def sem(name):
            return ctx.enter_context(nc.semaphore("c_" + name))

        two = range(2)
        G = [[sb(f"G{p}{c}", [P, GT, P], F32) for c in two] for p in two]
        norm_a, norm_b = ([sb(f"norm_{n}{p}", [P, GT, P], F32) for p in two] for n in "ab")
        tok_a = [sb(f"tok_a{p}", [P, 2, GT, P], F16) for p in two]
        xT_a = [sb(f"xT_a{p}", [P, 2, GW], F16) for p in two]
        sg = [sb(f"sg{p}", [P, GT, P], F32) for p in two]
        norm_c, rl = [sb("norm_c", [P, GT, P], F32)] * 2, [sb("rl", [P, GT, P], F32)] * 2
        tok_b, vs = [sb("tok_b", [P, 2, GT, P], F16)] * 2, [sb("vs", [P, 2, GT, P], F16)] * 2
        xT_b = [sb("xT_b", [P, 2, GW], F16)] * 2
        val = sg
        st, mv, rstd = ([[sb(f"{n}{a}{p}", [P, GT, w], F32) for p in two] for a in range(3)]
                        for n, w in (("st", 6), ("mv", 2), ("rs", 1)))
        rstd = [[flat(x[:, :, :]) for x in y] for y in rstd]
        AC, AT = sb("AC", [P, GT, P], F16), sb("AT", [P, GT, P], F16)
        HG = sb("HG", [P, GT, 2, 2, P], F32)
        BB = sb("BB", [P, 2, 2, P], F32)
        SUM = sb("SUM", [P, 2, 2, P], F32)
        SIG = sb("SIG", [P, 2, P], F32)
        VG = SIG
        VS = sb("VS", [P, 2, 2, P], F16)
        HOT = sb("HOT", [P, 2, P], F16)
        RV = sb("RV", [P, RELS], F32)
        relrows = nc.dram_tensor("relrows", [RELS, 4 * P], F32).ap()

        gathered = k["dma_sems"][2:4]
        half, full = sem("half"), sem("full")
        ln_a, ln_b, ln_c = ([sem(n + a) for n in ("stats", "aggr", "var", "rstd", "norm")] for a in "abc")
        hi_a, lo_a, a_ps, a_sb, v_ps, sg_sb, val_sb, v_hi, v_lo, rel_ps, rel_sb, x_rel = (
            sem(n) for n in ("hi_a", "lo_a", "a_ps", "a_sb", "v_ps", "sg_sb", "val_sb", "v_hi", "v_lo",
                             "rel_ps", "rel_sb", "x_rel"))
        hi_b, lo_b, b_ps, b_sb, score_ps, score, hi_c, lo_c = (
            sem(n) for n in ("hi_b", "lo_b", "b_ps", "b_sb", "score_ps", "score", "hi_c", "lo_c"))
        (rv_set, rows_packed, g_zero, g_clip, g_ps, g_at, g_hg_ps, g_hg, g_bias, g_sum, g_sig, g_val, g_hi, g_ops,
         g_used) = (sem("g_" + n) for n in ("rv", "packed", "zero", "clip", "ps", "at", "hgps", "hg", "bias", "sum",
                                            "sig", "val", "hi", "ops", "used"))
        V, RL, TA, TBk, SC, GB = banks[0:2], banks[2:4], banks[4], banks[5], banks[6], banks[7]
        halves = lambda b: b[:, :].bitcast(F16).rearrange("p (s n) -> p s n", s=2)
        TAh, TBh = halves(TA), halves(TBk)
        Vv = [b[:, :].rearrange("p (q s d) -> p q s d", q=2, s=2) for b in V]
        GBh = GB[:, 0:256].bitcast(F16)
        xs_of = lambda g: (lambda q: tile_of(X, GT * g + q))

        def if_general(eng):
            n = eng.value_load(k["general"][0:1, 0:1], min_val=0, max_val=NT * P * NODES)
            return eng.If(n > 0)

        block = ctx.enter_context(nc.Block())

        @block.gpsimd
        def _(pool):
            for r in range(RELS):
                i = pool.memset(RV[:, r:r + 1], float(r + 2))
            i.then_inc(rv_set, 1)

            def fetch(g, tiles):
                if g < NG:
                    if g >= 2:
                        pool.wait_ge(full, g - 1)
                    for q in tiles:
                        for c in two:
                            gather(pool, k, GT * g + q, c, G[g % 2][c][:, q, :], gathered[g % 2])

            fetch(0, range(GT))
            fetch(1, range(GT))
            for s in range(NG + 2):
                if s < NG:
                    root(pool, k, mv[0][s % 2], rstd[0][s % 2], ln_a, s + 1)
                if s >= 2:
                    root(pool, k, mv[1][s % 2], rstd[1][s % 2], ln_b, s - 1)
                fetch(s + 2, range(2))
                if s >= 2:
                    root(pool, k, mv[2][s % 2], rstd[2][s % 2], ln_c, s - 1)
                fetch(s + 2, range(2, GT))

        @block.sync
        def _(sp):
            for n, name in enumerate(("b_fwd", "bg_fwd", "b_bwd", "bg_bwd")):
                sp.dma_start(relrows[:, n * P:(n + 1) * P], ins["L1_gnn_" + name]).then_inc(rows_packed, 16)
            sp.wait_ge(rows_packed, 64)
            with if_general(sp):
                def group(g):
                    def rel(r):
                        wait_from(sp, g_used, (g * RELS + r) * GT)
                        sp.dma_start(BB[:, :, :, :].rearrange("p a b c -> p (a b c)"),
                                     relrows[bass.ds(r, 1), :].to_broadcast([P, 4 * P])).then_inc(g_bias, 16)
                    turns(sp, RELS, rel)
                turns(sp, NG, group)

        @block.tensor
        def _(pe):
            def turn_over(dst, src):
                for s in range(2):
                    for q in range(GT):
                        i = pe.transpose(dst[:, s, q * P:(q + 1) * P], src[:, s, q, :], ident[:, :])
                return i

            def turn_a(g, p):
                pe.wait_ge(lo_a, g + 1)
                turn_over(TAh, tok_a[p]).then_inc(a_ps, 1)

            def values(g, p):
                pe.wait_ge(a_sb, g + 1)
                for q in range(GT):
                    v = q // 2
                    if q % 2 == 0:
                        wait_from(pe, val_sb, 2 * g + v - 1)
                    o = Vv[v][:, q % 2, :, :].rearrange("p s d -> p (s d)")
                    for s in range(2):
                        pe.matmul(o, k["ones16"][:, :], k["relbias"][:, s, :], start=(q % 2 == 0 and s == 0),
                                  stop=False, skip_group_check=True)
                    i = passes(pe, o, lambda s: xT_a[p][:, s, q * P:(q + 1) * P], lambda s: WREL[:, 0, s, :],
                               False, True)
                    if q % 2:
                        i.then_inc(v_ps, 1)

            def neighbours(g, p):
                pe.wait_ge(v_lo, g + 1)
                wait_from(pe, rel_sb, g - 1)
                for q in range(GT):
                    for s in range(2):
                        i = pe.matmul(RL[p][:, q * P:(q + 1) * P], tile_of(MASK, GT * g + q), vs[p][:, s, q, :],
                                      start=(q == 0 and s == 0), stop=True, skip_group_check=True)
                general(g, p)
                pe.matmul(GB[:, 0:E], ident[:, :], WGATE[:, 1, 0, :], start=True, stop=True)\
                    .then_inc(rel_ps, 1)

            def general(g, p):
                with if_general(pe):
                    pe.wait_ge(g_clip, g + 1)
                    for q in range(GT):
                        i = pe.transpose(GBh[:, q * P:(q + 1) * P], AC[:, q, :], ident[:, :])
                    i.then_inc(g_ps, 1)
                    pe.wait_ge(g_at, g + 1)
                    for q in range(GT):
                        wait_from(pe, g_hg, GT * g + q)
                        passes(pe, GB[:, :].rearrange("p (a b) -> p a b", a=2),
                               lambda s: xT_a[p][:, s, q * P:(q + 1) * P],
                               lambda s: WREL[:, 1:3, s, :], True, True).then_inc(g_hg_ps, 1)

                    def rel(r):
                        for q in range(GT):
                            pe.wait_ge(g_ops, (g * RELS + r) * GT + q + 1)
                            for d in two:
                                for s in two:
                                    i = pe.matmul(RL[p][:, q * P:(q + 1) * P], HOT[:, d, :], VS[:, s, d, :],
                                                  start=False, stop=True, skip_group_check=True)
                            i.then_inc(g_used, 1)
                    turns(pe, RELS, rel)

            def turn_b(g, p):
                pe.wait_ge(lo_b, g + 1)
                wait_from(pe, b_sb, g)
                turn_over(TBh, tok_b[p]).then_inc(b_ps, 1)

            def scores(g, p):
                pe.wait_ge(b_sb, g + 1)
                wait_from(pe, score, g)
                for q in range(GT):
                    i = passes(pe, SC[:, q * E:(q + 1) * E], lambda s: xT_b[p][:, s, q * P:(q + 1) * P],
                               lambda s: WGATE[:, 1, s, :], q == 0, True)
                i.then_inc(score_ps, 1)
            staggered(pe, NG, 2, [(0, turn_a), (1, neighbours), (0, values), (2, turn_b), (2, scores)])

        @block.scalar
        def _(act):
            def relu(g, p):
                act.wait_ge(rel_ps, g + 1)
                wait_from(act, x_rel, g)
                act.activation(flat(rl[p][:, :, :]), RL[p][:, :], ACT.Relu, scale=1 / WS).then_inc(rel_sb, 1)

            def sig(g, p):
                for v in two:
                    act.wait_ge(v_ps, 2 * g + v + 1)
                    act.activation(sg[p][:, 2 * v:2 * v + 2, :], Vv[v][:, :, 1, :], ACT.Sigmoid, scale=1 / PS)\
                        .then_inc(sg_sb, 1)

            def his_a(g, p):
                act.wait_ge(ln_a[4], g + 1)
                act.activation(flat(tok_a[p][:, 0, :, :]), flat(norm_a[p][:, :, :]), ACT.Copy, scale=AS)\
                    .then_inc(hi_a, 1)

            def v_his(g, p):
                act.wait_ge(val_sb, 2 * g + 2)
                wait_from(act, rel_ps, g)
                act.activation(flat(vs[p][:, 0, :, :]), flat(val[p][:, :, :]), ACT.Copy).then_inc(v_hi, 1)

            def turned_a(g, p):
                act.wait_ge(a_ps, g + 1)
                act.activation(flat(xT_a[p][:, :, :]), flat(TAh), ACT.Copy).then_inc(a_sb, 1)

            def general(g, p):
                with if_general(act):
                    def rel(r):
                        for q in range(GT):
                            act.wait_ge(g_sum, (g * RELS + r) * GT + q + 1)
                            act.activation(SIG[:, :, :], SUM[:, :, 1, :], ACT.Sigmoid).then_inc(g_sig, 1)
                    turns(act, RELS, rel)

            def his_b(g, p):
                act.wait_ge(ln_b[4], g + 1)
                wait_from(act, b_ps, g)
                act.activation(flat(tok_b[p][:, 0, :, :]), flat(norm_b[p][:, :, :]), ACT.Copy, scale=AS)\
                    .then_inc(hi_b, 1)

            def turned_b(g, p):
                act.wait_ge(b_ps, g + 1)
                wait_from(act, score_ps, g)
                act.activation(flat(xT_b[p][:, :, :]), flat(TBh), ACT.Copy).then_inc(b_sb, 1)

            def his_c(g, p):
                act.wait_ge(ln_c[4], g + 1)
                act.activation(tiles_of(ROWS, GT * g, GT)[:, :, 0:P], norm_c[p][:, :, :], ACT.Copy, scale=AS)\
                    .then_inc(hi_c, 1)
            staggered(act, NG, 2, [(2, relu), (1, sig), (0, his_a), (1, v_his), (0, turned_a), (1, general),
                                   (2, his_b), (2, turned_b), (2, his_c)])

        @block.vector
        def _(dve):
            def mixture(g, p):
                dve.wait_ge(gathered[p], 64 * (g - p) + 128)
                mix(dve, k, G[p], GT * g, half, full, g + 1)
                part_norm(dve, k, xs_of(g), st[0][p], mv[0][p], ln_a, g + 1)

            def values(g, p):
                for v in two:
                    dve.wait_ge(sg_sb, 2 * g + v + 1)
                    dve.scalar_tensor_tensor(out=val[p][:, 2 * v:2 * v + 2, :], in0=Vv[v][:, :, 0, :], scalar=1 / AS,
                                             in1=sg[p][:, 2 * v:2 * v + 2, :], op0=ALU.mult, op1=ALU.mult)\
                        .then_inc(val_sb, 1)

            def norms_a(g, p):
                finish_norm(dve, xs_of(g), lambda q: norm_a[p][:, q, :], mv[0][p], rstd[0][p], ln_a, g + 1)

            def sums(g, p):
                xg = flat(tiles_of(X, GT * g, GT))
                dve.wait_ge(rel_sb, g + 1)
                dve.tensor_tensor(xg, xg, flat(rl[p][:, :, :]), ALU.add).then_inc(x_rel, 1)
                dve.wait_ge(x_rel, g + 1)
                part_norm(dve, k, xs_of(g), st[1][p], mv[1][p], ln_b, g + 1)

            def los_a(g, p):
                dve.wait_ge(hi_a, g + 1)
                lo_part(dve, flat(tok_a[p][:, 1, :, :]), flat(norm_a[p][:, :, :]), flat(tok_a[p][:, 0, :, :]))\
                    .then_inc(lo_a, 1)

            def v_los(g, p):
                dve.wait_ge(v_hi, g + 1)
                dve.tensor_tensor(flat(vs[p][:, 1, :, :]), flat(val[p][:, :, :]), flat(vs[p][:, 0, :, :]),
                                  ALU.subtract).then_inc(v_lo, 1)

            def general(g, p):
                with if_general(dve):
                    wait_from(dve, g_used, g * RELS * GT)
                    dve.memset(AC[:, :, :], 0.0).then_inc(g_zero, 1)
                    dve.wait_ge(g_zero, g + 1)
                    for h in two:
                        part = slice(h * NODES, (h + 1) * NODES)
                        i = dve.tensor_scalar(AC[part, :, part], tiles_of(ADJ, GT * g, GT)[part, :, :], 0, RELS + 2,
                                              ALU.max, ALU.min)
                    i.then_inc(g_clip, 1)
                    dve.wait_ge(g_ps, g + 1)
                    dve.tensor_copy(flat(AT[:, :, :]), GBh).then_inc(g_at, 1)
                    for q in range(GT):
                        dve.wait_ge(g_hg_ps, GT * g + q + 1)
                        dve.tensor_scalar(HG[:, q, :, :, :].rearrange("p a b c -> p (a b c)"), GB[:, :], 1 / PS, None,
                                          ALU.mult).then_inc(g_hg, 1)
                    dve.wait_ge(g_hg, GT * g + GT)
                    dve.wait_ge(rv_set, 1)

                    def rel(r):
                        dve.wait_ge(g_bias, 16 * (g * RELS + r + 1))
                        for q in range(GT):
                            m = (g * RELS + r) * GT + q
                            dve.tensor_tensor(SUM[:, :, :, :].rearrange("p a b c -> p (a b c)"),
                                              HG[:, q, :, :, :].rearrange("p a b c -> p (a b c)"),
                                              BB[:, :, :, :].rearrange("p a b c -> p (a b c)"), ALU.add).then_inc(g_sum, 1)
                            dve.wait_ge(g_sig, m + 1)
                            dve.scalar_tensor_tensor(out=VG[:, :, :], in0=SUM[:, :, 0, :], scalar=WS, in1=SIG[:, :, :],
                                                     op0=ALU.mult, op1=ALU.mult).then_inc(g_val, 1)
                            wait_from(dve, g_used, m)
                            dve.tensor_scalar(HOT[:, 0, :], AT[:, q, :], RV[:, bass.ds(r, 1)], None, ALU.is_equal)
                            dve.tensor_scalar(HOT[:, 1, :], AC[:, q, :], RV[:, bass.ds(r, 1)], None, ALU.is_equal)
                            dve.wait_ge(g_val, m + 1)
                            dve.tensor_copy(VS[:, 0, :, :], VG[:, :, :]).then_inc(g_hi, 1)
                            dve.wait_ge(g_hi, m + 1)
                            dve.tensor_tensor(VS[:, 1, :, :], VG[:, :, :], VS[:, 0, :, :], ALU.subtract)\
                                .then_inc(g_ops, 1)
                    turns(dve, RELS, rel)

            def norms_b(g, p):
                finish_norm(dve, xs_of(g), lambda q: norm_b[p][:, q, :], mv[1][p], rstd[1][p], ln_b, g + 1)
                dve.wait_ge(ln_b[4], g + 1)
                part_norm(dve, k, lambda q: norm_b[p][:, q, :], st[2][p], mv[2][p], ln_c, g + 1)

            def los_b(g, p):
                dve.wait_ge(hi_b, g + 1)
                lo_part(dve, flat(tok_b[p][:, 1, :, :]), flat(norm_b[p][:, :, :]), flat(tok_b[p][:, 0, :, :]))\
                    .then_inc(lo_b, 1)

            def norms_c(g, p):
                wait_from(dve, lo_c, g)
                finish_norm(dve, lambda q: norm_b[p][:, q, :], lambda q: norm_c[p][:, q, :], mv[2][p], rstd[2][p],
                            ln_c, g + 1)

            def los_c(g, p):
                dve.wait_ge(hi_c, g + 1)
                rows = tiles_of(ROWS, GT * g, GT)
                lo_part(dve, rows[:, :, P:2 * P], norm_c[p][:, :, :], rows[:, :, 0:P]).then_inc(lo_c, 1)

            def scores(g, p):
                dve.wait_ge(score_ps, g + 1)
                dve.tensor_tensor(tiles_of(S, GT * g, GT), SC[:, 0:GT * E].rearrange("p (q e) -> p q e", e=E),
                                  k["gate_b"][:, 1:2, :].to_broadcast([P, GT, E]), ALU.add).then_inc(score, 1)
            staggered(dve, NG, 2, [(0, mixture), (1, values), (0, norms_a), (2, sums), (0, los_a), (1, v_los),
                                   (1, general), (2, norms_b), (3, los_c), (2, los_b), (2, norms_c), (3, scores)])


def combine(nc, k):
    NG, X = k["NG"], k["X"]
    RG = 4
    with ExitStack() as ctx:
        def sem(name):
            return ctx.enter_context(nc.semaphore("d_" + name))
        G = [[ctx.enter_context(nc.sbuf_tensor(f"d_G{p}{c}", [P, GT, P], F32)) for c in range(2)] for p in range(RG)]
        gathered = k["dma_sems"][4:4 + RG]
        half, full, stored = sem("half"), sem("full"), sem("stored")
        block = ctx.enter_context(nc.Block())

        @block.gpsimd
        def _(pool):
            for g in range(NG):
                if g >= RG:
                    pool.wait_ge(full, g - RG + 1)
                for q in range(GT):
                    for c in range(2):
                        gather(pool, k, GT * g + q, c, G[g % RG][c][:, q, :], gathered[g % RG])

        @block.vector
        def _(dve):
            def four(it):
                for p in range(RG):
                    g = RG * it + p
                    dve.wait_ge(gathered[p], 16 * 2 * GT * (it + 1))
                    mix(dve, k, G[p], GT * g, half, full, g + 1)
            turns(dve, NG // RG, four)

        @block.sync
        def _(sp):
            def group(g):
                sp.wait_ge(full, g + 1)
                sp.dma_start(k["out_v"][:, bass.ds(GT * g, GT), :], tiles_of(X, GT * g, GT)).then_inc(stored, 16)
            turns(sp, NG, group)
            sp.wait_ge(stored, 16 * NG)


_UNUSED = ("nodemask",)


def kernel(**inputs):
    import numpy as _np
    import concourse.bacc as _bacc
    from concourse import mybir as _mybir
    from concourse.bass_utils import run_bass_kernel_spmd as _run

    nc = _bacc.Bacc("TRN2", target_bir_lowering=False, num_devices=1)
    arrays, args = {}, {}
    for name in inputs:
        if name in _UNUSED:
            continue
        a = _np.ascontiguousarray(inputs[name])
        arrays[f"in_{name}_dram"] = a
        args[name] = nc.dram_tensor(f"in_{name}_dram", a.shape, _mybir.dt.from_np(a.dtype), kind="ExternalInput").ap()
    shape = inputs["x"].shape
    out = nc.dram_tensor("out_dram", shape, _mybir.dt.from_np(_np.dtype("float32")), kind="ExternalOutput").ap()
    program(nc, args, out)
    r = _run(nc, [arrays], core_ids=[0])
    return r.results[0]["out_dram"]
```
